# Optimizing a Trainium2 kernel written in Bass

```python
import numpy as np
import jax
import jax.numpy as jnp

def _softmax(x, axis=-1):
    return jax.nn.softmax(x, axis=axis)

def _gelu(x):
    return jax.nn.gelu(x, approximate=True)

def _silu(x):
    return jax.nn.silu(x)

def _sigmoid(x):
    return jax.nn.sigmoid(x)

def _layernorm(x, axis=-1, eps=1e-05):
    m = jnp.mean(x, axis=axis, keepdims=True)
    v = jnp.var(x, axis=axis, keepdims=True)
    return (x - m) / jnp.sqrt(v + eps)

def _scatter_add(tgt, idx, src, axis=0):
    return tgt.at[idx].add(src)

def _segment_sum(src, seg, n):
    return jax.ops.segment_sum(src, seg, n)
kernel_name = 'mk_lm_tower_d2_tok_ids256_r4_970864'

def setup_inputs(seed: int=0):
    np.random.seed(seed)
    _w = jnp.asarray

    def _rec_inputs():
        import jax
        import jax.numpy as jnp
        _rk = jax.random.key(seed)
        x = jax.random.randint(jax.random.fold_in(_rk, 1), (32, 128), 0, 999990, jnp.int32)
        fside_1S_w_gate = 0.000122222 + 0.0104139 * jax.random.normal(jax.random.fold_in(_rk, 21), (1, 128), jnp.float32)
        return (x, fside_1S_w_gate)
    x, fside_1S_w_gate = _rec_inputs()

    def _L0_tok_setup():
        import jax, jax.numpy as jnp
        import numpy as np
        NUM_ITEMS = 250000
        EMB_D = 64
        FOURIER_D = 64
        VISIT_D = 24
        B, S = (64, 128)
        GEO_GATE_MAX_SCALE = 0.2
        key = jax.random.key(seed)
        ks = jax.random.split(key, 7)
        item_ids = jax.random.randint(ks[0], (B, S), 0, NUM_ITEMS + 1)
        emb_table = 0.02 * jax.random.normal(ks[1], (NUM_ITEMS + 1, EMB_D), dtype=jnp.float32)
        emb_table = emb_table.at[0].set(0.0)
        fourier_table = jax.random.normal(ks[2], (NUM_ITEMS + 1, FOURIER_D), dtype=jnp.float32)
        visit_table = jax.random.normal(ks[3], (NUM_ITEMS + 1, VISIT_D), dtype=jnp.float32)
        w_proj = jax.random.normal(ks[4], (EMB_D, FOURIER_D + VISIT_D), dtype=jnp.float32) * (1.0 / np.sqrt(FOURIER_D + VISIT_D))
        w_gate = 0.01 * jax.random.normal(ks[5], (1, 2 * EMB_D), dtype=jnp.float32)
        b_gate = jnp.full((1,), -1.0986123, dtype=jnp.float32)
        return {'item_ids': item_ids, 'emb_table': emb_table, 'fourier_table': fourier_table, 'visit_table': visit_table, 'w_proj': w_proj, 'w_gate': w_gate, 'b_gate': b_gate}
    _L0_tok_all = _L0_tok_setup()
    _L0_tok_in = {k: v for k, v in _L0_tok_all.items() if k in ('emb_table', 'fourier_table', 'visit_table', 'w_proj', 'b_gate')}
    del _L0_tok_all

    def _L0_attn_setup():
        import jax, jax.numpy as jnp
        import numpy as np
        TEMPERATURE = 1.0
        W_BLEND = 0.8
        EPS = 1e-12

        def _l2norm(x):
            n = jnp.sqrt(jnp.sum(x * x, axis=-1, keepdims=True))
            return x / jnp.maximum(n, EPS)
        key = jax.random.key(seed)
        feats = jax.random.normal(key, (4, 512, 64), dtype=jnp.float32)
        return {'feats': feats}
    _L0_attn_all = _L0_attn_setup()
    _L0_attn_in = {k: v for k, v in _L0_attn_all.items() if k in ()}
    del _L0_attn_all

    def _L0_ffn_setup():
        import jax, jax.numpy as jnp
        import numpy as np
        B, S, H, NH, NE = (4, 256, 64, 4, 4)
        D = H // NH
        EPS = 1e-08

        def layernorm(x, g, b):
            m = jnp.mean(x, axis=-1, keepdims=True)
            v = jnp.mean((x - m) ** 2, axis=-1, keepdims=True)
            return (x - m) / jnp.sqrt(v + EPS) * g + b
        key = jax.random.key(seed)
        ks = jax.random.split(key, 18)
        sc = 0.05
        return {'x': jax.random.normal(ks[0], (B, S, H), jnp.float32), 'hl_w': jax.random.normal(ks[1], (NH, D, H), jnp.float32) * sc, 'hl_b': jax.random.normal(ks[2], (NH, D), jnp.float32) * sc, 'wq': jax.random.normal(ks[3], (NH, NE, D, D), jnp.float32) * sc, 'wk': jax.random.normal(ks[4], (NH, D, D), jnp.float32) * sc, 'wv': jax.random.normal(ks[5], (NH, D, D), jnp.float32) * sc, 'gate_w': jax.random.normal(ks[6], (NH, NE, NE * D), jnp.float32) * sc, 'gate_b': jax.random.normal(ks[7], (NH, NE), jnp.float32) * sc, 'ln_g': jnp.ones((D,), jnp.float32), 'ln_b': jnp.zeros((D,), jnp.float32), 'fc1_w': jax.random.normal(ks[8], (D, D), jnp.float32) * sc, 'fc1_b': jax.random.normal(ks[9], (D,), jnp.float32) * sc, 'fc2_w': jax.random.normal(ks[10], (D, D), jnp.float32) * sc, 'fc2_b': jax.random.normal(ks[11], (D,), jnp.float32) * sc, 'fnorm_g': jnp.ones((D,), jnp.float32), 'fnorm_b': jnp.zeros((D,), jnp.float32), 'fgate_w': jax.random.normal(ks[12], (NH, H), jnp.float32) * sc}
    _L0_ffn_all = _L0_ffn_setup()
    _L0_ffn_in = {k: v for k, v in _L0_ffn_all.items() if k in ('hl_w', 'hl_b', 'wq', 'wk', 'wv', 'gate_w', 'gate_b', 'ln_g', 'ln_b', 'fc1_w', 'fc1_b', 'fc2_w', 'fc2_b', 'fnorm_g', 'fnorm_b', 'fgate_w')}
    del _L0_ffn_all

    def _L1_attn_setup():
        import jax, jax.numpy as jnp
        import numpy as np
        B, T, C, HR = (8, 1024, 64, 4)
        N_LAYER, LAYER_ID = (12, 3)
        HID = HR * C

        def _fancy_decay_first():
            r01 = LAYER_ID / (N_LAYER - 1)
            h = np.arange(C, dtype=np.float32)
            decay = -5.0 + 8.0 * (h / (C - 1)) ** (0.7 + 1.3 * r01)
            zig = (np.arange(1, C + 1) % 3 - 1).astype(np.float32) * 0.5
            first = np.float32(np.log(0.3)) + zig
            return (jnp.asarray(decay, jnp.float32), jnp.asarray(first, jnp.float32))

        def _ln(x, g, b):
            m = jnp.mean(x, axis=-1, keepdims=True)
            v = jnp.var(x, axis=-1, keepdims=True)
            return (x - m) * jax.lax.rsqrt(v + 1e-05) * g + b

        def _wkv(w, u, k, v):
            Bb, Tt, Cc = k.shape
            kT = jnp.swapaxes(k, 0, 1)
            vT = jnp.swapaxes(v, 0, 1)

            def step(carry, kv):
                p, q, o = carry
                kt, vt = kv
                no = jnp.maximum(o, u + kt)
                A = jnp.exp(o - no)
                E = jnp.exp(u + kt - no)
                y = (A * p + E * vt) / (A * q + E)
                no2 = jnp.maximum(w + o, kt)
                A2 = jnp.exp(w + o - no2)
                E2 = jnp.exp(kt - no2)
                return ((A2 * p + E2 * vt, A2 * q + E2, no2), y)
            init = (jnp.zeros((Bb, Cc), k.dtype), jnp.zeros((Bb, Cc), k.dtype), jnp.full((Bb, Cc), -1e+38, k.dtype))
            _, yT = jax.lax.scan(step, init, (kT, vT))
            return jnp.swapaxes(yT, 0, 1)
        key = jax.random.key(seed)
        ks = jax.random.split(key, 12)
        s = 0.02
        decay, first = _fancy_decay_first()
        return {'x': jax.random.normal(ks[0], (B, T, C), jnp.float32), 'Wk': jax.random.normal(ks[1], (C, C), jnp.float32) * s, 'Wv': jax.random.normal(ks[2], (C, C), jnp.float32) * s, 'Wr': jax.random.normal(ks[3], (C, C), jnp.float32) * s, 'Wo': jax.random.normal(ks[4], (C, C), jnp.float32) * s, 'Wk_ffn': jax.random.normal(ks[5], (C, HID), jnp.float32) * s, 'Wv_ffn': jax.random.normal(ks[6], (HID, C), jnp.float32) * s, 'Wr_ffn': jax.random.normal(ks[7], (C, C), jnp.float32) * s, 'g1': 1.0 + 0.1 * jax.random.normal(ks[8], (C,), jnp.float32), 'b1': 0.1 * jax.random.normal(ks[9], (C,), jnp.float32), 'g2': 1.0 + 0.1 * jax.random.normal(ks[10], (C,), jnp.float32), 'b2': 0.1 * jax.random.normal(ks[11], (C,), jnp.float32), 'spatial_decay': decay, 'spatial_first': first}
    _L1_attn_all = _L1_attn_setup()
    _L1_attn_in = {k: v for k, v in _L1_attn_all.items() if k in ('Wk', 'Wv', 'Wr', 'Wo', 'Wk_ffn', 'Wv_ffn', 'Wr_ffn', 'g1', 'b1', 'g2', 'b2', 'spatial_decay', 'spatial_first')}
    del _L1_attn_all

    def _L1_ffn_setup():
        import jax, jax.numpy as jnp
        import numpy as np
        C = 64
        HID = 256
        E = 8
        TEMP = 1.0
        key = jax.random.key(seed)
        ks = jax.random.split(key, 7)
        x = jax.random.normal(ks[0], (8, 4096, C), dtype=jnp.float32)
        W1 = jax.random.normal(ks[1], (C, HID), dtype=jnp.float32) * 0.02
        b1 = jnp.zeros((HID,), dtype=jnp.float32)
        Wg = jax.random.normal(ks[2], (HID, E), dtype=jnp.float32) * 0.02
        bg = jnp.zeros((E,), dtype=jnp.float32)
        Wd = jax.random.normal(ks[3], (E, HID, C), dtype=jnp.float32) * 0.02
        bd = jnp.zeros((E, C), dtype=jnp.float32)
        return {'x': x, 'W1': W1, 'b1': b1, 'Wg': Wg, 'bg': bg, 'Wd': Wd, 'bd': bd}
    _L1_ffn_all = _L1_ffn_setup()
    _L1_ffn_in = {k: v for k, v in _L1_ffn_all.items() if k in ('W1', 'b1', 'Wg', 'bg', 'Wd', 'bd')}
    del _L1_ffn_all
    return {'x': x, 'fside_1S_w_gate': fside_1S_w_gate, 'L0_tok_emb_table': _L0_tok_in['emb_table'], 'L0_tok_fourier_table': _L0_tok_in['fourier_table'], 'L0_tok_visit_table': _L0_tok_in['visit_table'], 'L0_tok_w_proj': _L0_tok_in['w_proj'], 'L0_tok_b_gate': _L0_tok_in['b_gate'], 'L0_ffn_hl_w': _L0_ffn_in['hl_w'], 'L0_ffn_hl_b': _L0_ffn_in['hl_b'], 'L0_ffn_wq': _L0_ffn_in['wq'], 'L0_ffn_wk': _L0_ffn_in['wk'], 'L0_ffn_wv': _L0_ffn_in['wv'], 'L0_ffn_gate_w': _L0_ffn_in['gate_w'], 'L0_ffn_gate_b': _L0_ffn_in['gate_b'], 'L0_ffn_ln_g': _L0_ffn_in['ln_g'], 'L0_ffn_ln_b': _L0_ffn_in['ln_b'], 'L0_ffn_fc1_w': _L0_ffn_in['fc1_w'], 'L0_ffn_fc1_b': _L0_ffn_in['fc1_b'], 'L0_ffn_fc2_w': _L0_ffn_in['fc2_w'], 'L0_ffn_fc2_b': _L0_ffn_in['fc2_b'], 'L0_ffn_fnorm_g': _L0_ffn_in['fnorm_g'], 'L0_ffn_fnorm_b': _L0_ffn_in['fnorm_b'], 'L0_ffn_fgate_w': _L0_ffn_in['fgate_w'], 'L1_attn_Wk': _L1_attn_in['Wk'], 'L1_attn_Wv': _L1_attn_in['Wv'], 'L1_attn_Wr': _L1_attn_in['Wr'], 'L1_attn_Wo': _L1_attn_in['Wo'], 'L1_attn_Wk_ffn': _L1_attn_in['Wk_ffn'], 'L1_attn_Wv_ffn': _L1_attn_in['Wv_ffn'], 'L1_attn_Wr_ffn': _L1_attn_in['Wr_ffn'], 'L1_attn_g1': _L1_attn_in['g1'], 'L1_attn_b1': _L1_attn_in['b1'], 'L1_attn_g2': _L1_attn_in['g2'], 'L1_attn_b2': _L1_attn_in['b2'], 'L1_attn_spatial_decay': _L1_attn_in['spatial_decay'], 'L1_attn_spatial_first': _L1_attn_in['spatial_first'], 'L1_ffn_W1': _L1_ffn_in['W1'], 'L1_ffn_b1': _L1_ffn_in['b1'], 'L1_ffn_Wg': _L1_ffn_in['Wg'], 'L1_ffn_bg': _L1_ffn_in['bg'], 'L1_ffn_Wd': _L1_ffn_in['Wd'], 'L1_ffn_bd': _L1_ffn_in['bd']}

def reference(x, fside_1S_w_gate, L0_tok_emb_table, L0_tok_fourier_table, L0_tok_visit_table, L0_tok_w_proj, L0_tok_b_gate, L0_ffn_hl_w, L0_ffn_hl_b, L0_ffn_wq, L0_ffn_wk, L0_ffn_wv, L0_ffn_gate_w, L0_ffn_gate_b, L0_ffn_ln_g, L0_ffn_ln_b, L0_ffn_fc1_w, L0_ffn_fc1_b, L0_ffn_fc2_w, L0_ffn_fc2_b, L0_ffn_fnorm_g, L0_ffn_fnorm_b, L0_ffn_fgate_w, L1_attn_Wk, L1_attn_Wv, L1_attn_Wr, L1_attn_Wo, L1_attn_Wk_ffn, L1_attn_Wv_ffn, L1_attn_Wr_ffn, L1_attn_g1, L1_attn_b1, L1_attn_g2, L1_attn_b2, L1_attn_spatial_decay, L1_attn_spatial_first, L1_ffn_W1, L1_ffn_b1, L1_ffn_Wg, L1_ffn_bg, L1_ffn_Wd, L1_ffn_bd):
    import jax
    import jax.numpy as jnp

    def _L0_tok_ref(item_ids, emb_table, fourier_table, visit_table, w_proj, w_gate, b_gate):
        import jax, jax.numpy as jnp
        import numpy as np
        NUM_ITEMS = 250000
        EMB_D = 64
        FOURIER_D = 64
        VISIT_D = 24
        B, S = (64, 128)
        GEO_GATE_MAX_SCALE = 0.2
        max_id = emb_table.shape[0] - 1
        safe_ids = jnp.clip(item_ids, 0, max_id)
        item_emb = emb_table[safe_ids]
        fourier_feat = fourier_table[safe_ids]
        visit_feat = visit_table[safe_ids]
        full_geo = jnp.concatenate([fourier_feat, visit_feat], axis=-1)
        geo_delta = jnp.einsum('bsf,df->bsd', full_geo, w_proj)
        valid_mask = (item_ids != 0).astype(geo_delta.dtype)[..., None]
        geo_delta = geo_delta * valid_mask
        gate_in = jnp.concatenate([item_emb, geo_delta], axis=-1)
        gate_logit = jnp.einsum('bsf,of->bso', gate_in, w_gate) + b_gate
        gate = GEO_GATE_MAX_SCALE * jax.nn.sigmoid(gate_logit) * valid_mask
        return item_emb + gate * geo_delta

    def _L0_attn_ref(feats):
        import jax, jax.numpy as jnp
        import numpy as np
        TEMPERATURE = 1.0
        W_BLEND = 0.8
        EPS = 1e-12

        def _l2norm(x):
            n = jnp.sqrt(jnp.sum(x * x, axis=-1, keepdims=True))
            return x / jnp.maximum(n, EPS)
        B, N, C = feats.shape
        f = _l2norm(feats.reshape(B * N, C))
        scores = jnp.matmul(f, f.T) / TEMPERATURE
        attn = jax.nn.softmax(scores, axis=-1)
        feats_att = jnp.matmul(attn, f)
        feats_fcm = f * W_BLEND + feats_att * (1.0 - W_BLEND)
        return _l2norm(feats_fcm.reshape(B, N, C))

    def _L0_ffn_ref(x, hl_w, hl_b, wq, wk, wv, gate_w, gate_b, ln_g, ln_b, fc1_w, fc1_b, fc2_w, fc2_b, fnorm_g, fnorm_b, fgate_w):
        import jax, jax.numpy as jnp
        import numpy as np
        B, S, H, NH, NE = (4, 256, 64, 4, 4)
        D = H // NH
        EPS = 1e-08

        def layernorm(x, g, b):
            m = jnp.mean(x, axis=-1, keepdims=True)
            v = jnp.mean((x - m) ** 2, axis=-1, keepdims=True)
            return (x - m) / jnp.sqrt(v + EPS) * g + b
        b, s, h = x.shape
        nh, d, _ = wk.shape
        ne = wq.shape[1]
        sx = jnp.einsum('bsh,ndh->bnsd', x, hl_w) + hl_b[None, :, None, :]
        pad = sx == 0
        q = jnp.einsum('bnsd,neod->bneso', sx, wq)
        k = jnp.einsum('bnsd,nod->bnso', sx, wk)
        v = jnp.einsum('bnsd,nod->bnso', sx, wv)
        causal = jnp.where(jnp.tril(jnp.ones((s, s), bool)), 0.0, -jnp.inf).astype(x.dtype)
        scores = jnp.einsum('bnesd,bntd->bnest', q, k) * d ** 0.5 + causal
        att = jax.nn.softmax(scores, axis=-1)
        qkv = jnp.einsum('bnest,bntd->bnesd', att, v)
        qkv = jnp.where(pad[:, :, None], 0.0, qkv)
        out = jnp.transpose(qkv, (0, 1, 3, 2, 4)).reshape(b, nh, s, ne * d)
        gs = jax.nn.softmax(jnp.einsum('bnsf,nef->bnse', out, gate_w) + gate_b[None, :, None, :], axis=-1)
        mixed = jnp.einsum('bnsed,bnse->bnsd', out.reshape(b, nh, s, ne, d), gs)
        resid = sx[jnp.arange(nh), jnp.arange(nh)]
        hn = layernorm(mixed + resid, ln_g, ln_b)
        f_n = jnp.transpose(hn, (0, 2, 1, 3)).reshape(b, s, h)
        fx = f_n.reshape(b, s, nh, d)
        pm = fx == 0
        hx = jnp.where(pm, 0.0, fx @ fc1_w.T + fc1_b)
        hx = jax.nn.relu(hx)
        hx = jnp.where(pm, 0.0, hx @ fc2_w.T + fc2_b)
        hx = layernorm(hx + fx, fnorm_g, fnorm_b)
        fout = hx.reshape(b, s, h)
        fg = jax.nn.softmax(fout @ fgate_w.T, axis=-1)
        return (fout.reshape(b, s, nh, d) * fg[..., None]).reshape(b, s, h)

    def _L1_attn_ref(x, Wk, Wv, Wr, Wo, Wk_ffn, Wv_ffn, Wr_ffn, g1, b1, g2, b2, spatial_decay, spatial_first):
        import jax, jax.numpy as jnp
        import numpy as np
        B, T, C, HR = (8, 1024, 64, 4)
        N_LAYER, LAYER_ID = (12, 3)
        HID = HR * C

        def _fancy_decay_first():
            r01 = LAYER_ID / (N_LAYER - 1)
            h = np.arange(C, dtype=np.float32)
            decay = -5.0 + 8.0 * (h / (C - 1)) ** (0.7 + 1.3 * r01)
            zig = (np.arange(1, C + 1) % 3 - 1).astype(np.float32) * 0.5
            first = np.float32(np.log(0.3)) + zig
            return (jnp.asarray(decay, jnp.float32), jnp.asarray(first, jnp.float32))

        def _ln(x, g, b):
            m = jnp.mean(x, axis=-1, keepdims=True)
            v = jnp.var(x, axis=-1, keepdims=True)
            return (x - m) * jax.lax.rsqrt(v + 1e-05) * g + b

        def _wkv(w, u, k, v):
            Bb, Tt, Cc = k.shape
            kT = jnp.swapaxes(k, 0, 1)
            vT = jnp.swapaxes(v, 0, 1)

            def step(carry, kv):
                p, q, o = carry
                kt, vt = kv
                no = jnp.maximum(o, u + kt)
                A = jnp.exp(o - no)
                E = jnp.exp(u + kt - no)
                y = (A * p + E * vt) / (A * q + E)
                no2 = jnp.maximum(w + o, kt)
                A2 = jnp.exp(w + o - no2)
                E2 = jnp.exp(kt - no2)
                return ((A2 * p + E2 * vt, A2 * q + E2, no2), y)
            init = (jnp.zeros((Bb, Cc), k.dtype), jnp.zeros((Bb, Cc), k.dtype), jnp.full((Bb, Cc), -1e+38, k.dtype))
            _, yT = jax.lax.scan(step, init, (kT, vT))
            return jnp.swapaxes(yT, 0, 1)
        Tlen = x.shape[1]
        h = _ln(x, g1, b1)
        k = h @ Wk
        v = h @ Wv
        sr = jax.nn.sigmoid(h @ Wr)
        y = _wkv(spatial_decay / Tlen, spatial_first / Tlen, k, v)
        x = x + sr * y @ Wo
        h2 = _ln(x, g2, b2)
        kk = jnp.square(jax.nn.relu(h2 @ Wk_ffn))
        x = x + jax.nn.sigmoid(h2 @ Wr_ffn) * (kk @ Wv_ffn)
        return x

    def _L1_ffn_ref(x, W1, b1, Wg, bg, Wd, bd):
        import jax, jax.numpy as jnp
        import numpy as np
        C = 64
        HID = 256
        E = 8
        TEMP = 1.0
        orig_shape = x.shape
        xf = x.reshape(-1, orig_shape[-1])
        H = jax.nn.gelu(xf @ W1 + b1, approximate=False)
        probs = jax.nn.softmax((H @ Wg + bg) / TEMP, axis=-1)
        assign = jnp.argmax(probs, axis=-1)
        out = jnp.zeros_like(xf)
        for e in range(Wd.shape[0]):
            y = H @ Wd[e] + bd[e]
            sel = (assign == e)[:, None]
            out = out + jnp.where(sel, probs[:, e:e + 1] * y, 0.0)
        return out.reshape(orig_shape)
    h = _L0_tok_ref(x, L0_tok_emb_table, L0_tok_fourier_table, L0_tok_visit_table, L0_tok_w_proj, fside_1S_w_gate, L0_tok_b_gate)
    h = h + _L0_attn_ref(_layernorm(h, axis=-1))
    h = h + _L0_ffn_ref(_layernorm(h, axis=-1), L0_ffn_hl_w, L0_ffn_hl_b, L0_ffn_wq, L0_ffn_wk, L0_ffn_wv, L0_ffn_gate_w, L0_ffn_gate_b, L0_ffn_ln_g, L0_ffn_ln_b, L0_ffn_fc1_w, L0_ffn_fc1_b, L0_ffn_fc2_w, L0_ffn_fc2_b, L0_ffn_fnorm_g, L0_ffn_fnorm_b, L0_ffn_fgate_w)
    h = h + _L1_attn_ref(_layernorm(h, axis=-1), L1_attn_Wk, L1_attn_Wv, L1_attn_Wr, L1_attn_Wo, L1_attn_Wk_ffn, L1_attn_Wv_ffn, L1_attn_Wr_ffn, L1_attn_g1, L1_attn_b1, L1_attn_g2, L1_attn_b2, L1_attn_spatial_decay, L1_attn_spatial_first)
    h = h + _L1_ffn_ref(_layernorm(h, axis=-1), L1_ffn_W1, L1_ffn_b1, L1_ffn_Wg, L1_ffn_bg, L1_ffn_Wd, L1_ffn_bd)
    return h

_drawn_inputs = setup_inputs


def setup_inputs(seed=0):
    import zlib

    import numpy as np

    out = dict(_drawn_inputs(seed))
    spreads = {'L0_ffn_ln_g': (1.0, 0.2),
     'L0_ffn_ln_b': (0.0, 0.1),
     'L0_ffn_fnorm_g': (1.0, 0.2),
     'L0_ffn_fnorm_b': (0.0, 0.1),
     'L1_ffn_b1': (0.0, 2.0),
     'L1_ffn_bg': (0.0, 2.0),
     'L1_ffn_bd': (0.0, 2.0)}
    factors = {'L0_ffn_wq': 8.0,
     'L0_ffn_wk': 8.0,
     'L0_ffn_gate_w': 8.0,
     'L0_ffn_gate_b': 8.0,
     'L0_ffn_fc1_w': 2.772,
     'L0_ffn_fc1_b': 8.0,
     'L1_attn_Wk': 8.0,
     'L1_attn_Wv': 8.0,
     'L1_attn_Wr': 8.0,
     'L1_attn_Wo': 8.0,
     'L1_attn_Wk_ffn': 8.0,
     'L1_attn_Wv_ffn': 8.0,
     'L1_attn_Wr_ffn': 8.0,
     'L1_attn_g1': 8.0,
     'L1_attn_b1': 8.0,
     'L1_attn_g2': 8.0,
     'L1_attn_b2': 8.0,
     'L1_attn_spatial_decay': 8.0,
     'L1_attn_spatial_first': 64.0,
     'L1_ffn_W1': 62.829,
     'L1_ffn_Wg': 63.775,
     'L1_ffn_Wd': 58.713}
    for name, (base, spread) in spreads.items():
        noise = np.random.default_rng([zlib.crc32(name.encode()), seed]).standard_normal(out[name].shape)
        drawn = base * np.exp(spread * noise) if base else spread * noise
        out[name] = jnp.asarray(drawn.astype(out[name].dtype))
    for name, factor in factors.items():
        out[name] = (out[name] * factor).astype(out[name].dtype)
    return out
```

```python
from contextlib import ExitStack

import concourse.bass as bass
from concourse import mybir

ALU = mybir.AluOpType
ACT = mybir.ActivationFunctionType
AX = mybir.AxisListType
F32 = mybir.dt.float32
F16 = mybir.dt.float16
BF16 = mybir.dt.bfloat16
I32 = mybir.dt.int32
U32 = mybir.dt.uint32

P = 128
C = 64
NH = 4
NE = 4
D = C // NH
BANK = 512
LN_EPS = 1e-5
FFN_EPS = 1e-8
FSCALE = 64.0
MASKED = -1e30
NEG = -1e38
MAX_GATE = 0.2
BLEND = 0.8


def tower(nc, a, out, stop_after=4):
    B, S = a["x"].shape
    NT = B
    NP = NT // 2
    T = B * S
    TP = T // 2
    NQ = TP // BANK
    assert S == P and NT % 8 == 0
    EMB = a["L0_tok_emb_table"].shape[1]
    FOUR = a["L0_tok_fourier_table"].shape[1]
    VIS = a["L0_tok_visit_table"].shape[1]
    GEO = FOUR + VIS
    ITEMS = a["L0_tok_emb_table"].shape[0]
    HID = a["L1_ffn_W1"].shape[1]
    EX = a["L1_ffn_Wd"].shape[0]
    GT = 8
    NG = NT // GT

    ctx = ExitStack()
    with ctx:
        def sb(name, shape, dt=F32):
            return ctx.enter_context(nc.sbuf_tensor(name, shape, dt))

        sems = {}

        def sem(name):
            if name not in sems:
                sems[name] = ctx.enter_context(nc.semaphore(name))
            return sems[name]

        ident = sb("ident", [P, P])
        ident2 = sb("ident2", [P, C])
        ident16 = sb("ident16", [P, P], F16)
        x_int = sb("x_int", [NT, P], I32)
        x_f = sb("x_f", [NT, P])
        idx = sb("idx", [P, NT], U32)
        idf = sb("idf", [P, NT])
        valid = sb("valid", [P, NT])
        gate_w = sb("gate_w", [P, EMB + C])
        gate_b = sb("gate_b", [P, 1])
        wproj = sb("wproj", [C, GEO])
        wprojT = sb("wprojT", [GEO, C])
        R1 = sb("R1", [P, 8192])
        R2 = sb("R2", [P, 8192])
        R3 = sb("R3", [P, 8192])
        gate_in = R1[:, 0:NT * P].rearrange("p (t c) -> p t c", t=NT)
        geo_raw = R2[:, 0:NT * GEO].rearrange("p (t c) -> p t c", t=NT)
        prod = R3[:, 0:NT * P].rearrange("p (t c) -> p t c", t=NT)
        geoT = sb("geoT", [GEO, 2, BANK])
        glogit = sb("glogit", [P, NT])
        gate = sb("gate", [P, NT])
        h = sb("h", [P, NT, C])
        xc = sb("xc", [P, NT, C])
        sq = sb("sq", [P, NT, C])
        fn = sb("fn", [P, NT, C])
        st = [sb(f"st{i}", [P, 8, NT]) for i in range(2)]
        stD = sb("stD", [P, 8, NT * NH])
        F4 = sb("F4", [P, NT, 4 * C], F16)
        F_hi = F4[:, :, C:2 * C]
        F_lo = F4[:, :, 2 * C:3 * C]
        ps = ctx.enter_context(nc.psum_tensor("ps", [P, 8, BANK], F32))
        A_hl = R1[:, 0:T // 2].bitcast(F16)
        M_hh = R1[:, T // 2:T].bitcast(F16)
        M_ll = R1[:, T:T + T // 2].bitcast(F16)
        e32 = R2[:, 0:4096].rearrange("p (u n) -> p u n", u=4)
        eh = R2[:, 4096:6144].bitcast(F16).rearrange("p (u n) -> p u n", u=4)
        el = R2[:, 6144:8192].bitcast(F16).rearrange("p (u n) -> p u n", u=4)
        attT = R3[:, 0:T]
        racc = sb("racc", [P, NT, 4])
        zero16 = sb("zero16", [P, P], F16)

        ident_bf = sb("ident_bf", [P, P], BF16)
        masked = sb("masked", [P, NH, P], BF16)
        own_rows = sb("own_rows", [P, 2 * NH])
        WCOL = {"hl": 0, "wq0": 128, "wq1": 320, "wk": 512, "wv": 704, "fc1": 832, "fc2": 960, "fg": 1088,
                "gate0": 1216, "gate1": 1344}
        wn = sb("wn", [P, 1472])
        WT = sb("WT", [P, 2 * BANK + 296])
        wT_hl = WT[:, 0:P]
        wT_q = [[WT[:, (1 + 2 * ep + par) * P:(2 + 2 * ep + par) * P] for par in range(2)] for ep in range(2)]
        wT_k = [WT[:, (5 + par) * P:(6 + par) * P] for par in range(2)]
        wT_v = WT[:, 7 * P:8 * P]
        wT_fc1 = WT[:, 8 * P:9 * P]
        wT_fc2 = WT[:, 9 * P:10 * P]
        wT_fg = WT[:, 10 * P:10 * P + 2 * NH]
        wT_gate = [WT[:, 10 * P + 8 + 16 * c:10 * P + 24 + 16 * c] for c in range(2)]
        cols = sb("cols", [P, 16])
        HL_B, FC1_B, G1, B1, G2, B2, DECAY, FIRST, HID_B, W_COL, U_COL = [*range(9), 10, 11]
        rows = sb("rows", [P, 8, C])
        LN_G, LN_B, FN_G, FN_B, FC2_B, GATE_B, EX_B = range(7)
        sx = sb("sx", [P, NT, C])
        kept = sb("kept", [P, NT, C])
        GL = sb("GL", [P, NT, NH * NE])
        xT = R3[:, 0:TP]
        sxT = R1[:, 0:TP]
        Pb = R1[:, 2048:4096].rearrange("p (e n) -> p e n", e=NE)
        PT = R1[:, 4096:8192].rearrange("p (z e n) -> p z e n", z=2, e=NE)
        O_all = R2[:, :].rearrange("p (t n) -> p t n", t=NT)
        KZ = R3[:, 2048:4096].rearrange("p (z n) -> p z n", z=2)
        qs = R3[:, 4096:5120].rearrange("p (z n) -> p z n", z=2)
        ks = R3[:, 5120:5376].rearrange("p (z n) -> p z n", z=2)
        vs = R3[:, 5376:5888].rearrange("p (z a n d) -> p z a n d", z=2, a=2, n=NH)
        ATs = R3[:, 5888:6400]
        Ost = R3[:, 6400:6912].rearrange("p (z n) -> p z n", z=2)
        OTs = R3[:, 6912:7168]
        O1 = R3[:, 7168:7424]
        sxs = R3[:, 7424:7552]
        hxT = R1[:, 0:TP]
        mixp = R1[:, :].rearrange("p (g d) -> p g d", d=D)
        resid = sb("resid", [P, C])
        fg = sb("fg", [P, NT * NH])
        negmax = R3[:, 7552:7568].rearrange("p (e n) -> p e n", e=NE)
        rl = R3[:, 7568:7584].rearrange("p (e n) -> p e n", e=NE)

        wl = F4[:, :, :].rearrange("p t c -> p (t c)").bitcast(F32)
        w_bd = wl[:, 0:5 * P].rearrange("p (i n) -> p i n", i=5)
        WK, WV, WR, WO, WRF = range(5)
        w_kf = wl[:, 640:1152].rearrange("p (a n) -> p a n", a=2)
        w_1 = wl[:, 1152:1664].rearrange("p (a n) -> p a n", a=2)
        w_vf = wl[:, 1664:1792].rearrange("p (k n) -> p k n", k=2)
        w_g = wl[:, 1792:1856].rearrange("p (k n) -> p k n", k=2)
        w_bias = wl[:, 1856:2880]
        w_d = wl[:, 2880:3904].rearrange("p (k n) -> p k n", k=2)
        kT, vT, srT, W_t = (R1[:, i * TP:(i + 1) * TP] for i in range(4))
        O_prev, k_last, A2, E2 = (R2[:, i * TP:(i + 1) * TP] for i in range(4))
        hT, EV, P_prev, Q_prev = (R3[:, i * TP:(i + 1) * TP] for i in range(4))
        hidT = R1[:, :].rearrange("p (i n) -> p i n", i=4)
        srfT, gatedT = R2[:, 0:TP], R2[:, TP:2 * TP]
        scratch = R2[:, 2 * TP:4 * TP].rearrange("p (z n) -> p z n", z=8)
        lgT = R3[0:C, TP:2 * TP]
        coef = sb("coef", [P, NT, EX])
        tmp8 = sb("tmp8", [P, NT, EX])
        rank = sb("rank", [P, EX])
        coefT = sb("coefT", [P, 2 * P])
        xp = R3[:, 2 * TP:3 * TP].rearrange("p (t c) -> p t c", c=C)

        block = ctx.enter_context(nc.Block())

        def bc(ap, n):
            return ap.unsqueeze(2).broadcast_to(tuple(ap.shape) + (n,))

        def row(ap, t):
            return ap.unsqueeze(1).broadcast_to((ap.shape[0], t, ap.shape[1]))

        class Chain:

            def __init__(self, eng, name):
                self.eng, self.sem, self.n = eng, sem(name), 0

            def __call__(self, ins):
                self.n += 1
                ins.then_inc(self.sem, 1)
                self.eng.wait_ge(self.sem, self.n)

        NORMS = ("ln1", "ln2", "mix", "hx", "ln3", "ln4", "ln5", "ln6")
        TURNS = ("x", "fx", "fo", "x4", "x5", "x6")

        def nth(name):
            return NORMS.index(name) + 1

        def turned(name, q):
            return TURNS.index(name) * NQ + q + 1

        def turned_out(name, q):
            return TURNS.index(name) * (NQ // 2) + q // 2 + 1

        def layer_norm_stats(dve, ch, name, x, s, eps=LN_EPS, w=C):
            xcv = xc[:, :, :].rearrange("p t (n d) -> p (t n) d", d=w)
            sqv = sq[:, :, :].rearrange("p t (n d) -> p (t n) d", d=w)
            ch(dve.tensor_reduce(s[:, 0, :], x, AX.X, ALU.add))
            ch(dve.tensor_scalar(s[:, 1, :], s[:, 0, :], 1.0 / w, None, ALU.mult))
            dve.tensor_tensor(xcv, x, bc(s[:, 1, :], w), ALU.subtract).then_inc(sem("ln_centred"), 1)
            dve.wait_ge(sem("ln_squared"), nth(name))
            ch(dve.tensor_reduce(s[:, 3, :], sqv, AX.X, ALU.add))
            dve.tensor_scalar(s[:, 4, :], s[:, 3, :], 1.0 / w, eps, ALU.mult, ALU.add).then_inc(sem("ln_var"), 1)
            dve.wait_ge(sem("ln_root"), nth(name))
            dve.wait_ge(sem("ln_var"), nth(name))
            ch(dve.reciprocal(s[:, 2, :], s[:, 5, :]))
            ch(dve.tensor_tensor(s[:, 6, :], s[:, 2, :], s[:, 2, :], ALU.mult))
            ch(dve.tensor_tensor(s[:, 6, :], s[:, 6, :], s[:, 4, :], ALU.mult))
            ch(dve.tensor_scalar(s[:, 6, :], s[:, 6, :], -0.5, 1.5, ALU.mult, ALU.add))
            ch(dve.tensor_tensor(s[:, 2, :], s[:, 2, :], s[:, 6, :], ALU.mult))
            return xcv

        def ln_act(act, name, s):
            act.wait_ge(sem("ln_centred"), nth(name))
            act.activation(sq[:, :, :], xc[:, :, :], ACT.Square).then_inc(sem("ln_squared"), 1)
            act.wait_ge(sem("ln_var"), nth(name))
            act.activation(s[:, 5, :], s[:, 4, :], ACT.Sqrt).then_inc(sem("ln_root"), 1)

        HALF = T // 2
        SLOT = HALF // 2
        STEPS = 2 * NT
        U = 4
        SPLITS = [(A_hl, C), (M_hh, 0), (M_ll, 2 * C)]
        FG = [(m, q) for q in range(NT // 8) for m in range(3)]

        def fT_out(eng, g):
            m, q = FG[g]
            eng.wait_ge(sem("fT_done"), g + 1)
            dst = SPLITS[m][0][:, q * 1024:(q + 1) * 1024]
            src = ps[:, g % 8, :].bitcast(F16)
            name = f"fT_out{g % 2}"
            if g % 2:
                eng.tensor_copy(dst, src).then_inc(sem(name), 1)
            else:
                eng.activation(dst, src, ACT.Copy).then_inc(sem(name), 1)

        def attention_act(act):
            act.wait_ge(sem("f_ready"), 1)
            act.activation(F4[:, :, 0:C], fn[:, :, :], ACT.Copy, scale=FSCALE).then_inc(sem("f_doubled"), 1)
            act.wait_ge(sem("f_split"), 1)
            act.activation(F4[:, :, 3 * C:], F_lo, ACT.Copy).then_inc(sem("f_doubled"), 1)
            for g in range(0, len(FG), 2):
                fT_out(act, g)
            for half in range(2):
                base = half * STEPS
                with act.Fori(0, STEPS // U) as it:
                    for u in range(U):
                        slot = u % 2
                        s_in = ps[:, 4 + 2 * slot:6 + 2 * slot, :]
                        act.wait_ge(sem("scores_done"), it * U + base + u + 1)
                        if slot == 0:
                            act.activation(eh[:, u, :].rearrange("p (b n) -> p b n", b=2), s_in, ACT.Exp,
                                           scale=1.0 / FSCALE ** 2)
                        act.activation(e32[:, u, :].rearrange("p (b n) -> p b n", b=2), s_in, ACT.Exp,
                                       scale=1.0 / FSCALE ** 2,
                                       accum_out=racc[:, bass.ds(it * (U // 2) + u // 2, 1), 2 * half + slot])\
                            .then_inc(sem("exp_done"), 1)
                act.wait_ge(sem("att_done"), half + 1)
                act.activation(attT[:, half * HALF:half * HALF + SLOT].rearrange("p (b n) -> p b n", b=2),
                               ps[:, 0:2, :], ACT.Copy).then_inc(sem("att_out_act"), 1)
            act.wait_ge(sem("fcm_ready"), 1)
            act.activation(sq[:, :, :], xc[:, :, :], ACT.Square).then_inc(sem("fcm_squared"), 1)
            act.wait_ge(sem("fcm_ss"), 1)
            act.activation(st[1][:, 5, :], st[1][:, 4, :], ACT.Sqrt).then_inc(sem("fcm_root"), 1)

        def attention_dve(dve, ch):
            s = st[0]
            dve.wait_ge(sem("ss_root"), 1)
            ch(dve.tensor_tensor(s[:, 6, :], s[:, 7, :], s[:, 2, :], ALU.mult))
            ch(dve.tensor_scalar(s[:, 6, :], s[:, 6, :], 1e-12, None, ALU.max))
            ch(dve.reciprocal(s[:, 6, :], s[:, 6, :]))
            ch(dve.tensor_tensor(s[:, 6, :], s[:, 6, :], s[:, 2, :], ALU.mult))
            dve.tensor_tensor(fn[:, :, :], xc[:, :, :], bc(s[:, 6, :], C), ALU.mult).then_inc(sem("f_ready"), 1)
            dve.wait_ge(sem("f_ready"), 1)
            ch(dve.tensor_scalar(F_hi, fn[:, :, :], FSCALE, None, ALU.mult))
            dve.scalar_tensor_tensor(F_lo, fn[:, :, :], FSCALE, F_hi, ALU.mult, ALU.subtract).then_inc(sem("f_split"), 1)
            for g in range(1, len(FG), 2):
                fT_out(dve, g)
            for half in range(2):
                base = half * STEPS
                with dve.Fori(0, STEPS // U) as it:
                    for u in range(U):
                        dve.wait_ge(sem("exp_done"), it * U + base + u + 1)
                        if u % 2 == 1:
                            dve.tensor_copy(eh[:, u, :], e32[:, u, :]).then_inc(sem("eh_done"), 1)
                            dve.wait_ge(sem("eh_done"), it * (U // 2) + base // 2 + u // 2 + 1)
                        dve.tensor_tensor(el[:, u, :], e32[:, u, :], eh[:, u, :], ALU.subtract)\
                            .then_inc(sem("e_split"), 1)
                dve.wait_ge(sem("att_done"), half + 1)
                dve.tensor_copy(attT[:, half * HALF + SLOT:(half + 1) * HALF].rearrange("p (b n) -> p b n", b=2),
                                ps[:, 2:4, :]).then_inc(sem("att_out_dve"), 1)
            s = st[1]
            ch(dve.tensor_reduce(s[:, 0, :], racc[:, :, :], AX.X, ALU.add))
            ch(dve.reciprocal(s[:, 1, :], s[:, 0, :]))
            ch(dve.tensor_scalar(s[:, 1, :], s[:, 1, :], (1.0 - BLEND) / FSCALE, None, ALU.mult))
            dve.wait_ge(sem("att_token"), 1)
            ch(dve.tensor_tensor(xc[:, :, :], ps[:, 0:4, :].rearrange("p k (t c) -> p (k t) c", c=C),
                                 bc(s[:, 1, :], C), ALU.mult))
            dve.scalar_tensor_tensor(xc[:, :, :], fn[:, :, :], BLEND, xc[:, :, :], ALU.mult, ALU.add)\
                .then_inc(sem("fcm_ready"), 1)
            dve.wait_ge(sem("fcm_squared"), 1)
            dve.tensor_reduce(s[:, 4, :], sq[:, :, :], AX.X, ALU.add).then_inc(sem("fcm_ss"), 1)
            dve.wait_ge(sem("fcm_root"), 1)
            ch(dve.tensor_scalar(s[:, 6, :], s[:, 5, :], 1e-12, None, ALU.max))
            ch(dve.reciprocal(s[:, 6, :], s[:, 6, :]))
            ch(dve.tensor_tensor(xc[:, :, :], xc[:, :, :], bc(s[:, 6, :], C), ALU.mult))
            ch(dve.tensor_tensor(h[:, :, :], h[:, :, :], xc[:, :, :], ALU.add))

        def attention_pe(pe):
            pe.wait_ge(sem("f_split"), 1)
            pe.wait_ge(sem("f_doubled"), 2)
            pe.wait_ge(sem("ident_ready"), 2)
            for g, (m, q) in enumerate(FG):
                if g >= 8:
                    pe.wait_ge(sem(f"fT_out{g % 2}"), (g - 8) // 2 + 1)
                bank = ps[:, g % 8, :].bitcast(F16)
                for i in range(8):
                    last = pe.transpose(bank[:, i * P:(i + 1) * P], F4[:, 8 * q + i, SPLITS[m][1]:SPLITS[m][1] + P], ident16[:, :])
                last.then_inc(sem("fT_done"), 1)

            def scores(half, slot, j):
                for c in range(2):
                    col = half * HALF + slot * SLOT + c * BANK
                    lhs = A_hl[:, bass.ds(j * P, P)]
                    pe.matmul(ps[:, 4 + 2 * slot + c, :], lhs, M_hh[:, col:col + BANK], start=True, stop=False)
                    last = pe.matmul(ps[:, 4 + 2 * slot + c, :], lhs, M_ll[:, col:col + BANK], start=False, stop=True)
                last.then_inc(sem("scores_done"), 1)

            def weigh(slot, u, j):
                for part in (eh, el):
                    for c in range(2):
                        pe.matmul(ps[:, 2 * slot + c, :], F4[:, bass.ds(j, 1), C:3 * C].rearrange("p t c -> p (t c)"),
                                  part[:, u, c * BANK:(c + 1) * BANK], start=False, stop=False, skip_group_check=True)

            for half in range(2):
                base = half * STEPS
                if half == 0:
                    pe.wait_ge(sem("fT_out0"), len(FG) // 2)
                    pe.wait_ge(sem("fT_out1"), len(FG) // 2)
                else:
                    pe.wait_ge(sem("att_out_act"), half)
                    pe.wait_ge(sem("att_out_dve"), half)
                for c in range(4):
                    pe.matmul(ps[:, c, :], zero16[:, :], M_hh[:, c * BANK:(c + 1) * BANK], start=True, stop=False,
                              skip_group_check=True)
                scores(half, 0, 0)
                scores(half, 1, 0)
                with pe.Fori(0, STEPS // U - 1) as it:
                    for u in range(U):
                        pe.wait_ge(sem("exp_done"), it * U + base + u + 1)
                        scores(half, u % 2, it * (U // 2) + u // 2 + 1)
                        pe.wait_ge(sem("e_split"), it * U + base + u + 1)
                        weigh(u % 2, u, it * (U // 2) + u // 2)
                for u in range(U):
                    k = STEPS - U + u
                    if u < 2:
                        pe.wait_ge(sem("exp_done"), base + k + 1)
                        scores(half, u % 2, k // 2 + 1)
                    pe.wait_ge(sem("e_split"), base + k + 1)
                    weigh(u % 2, u, k // 2)
                for c in range(4):
                    last = pe.matmul(ps[:, c, :], zero16[:, :], M_hh[:, c * BANK:(c + 1) * BANK], start=False,
                                     stop=True, skip_group_check=True)
                last.then_inc(sem("att_done"), 1)
            pe.wait_ge(sem("att_out_act"), 2)
            pe.wait_ge(sem("att_out_dve"), 2)
            for t in range(NT):
                last = pe.matmul(ps[:, t // 8, t % 8 * C:(t % 8 + 1) * C], attT[:, t * P:(t + 1) * P], ident2[:, :],
                                 start=True, stop=True)
            last.then_inc(sem("att_token"), 1)

        WN_LOADS, COL_LOADS, ROW_LOADS, WL_LOADS = 2 * (1 + NH * 6 + 1) + NH, 2 + 8 + 12 + 2, 5 * NH + 2, 10 + 4 + 4 + P // EX
        wn_loads, col_loads, row_loads = [], [], []

        def transpose_pairs(pe, src, first_bank=0):
            for p in range(NP):
                last = pe.transpose(ps[:, first_bank + p // 4, p % 4 * P:(p % 4 + 1) * P],
                                    src[:, 2 * p:2 * p + 2, :].rearrange("p t c -> p (t c)"), ident[:, :])
                if p % 4 == 3:
                    last.then_inc(sem("pairs_turned"), 1)

        def project(pe, w, src, name, first_bank):
            for q in range(NQ):
                pe.matmul(ps[:, first_bank + q, :], w, src[:, q * BANK:(q + 1) * BANK], start=True, stop=True)\
                    .then_inc(sem(name), 1)

        def batches(eng, one):
            for b in range(4):
                one(b, b // 2, b, b)
            with eng.Fori(1, NT // 4 - 1) as it:
                for m in range(4):
                    one(it * 4 + m, it * 2 + m // 2, m, None)
            for b in range(NT - 4, NT + 3):
                one(b, b // 2, b % 4, b)

        def has(n, lo, hi=NT):
            return n is None or lo <= n < hi

        def heads_pool(pool):
            pool.wait_ge(sem("att_out_act"), 2)
            pool.wait_ge(sem("att_token"), 1)
            pool.memset(R3[:, 5376:5888], 0.0).then_inc(sem("vs_zeroed"), 1)
            pool.wait_ge(sem("vs_zeroed"), 1)
            pool.memset(vs[:, :, :, :, D:D + 1].rearrange("p z a n d -> p (z a n) d"), 1.0).then_inc(sem("vs_ones"), 1)

            pool.memset(wl[:, 0:3904], 0.0).then_inc(sem("wl_zeroed"), 1)
            for e in range(EX):
                last = pool.memset(rank[:, e:e + 1], float(EX - e))
            last.then_inc(sem("rank_ready"), 1)

            def stage_sxT(p, first=False):
                if not first:
                    pool.wait_ge(sem("v_done"), p)
                pool.tensor_copy(sxs[:, :], sxT[:, bass.ds(p * P, P)]).then_inc(sem("sxs_ready"), 1)

            def spread_keys(b, par, n):
                if n is None or n >= 2:
                    pool.wait_ge(sem("S_done"), (b - 1) * 4)
                pool.tensor_tensor(KZ[:, par, :].rearrange("p (c t) -> p c t", t=P), row(ks[:, par, :], 2 * NH),
                                   bc(own_rows[:, :], P), ALU.mult).then_inc(sem("kz_ready"), 1)

            pool.wait_ge(sem("sxT_ready"), 2)
            stage_sxT(0, True)
            pool.wait_ge(sem("k_out"), 1)
            spread_keys(0, 0, 0)
            stage_sxT(1)

            def one(b, p, m, n):
                par = m % 2
                if par == 0:
                    if has(n, 0):
                        spread_keys(b + 1, 1, n + 1 if n is not None else None)
                else:
                    if has(n, 0, NT - 2):
                        pool.wait_ge(sem("k_out"), p + 2)
                        spread_keys(b + 1, 0, n + 1 if n is not None else None)
                    if has(n, 0, NT - 4):
                        stage_sxT(p + 2)
                if has(n, 3, NT + 3):
                    pool.wait_ge(sem("O_done"), b - 2)
                    pool.tensor_copy(O_all[:, bass.ds(b - 3, 1), :].rearrange("p t n -> p (t n)"), Ost[:, (m + 1) % 2, :])\
                        .then_inc(sem("O_copied"), 1)
            batches(pool, one)

        def heads_pe(pe):
            pe.wait_ge(sem("ln2_done"), 1)
            transpose_pairs(pe, fn)
            pe.wait_ge(sem("WT_ready"), 3)
            for q in range(NQ):
                pe.wait_ge(sem(f"pairs_out{q % 2}"), turned_out("x", q))
                pe.matmul(ps[:, 4 + q, :], wT_hl, xT[:, q * BANK:(q + 1) * BANK], start=True, stop=True)\
                    .then_inc(sem("sxT_done"), 1)
            pe.wait_ge(sem("sxT_ready"), 2)
            pe.wait_ge(sem("masks_ready"), 1)

            def project_k(p):
                pe.wait_ge(sem("sxs_ready"), p + 1)
                for par in range(2):
                    pe.matmul(ps[:, 7, par * P:(par + 1) * P], wT_k[par], sxs[:, :], start=True, stop=True)
                pe.transpose(ps[:, 7, 3 * P:4 * P], sxs[:, :], ident[:, :]).then_inc(sem("k_done"), 1)

            def project_v(p):
                pe.matmul(ps[:, 7, 3 * P:4 * P], sxs[:, :], wT_v, start=True, stop=True).then_inc(sem("v_done"), 1)

            def project_q(p):
                pe.wait_ge(sem("k_out"), p + 1)
                pe.wait_ge(sem("sx_out"), p + 1)
                for par in range(2):
                    for ep in range(2):
                        c = (2 * par + ep) * P
                        last = pe.matmul(ps[:, 7, c:c + P], wT_q[ep][par], sxs[:, :], start=True, stop=True)
                last.then_inc(sem("q_done"), 1)

            project_k(0)
            project_q(0)
            pe.wait_ge(sem("q_out"), 1)
            project_v(0)

            def one(b, p, m, n):
                par, z = m % 2, m // 2
                for e in range(NE):
                    if n is None or n >= 1:
                        if has(n, 1, NT + 1):
                            pe.wait_ge(sem("exp2_done"), b * 4 + e - 3)
                    if has(n, 0):
                        if e == 0:
                            pe.wait_ge(sem("q_out"), p + 1)
                            pe.wait_ge(sem("kz_ready"), b + 1)
                        pe.matmul(ps[:, e, :], qs[:, z, (2 * par + e // 2) * P:(2 * par + e // 2 + 1) * P],
                                  KZ[:, par, e % 2 * BANK:(e % 2 + 1) * BANK], start=True, stop=False)
                        pe.matmul(ps[:, e, :], ident_bf[:, :], masked[:, :, :].rearrange("p n t -> p (n t)"),
                                  start=False, stop=True).then_inc(sem("S_done"), 1)
                    if has(n, 1, NT + 1):
                        if n is None or 4 * n + e - 5 > 0:
                            pe.wait_ge(sem("PT_out"), b * 4 + e - 5)
                        for g in range(NH):
                            last = pe.transpose(ps[:, 4 + e % 2, g * P:(g + 1) * P], Pb[:, e, g * P:(g + 1) * P],
                                                ident[:, :])
                        last.then_inc(sem("T_done"), 1)
                    if e == 0:
                        if has(n, 2, NT + 2):
                            pe.wait_ge(sem("PT_out"), b * 4 - 4)
                            pe.wait_ge(sem("v_out"), p)
                            if n is None or n >= 3:
                                pe.wait_ge(sem("O_done"), b - 2)
                            for g in range(NH):
                                last = pe.matmul(ps[32 * g:32 * g + 32, 6, :], vs[:, (m // 2 + 1) % 2, par, g, :],
                                                 PT[:, par, :, g * P:(g + 1) * P], start=True, stop=True)
                            last.then_inc(sem("AV_done"), 1)
                        if par == 1 and has(n, 0, NT - 2):
                            project_q(p + 1)
                    if e == 1 and has(n, 3, NT + 3):
                        pe.wait_ge(sem("O_done"), b - 2)
                        if par == 1:
                            if has(n, 0, NT - 2):
                                pe.wait_ge(sem("q_out"), p + 2)
                        elif has(n, 0):
                            pe.wait_ge(sem("v_out"), p + 1)
                        if n is None or n >= 4:
                            pe.wait_ge(sem("gl_out"), b - 3)
                        for c in range(2):
                            last = pe.transpose(ps[:, 7, c * P:(c + 1) * P], Ost[:, (m + 1) % 2, c * P:(c + 1) * P],
                                                ident[:, :])
                        last.then_inc(sem("OT_done"), 1)
                    if e == 2:
                        if has(n, 2, NT + 2):
                            pe.wait_ge(sem("AT_out"), b - 1)
                            for g in range(NE):
                                last = pe.transpose(ps[:, 6, g * P:(g + 1) * P], ATs[:, g * P:(g + 1) * P], ident[:, :])
                            last.then_inc(sem("ATt_done"), 1)
                        if has(n, 3, NT + 3):
                            pe.wait_ge(sem("OT_out"), b - 2)
                            for c in range(2):
                                last = pe.matmul(ps[:, 7, 256:256 + NH * NE], OTs[:, c * P:(c + 1) * P], wT_gate[c],
                                                 start=c == 0, stop=c == 1)
                            last.then_inc(sem("gl_done"), 1)
                        if par == 1 and has(n, 0, NT - 2):
                            if n is not None and n < 3:
                                pe.wait_ge(sem("q_out"), p + 2)
                            else:
                                pe.wait_ge(sem("gl_out"), b - 2)
                            project_v(p + 1)
                    if e == 3 and par == 0 and has(n, 0, NT - 2):
                        if n is None or n >= 3:
                            pe.wait_ge(sem("gl_out"), b - 2)
                        pe.wait_ge(sem("v_out"), p + 1)
                        project_k(p + 1)
            batches(pe, one)
            tail_pe(pe)

        def heads_act(act):
            ln_act(act, "ln2", st[0])
            for q in range(0, NQ, 2):
                act.wait_ge(sem("pairs_turned"), turned("x", q))
                act.activation(xT[:, q * BANK:(q + 1) * BANK], ps[:, q, :], ACT.Copy).then_inc(sem("pairs_out0"), 1)
            act.wait_ge(sem("cols_in"), 16 * COL_LOADS)
            act.wait_ge(sem("sxT_done"), 2)
            act.activation(sxT[:, 0:2 * BANK].rearrange("p (b n) -> p b n", b=2), ps[:, 4:6, :], ACT.Identity,
                           bias=cols[:, HL_B:HL_B + 1]).then_inc(sem("sxT_ready"), 1)
            act.wait_ge(sem("vs_ones"), 1)

            def k_out(p, z, b=None, n=0):
                act.wait_ge(sem("k_done"), p + 1)
                if b is not None:
                    act.wait_ge(sem("kz_ready"), b + 2)
                act.activation(ks[:, :, :].rearrange("p z n -> p (z n)"), ps[:, 7, 0:2 * P], ACT.Copy)\
                    .then_inc(sem("k_out"), 1)

            def v_out(p, z):
                act.wait_ge(sem("v_done"), p + 1)
                act.activation(vs[:, z, :, :, 0:D].rearrange("p a n d -> p (a n) d"),
                               ps[:, 7, 3 * P:4 * P].rearrange("p (g d) -> p g d", d=D), ACT.Copy)\
                    .then_inc(sem("v_out"), 1)

            def q_out(p, z):
                act.wait_ge(sem("q_done"), p + 1)
                act.activation(qs[:, z, :], ps[:, 7, :], ACT.Copy, scale=float(D) ** 0.5).then_inc(sem("q_out"), 1)

            k_out(0, 0)
            q_out(0, 0)
            v_out(0, 0)

            def one(b, p, m, n):
                par, z = m % 2, m // 2
                for e in range(NE):
                    if has(n, 0):
                        act.wait_ge(sem("max_done"), b * 4 + e + 1)
                        if n is None or n >= 1:
                            act.wait_ge(sem("T_done"), b * 4 + e - 3)
                        for g in range(NH):
                            last = act.activation(Pb[:, e, g * P:(g + 1) * P], ps[:, e, g * P:(g + 1) * P], ACT.Exp,
                                                  bias=negmax[:, e, g:g + 1])
                        last.then_inc(sem("exp2_done"), 1)
                    if e == 0:
                        if has(n, 2, NT + 2):
                            act.wait_ge(sem("AV_done"), b - 1)
                            act.activation(ATs[:, :], ps[:, 6, :], ACT.Copy).then_inc(sem("AT_out"), 1)
                        if par == 1 and has(n, 0, NT - 2):
                            q_out(p + 1, (z + 1) % 2)
                    if e == 1 and has(n, 3, NT + 3):
                        act.wait_ge(sem("OT_done"), b - 2)
                        act.activation(OTs[:, :], ps[:, 7, 0:2 * P], ACT.Copy).then_inc(sem("OT_out"), 1)
                    if e == 2 and has(n, 3, NT + 3):
                        act.wait_ge(sem("gl_done"), b - 2)
                        act.activation(GL[:, bass.ds(b - 3, 1), :].rearrange("p t n -> p (t n)"),
                                       ps[:, 7, 256:256 + NH * NE], ACT.Copy).then_inc(sem("gl_out"), 1)
                    if e == 2 and par == 1 and has(n, 0, NT - 2):
                        v_out(p + 1, (z + 1) % 2)
                    if e == 3 and par == 0 and has(n, 0, NT - 2):
                        k_out(p + 1, (z + 1) % 2, b)
            batches(act, one)
            tail_act(act)

        def heads_dve(dve, ch):
            s = st[0]
            layer_norm_stats(dve, ch, "ln2", h[:, :, :], s)
            dve.tensor_tensor(fn[:, :, :], xc[:, :, :], bc(s[:, 2, :], C), ALU.mult).then_inc(sem("ln2_done"), 1)
            for q in range(1, NQ, 2):
                dve.wait_ge(sem("pairs_turned"), turned("x", q))
                dve.tensor_copy(xT[:, q * BANK:(q + 1) * BANK], ps[:, q, :]).then_inc(sem("pairs_out1"), 1)
            dve.wait_ge(sem("cols_in"), 16 * COL_LOADS)
            dve.wait_ge(sem("sxT_done"), 4)
            dve.tensor_scalar(sxT[:, 2 * BANK:].rearrange("p (b n) -> p b n", b=2), ps[:, 6:8, :],
                              cols[:, HL_B:HL_B + 1], None, ALU.add).then_inc(sem("sxT_ready"), 1)

            def sx_out(p):
                dve.wait_ge(sem("k_done"), p + 1)
                dve.wait_ge(sem("k_out"), p + 1)
                dve.tensor_scalar(kept[:, bass.ds(p * 2, 2), :].rearrange("p t c -> p (t c)"), ps[:, 7, 3 * P:4 * P],
                                  0.0, None, ALU.not_equal)
                dve.tensor_copy(sx[:, bass.ds(p * 2, 2), :].rearrange("p t c -> p (t c)"), ps[:, 7, 3 * P:4 * P])\
                    .then_inc(sem("sx_out"), 1)

            sx_out(0)

            def one(b, p, m, n):
                par, z = m % 2, m // 2
                for e in range(NE):
                    if has(n, 0):
                        dve.wait_ge(sem("S_done"), b * 4 + e + 1)
                        dve.tensor_reduce(negmax[:, e, :], ps[:, e, :].rearrange("p (n t) -> p n t", t=P), AX.X,
                                          ALU.max, negate=True).then_inc(sem("max_done"), 1)
                    if has(n, 1, NT + 1):
                        dve.wait_ge(sem("T_done"), b * 4 + e - 3)
                        if n is None or n >= 3:
                            dve.wait_ge(sem("AV_done"), b - 2)
                        dve.tensor_copy(PT[:, (m + 1) % 2, e, :], ps[:, 4 + e % 2, :]).then_inc(sem("PT_out"), 1)
                if par == 0 and has(n, 0, NT - 2):
                    sx_out(p + 1)
                if has(n, 2, NT + 2):
                    dve.wait_ge(sem("ATt_done"), b - 1)
                    at = ps[:, 6, :].rearrange("p (e n d) -> p e n d", e=NE, n=NH)
                    dve.reciprocal(rl[:, :, :], at[:, :, :, D:D + 1].rearrange("p e n d -> p e (n d)"))\
                        .then_inc(sem("rl_done"), 1)
                    dve.wait_ge(sem("rl_done"), b - 1)
                    dve.tensor_tensor(O1[:, :].rearrange("p (n e d) -> p e n d", n=NH, e=NE), at[:, :, :, 0:D],
                                      rl[:, :, :].unsqueeze(3).broadcast_to((P, NE, NH, D)), ALU.mult)\
                        .then_inc(sem("O1_done"), 1)
                    dve.wait_ge(sem("O1_done"), b - 1)
                    if n is None or n >= 4:
                        dve.wait_ge(sem("O_copied"), b - 3)
                        dve.wait_ge(sem("OT_done"), b - 3)
                    keep = kept[:, bass.ds(b - 2, 1), :].rearrange("p t (n d) -> p (t n) d", d=D).unsqueeze(2)\
                        .broadcast_to((P, NH, NE, D))
                    dve.tensor_tensor(Ost[:, par, :].rearrange("p (n e d) -> p n e d", n=NH, e=NE), keep,
                                      O1[:, :].rearrange("p (n e d) -> p n e d", n=NH, e=NE), ALU.mult)\
                        .then_inc(sem("O_done"), 1)
            batches(dve, one)
            tail_dve(dve, ch)

        def tail_act(act):
            act.wait_ge(sem("gs_shifted"), 1)
            act.activation(GL[:, :, :], GL[:, :, :], ACT.Exp).then_inc(sem("gs_exp"), 1)
            ln_act(act, "mix", stD)
            for q in range(0, NQ, 2):
                act.wait_ge(sem("pairs_turned"), turned("fx", q))
                act.activation(xT[:, q * BANK:(q + 1) * BANK], ps[:, q, :], ACT.Copy).then_inc(sem("pairs_out0"), 1)
            for q in range(NQ):
                act.wait_ge(sem("fc1_done"), q + 1)
                act.activation(hxT[:, q * BANK:(q + 1) * BANK], ps[:, 4 + q, :], ACT.Relu,
                               bias=cols[:, FC1_B:FC1_B + 1]).then_inc(sem("hxT_relu"), 1)
            ln_act(act, "hx", stD)
            for q in range(0, NQ, 2):
                act.wait_ge(sem("pairs_turned"), turned("fo", q))
                act.activation(xT[:, q * BANK:(q + 1) * BANK], ps[:, 4 + q, :], ACT.Copy).then_inc(sem("pairs_out0"), 1)
            act.wait_ge(sem("fg_shifted"), 1)
            act.activation(fg[:, :], fg[:, :], ACT.Exp).then_inc(sem("fg_exp"), 1)

        def tail_dve(dve, ch):
            glv = GL[:, :, :].rearrange("p t (n e) -> p (t n) e", e=NE)
            m, r = stD[:, 0, :], stD[:, 1, :]
            dve.wait_ge(sem("rows_in"), 16 * ROW_LOADS)
            dve.wait_ge(sem("gl_out"), NT)
            ch(dve.tensor_tensor(GL[:, :, :], GL[:, :, :], row(rows[:, GATE_B, 0:NH * NE], NT), ALU.add))
            ch(dve.tensor_reduce(m, glv, AX.X, ALU.max))
            dve.tensor_tensor(glv, glv, bc(m, NE), ALU.subtract).then_inc(sem("gs_shifted"), 1)
            for n in range(NH):
                last = dve.tensor_copy(resid[:, n * D:(n + 1) * D], sx[:, n, n * D:(n + 1) * D])
            ch(last)
            dve.wait_ge(sem("gs_exp"), 1)
            ch(dve.tensor_reduce(r, glv, AX.X, ALU.add))
            ch(dve.reciprocal(r, r))
            ch(dve.tensor_tensor(glv, glv, bc(r, NE), ALU.mult))
            dve.wait_ge(sem("O_copied"), NT)
            ch(dve.tensor_tensor(mixp, O_all.rearrange("p t (g d) -> p (t g) d", d=D),
                                 bc(GL[:, :, :].rearrange("p t g -> p (t g)"), D), ALU.mult))
            ch(dve.tensor_reduce(fn[:, :, :].rearrange("p t (n d) -> p (t n) d", d=D),
                                 mixp.rearrange("p (g e) d -> p g d e", e=NE), AX.X, ALU.add))
            ch(dve.tensor_tensor(fn[:, :, :], fn[:, :, :], row(resid[:, :], NT), ALU.add))

            def norm_affine(name, g, b, done):
                x = layer_norm_stats(dve, ch, name, fn[:, :, :].rearrange("p t (n d) -> p (t n) d", d=D), stD,
                                     FFN_EPS, D)
                ch(dve.tensor_tensor(x, x, bc(stD[:, 2, :], D), ALU.mult))
                ch(dve.tensor_tensor(xc[:, :, :], xc[:, :, :], row(rows[:, g, :], NT), ALU.mult))
                dve.tensor_tensor(fn[:, :, :], xc[:, :, :], row(rows[:, b, :], NT), ALU.add).then_inc(sem(done), 1)

            norm_affine("mix", LN_G, LN_B, "fx_ready")
            for q in range(1, NQ, 2):
                dve.wait_ge(sem("pairs_turned"), turned("fx", q))
                dve.tensor_copy(xT[:, q * BANK:(q + 1) * BANK], ps[:, q, :]).then_inc(sem("pairs_out1"), 1)
            dve.wait_ge(sem("pairs_out1"), turned_out("fx", NQ - 1))
            dve.wait_ge(sem("pairs_out0"), turned_out("fx", NQ - 1))
            for q in range(NQ):
                c = slice(q * BANK, (q + 1) * BANK)
                dve.wait_ge(sem("hxT_relu"), q + 1)
                dve.scalar_tensor_tensor(hxT[:, c], xT[:, c], 0.0, hxT[:, c], ALU.not_equal, ALU.mult)\
                    .then_inc(sem("hxT_ready"), 1)
            dve.wait_ge(sem("fx_ready"), 1)
            dve.wait_ge(sem("fc2_done"), 1)
            ch(dve.tensor_tensor(xc[:, :, :], ps[:, 0:4, :].rearrange("p k (t c) -> p (k t) c", c=C),
                                 row(rows[:, FC2_B, :], NT), ALU.add))
            ch(dve.scalar_tensor_tensor(xc[:, :, :], fn[:, :, :], 0.0, xc[:, :, :], ALU.not_equal, ALU.mult))
            ch(dve.tensor_tensor(fn[:, :, :], fn[:, :, :], xc[:, :, :], ALU.add))
            norm_affine("hx", FN_G, FN_B, "fo_ready")
            for q in range(1, NQ, 2):
                dve.wait_ge(sem("pairs_turned"), turned("fo", q))
                dve.tensor_copy(xT[:, q * BANK:(q + 1) * BANK], ps[:, 4 + q, :]).then_inc(sem("pairs_out1"), 1)
            fgv = fg[:, :].rearrange("p (t n) -> p t n", n=NH)
            m, r = st[0][:, 0, :], st[0][:, 1, :]
            dve.wait_ge(sem("fg_done"), 1)
            ch(dve.tensor_reduce(m, ps[:, 0, 0:NT * NH].rearrange("p (t n) -> p t n", n=NH), AX.X, ALU.max))
            dve.tensor_tensor(fgv, ps[:, 0, 0:NT * NH].rearrange("p (t n) -> p t n", n=NH), bc(m, NH), ALU.subtract)\
                .then_inc(sem("fg_shifted"), 1)
            dve.wait_ge(sem("fg_exp"), 1)
            ch(dve.tensor_reduce(r, fgv, AX.X, ALU.add))
            ch(dve.reciprocal(r, r))
            ch(dve.tensor_tensor(fgv, fgv, bc(r, NH), ALU.mult))
            ch(dve.tensor_tensor(xc[:, :, :].rearrange("p t (n d) -> p (t n) d", d=D),
                                 fn[:, :, :].rearrange("p t (n d) -> p (t n) d", d=D), bc(fg[:, :], D), ALU.mult))
            ch(dve.tensor_tensor(h[:, :, :], h[:, :, :], xc[:, :, :], ALU.add))

        def tail_pe(pe):
            pe.wait_ge(sem("fx_ready"), 1)
            transpose_pairs(pe, fn)
            for q in range(NQ):
                pe.wait_ge(sem(f"pairs_out{q % 2}"), turned_out("fx", q))
                pe.matmul(ps[:, 4 + q, :], wT_fc1, xT[:, q * BANK:(q + 1) * BANK], start=True, stop=True)\
                    .then_inc(sem("fc1_done"), 1)
            for p in range(NP):
                if p % 4 == 0:
                    pe.wait_ge(sem("hxT_ready"), p // 4 + 1)
                last = pe.matmul(ps[:, p // 4, p % 4 * P:(p % 4 + 1) * P], hxT[:, p * P:(p + 1) * P], wT_fc2,
                                 start=True, stop=True)
            last.then_inc(sem("fc2_done"), 1)
            pe.wait_ge(sem("fo_ready"), 1)
            transpose_pairs(pe, fn, 4)
            for p in range(NP):
                if p % 4 == 0:
                    pe.wait_ge(sem(f"pairs_out{p // 4 % 2}"), turned_out("fo", p // 4))
                last = pe.matmul(ps[:, 0, p * 2 * NH:(p + 1) * 2 * NH], xT[:, p * P:(p + 1) * P], wT_fg,
                                 start=True, stop=True)
            last.then_inc(sem("fg_done"), 1)

        def seq(x):
            return x.rearrange("p (b t) -> p b t", t=P)

        def pairs_out(eng, name, first_bank, q, dst, scale=None, bias=None):
            eng.wait_ge(sem("pairs_turned"), turned(name, q))
            src, dst = ps[:, first_bank + q, :], dst[:, q * BANK:(q + 1) * BANK]
            if q % 2:
                if scale is None:
                    ins = eng.tensor_copy(dst, src)
                else:
                    ins = eng.tensor_scalar(dst, src, scale, bias, ALU.mult, ALU.add)
            elif scale is None:
                ins = eng.activation(dst, src, ACT.Copy)
            else:
                ins = eng.activation(dst, src, ACT.Identity, scale=scale, bias=bias)
            ins.then_inc(sem(f"pairs_out{q % 2}"), 1)

        def col(i):
            return cols[:, i:i + 1]

        def banks(first):
            return ps[:, first:first + NQ, :].rearrange("p k n -> p (k n)")

        def recurrent_pool(pool):
            pool.wait_ge(sem("fg_done"), 1)
            pool.memset(seq(k_last)[:, :, 0:1], NEG).then_inc(sem("starts_ready"), 1)
            pool.memset(seq(A2)[:, :, 0:1], 0.0).then_inc(sem("starts_ready"), 1)
            pool.memset(seq(E2)[:, :, 0:1], 0.0).then_inc(sem("starts_ready"), 1)
            pool.memset(seq(EV)[:, :, 0:1], 0.0).then_inc(sem("starts_ready"), 1)

        def recurrent_act(act):
            ln_act(act, "ln3", st[0])
            ln_act(act, "ln4", st[1])
            for q in range(0, NQ, 2):
                pairs_out(act, "x4", 0, q, hT, col(G1), col(B1))
            act.wait_ge(sem("starts_ready"), 4)
            act.wait_ge(sem("k_proj"), NQ)
            act.activation(seq(k_last)[:, :, 1:], seq(banks(4))[:, :, 0:P - 1], ACT.Copy).then_inc(sem("k_shifted"), 1)
            act.wait_ge(sem("v_proj"), NQ)
            act.activation(vT, banks(0), ACT.Copy).then_inc(sem("vT_ready"), 1)
            act.wait_ge(sem("r_proj"), NQ)
            act.activation(srT, banks(4), ACT.Sigmoid).then_inc(sem("srT_ready"), 1)
            act.wait_ge(sem("A2_log"), 1)
            act.activation(seq(A2)[:, :, 1:], seq(A2)[:, :, 1:], ACT.Exp, bias=col(W_COL)).then_inc(sem("A2_ready"), 1)
            act.wait_ge(sem("E2_log"), 1)
            act.activation(seq(E2)[:, :, 1:], seq(E2)[:, :, 1:], ACT.Exp).then_inc(sem("E2_ready"), 1)
            act.wait_ge(sem("A_log"), 1)
            act.activation(O_prev, O_prev, ACT.Exp).then_inc(sem("A_ready"), 1)
            act.wait_ge(sem("E_log"), 1)
            act.activation(kT, kT, ACT.Exp).then_inc(sem("E_ready"), 1)
            ln_act(act, "ln5", st[0])
            for q in range(0, NQ, 2):
                pairs_out(act, "x5", 4, q, hT, col(G2), col(B2))
            for q in range(NQ):
                for i in range(0, 4, 2):
                    act.wait_ge(sem("kk_proj"), 4 * q + i + 1)
                    dst = hidT[:, i, q * BANK:(q + 1) * BANK]
                    act.activation(dst, ps[:, (4 * q + i) % 8, :], ACT.Relu).then_inc(sem("kk_relu"), 1)
                    act.wait_ge(sem("kk_relu"), 2 * q + i // 2 + 1)
                    act.activation(dst, dst, ACT.Square).then_inc(sem("kk_act"), 1)
            act.wait_ge(sem("rf_proj"), NQ)
            act.activation(srfT, banks(4), ACT.Sigmoid).then_inc(sem("srfT_ready"), 1)

        def recurrent_dve(dve, ch):
            ch(dve.tensor_scalar(col(W_COL), col(DECAY), 1.0 / P, None, ALU.mult))
            ch(dve.tensor_scalar(col(U_COL), col(FIRST), 1.0 / P, None, ALU.mult))
            layer_norm_stats(dve, ch, "ln3", h[:, :, :], st[0])
            ch(dve.tensor_tensor(fn[:, :, :], xc[:, :, :], bc(st[0][:, 2, :], C), ALU.mult))
            layer_norm_stats(dve, ch, "ln4", fn[:, :, :], st[1])
            dve.tensor_tensor(xc[:, :, :], xc[:, :, :], bc(st[1][:, 2, :], C), ALU.mult).then_inc(sem("x4_ready"), 1)
            dve.tensor_copy(W_t, col(W_COL).broadcast_to((P, TP))).then_inc(sem("W_t_filled"), 1)
            dve.wait_ge(sem("W_t_filled"), 1)
            ch(dve.memset(seq(W_t)[:, :, 0:1], NEG))
            for q in range(1, NQ, 2):
                pairs_out(dve, "x4", 0, q, hT, col(G1), col(B1))
            dve.wait_ge(sem("k_shifted"), 1)
            dve.tensor_copy(kT, banks(4)).then_inc(sem("kT_ready"), 1)
            ch(dve.tensor_tensor_scan(O_prev, W_t, k_last, 0.0, ALU.add, ALU.max))
            dve.tensor_tensor(seq(A2)[:, :, 1:], seq(O_prev)[:, :, 0:P - 1], seq(O_prev)[:, :, 1:], ALU.subtract)\
                .then_inc(sem("A2_log"), 1)
            dve.wait_ge(sem("kT_ready"), 1)
            dve.tensor_tensor(seq(E2)[:, :, 1:], seq(kT)[:, :, 0:P - 1], seq(O_prev)[:, :, 1:], ALU.subtract)\
                .then_inc(sem("E2_log"), 1)
            no = W_t
            ch(dve.scalar_tensor_tensor(no, kT, col(U_COL), O_prev, ALU.add, ALU.max))
            dve.wait_ge(sem("E2_log"), 1)
            dve.scalar_tensor_tensor(kT, kT, col(U_COL), no, ALU.add, ALU.subtract).then_inc(sem("E_log"), 1)
            dve.wait_ge(sem("A2_log"), 1)
            dve.tensor_tensor(O_prev, O_prev, no, ALU.subtract).then_inc(sem("A_log"), 1)
            dve.wait_ge(sem("E2_ready"), 1)
            dve.wait_ge(sem("vT_ready"), 1)
            ch(dve.tensor_tensor(seq(EV)[:, :, 1:], seq(E2)[:, :, 1:], seq(vT)[:, :, 0:P - 1], ALU.mult))
            dve.wait_ge(sem("A2_ready"), 1)
            ch(dve.tensor_tensor_scan(P_prev, A2, EV, 0.0, ALU.mult, ALU.add))
            ch(dve.tensor_tensor_scan(Q_prev, A2, E2, 0.0, ALU.mult, ALU.add))
            dve.wait_ge(sem("A_ready"), 1)
            dve.wait_ge(sem("E_ready"), 1)
            ch(dve.tensor_tensor(P_prev, O_prev, P_prev, ALU.mult))
            ch(dve.tensor_tensor(Q_prev, O_prev, Q_prev, ALU.mult))
            ch(dve.tensor_tensor(vT, kT, vT, ALU.mult))
            ch(dve.tensor_tensor(P_prev, P_prev, vT, ALU.add))
            ch(dve.tensor_tensor(Q_prev, Q_prev, kT, ALU.add))
            ch(dve.reciprocal(Q_prev, Q_prev))
            ch(dve.tensor_tensor(P_prev, P_prev, Q_prev, ALU.mult))
            dve.wait_ge(sem("srT_ready"), 1)
            dve.tensor_tensor(P_prev, P_prev, srT, ALU.mult).then_inc(sem("ysT_ready"), 1)
            dve.wait_ge(sem("o_proj"), 1)
            ch(dve.tensor_tensor(fn[:, :, :], fn[:, :, :], banks(0).rearrange("p (t c) -> p t c", c=C), ALU.add))
            layer_norm_stats(dve, ch, "ln5", fn[:, :, :], st[0])
            dve.tensor_tensor(xc[:, :, :], xc[:, :, :], bc(st[0][:, 2, :], C), ALU.mult).then_inc(sem("x5_ready"), 1)
            ch(dve.tensor_tensor(h[:, :, :], h[:, :, :], fn[:, :, :], ALU.add))
            for q in range(1, NQ, 2):
                pairs_out(dve, "x5", 4, q, hT, col(G2), col(B2))
            for q in range(NQ):
                for i in range(1, 4, 2):
                    dve.wait_ge(sem("kk_proj"), 4 * q + i + 1)
                    src, dst = ps[:, (4 * q + i) % 8, :], hidT[:, i, q * BANK:(q + 1) * BANK]
                    ch(dve.tensor_scalar(dst, src, 0.0, None, ALU.max))
                    dve.tensor_tensor(dst, dst, dst, ALU.mult).then_inc(sem("kk_dve"), 1)
            dve.wait_ge(sem("srfT_ready"), 1)
            dve.wait_ge(sem("ff_proj"), NQ)
            dve.tensor_tensor(gatedT, srfT, banks(0), ALU.mult).then_inc(sem("gatedT_ready"), 1)
            dve.wait_ge(sem("gated_T"), NQ)
            ch(dve.tensor_tensor(h[:, :, :], h[:, :, :], banks(4).rearrange("p (t c) -> p t c", c=C), ALU.add))

        def recurrent_pe(pe):
            pe.wait_ge(sem("x4_ready"), 1)
            transpose_pairs(pe, xc)
            pe.wait_ge(sem("wl_in"), 16 * WL_LOADS)
            pe.wait_ge(sem("pairs_out0"), turned_out("x4", NQ - 1))
            pe.wait_ge(sem("pairs_out1"), turned_out("x4", NQ - 1))
            project(pe, w_bd[:, WK, :], hT, "k_proj", 4)
            project(pe, w_bd[:, WV, :], hT, "v_proj", 0)
            pe.wait_ge(sem("kT_ready"), 1)
            project(pe, w_bd[:, WR, :], hT, "r_proj", 4)
            pe.wait_ge(sem("ysT_ready"), 1)
            for p in range(NP):
                last = pe.matmul(ps[:, p // 4, p % 4 * P:(p % 4 + 1) * P], P_prev[:, p * P:(p + 1) * P],
                                 w_bd[:, WO, :], start=True, stop=True)
            last.then_inc(sem("o_proj"), 1)
            pe.wait_ge(sem("x5_ready"), 1)
            transpose_pairs(pe, xc, 4)
            pe.wait_ge(sem("pairs_out0"), turned_out("x5", NQ - 1))
            pe.wait_ge(sem("pairs_out1"), turned_out("x5", NQ - 1))
            for q in range(NQ):
                if q >= 2:
                    pe.wait_ge(sem("kk_act"), 2 * q - 2)
                    pe.wait_ge(sem("kk_dve"), 2 * q - 2)
                for i in range(4):
                    pe.matmul(ps[:, (4 * q + i) % 8, :], w_kf[:, i // 2, i % 2 * P:(i % 2 + 1) * P],
                              hT[:, q * BANK:(q + 1) * BANK], start=True, stop=True).then_inc(sem("kk_proj"), 1)
            pe.wait_ge(sem("kk_act"), 2 * NQ)
            pe.wait_ge(sem("kk_dve"), 2 * NQ)
            project(pe, w_bd[:, WRF, :], hT, "rf_proj", 4)
            for q in range(NQ):
                for par in range(2):
                    for k in range(2):
                        last = pe.matmul(ps[par * C:(par + 1) * C, q, :], w_vf[:, k, :],
                                         hidT[:, 2 * par + k, q * BANK:(q + 1) * BANK], start=k == 0, stop=k == 1)
                last.then_inc(sem("ff_proj"), 1)
            pe.wait_ge(sem("gatedT_ready"), 1)
            for p in range(NP):
                last = pe.transpose(ps[:, 4 + p // 4, p % 4 * P:(p % 4 + 1) * P], gatedT[:, p * P:(p + 1) * P], ident[:, :])
                if p % 4 == 3:
                    last.then_inc(sem("gated_T"), 1)

        def experts_act(act):
            ln_act(act, "ln6", st[1])
            for q in range(0, NQ, 2):
                pairs_out(act, "x6", 0, q, hT)
            for q in range(NQ):
                for i in range(4):
                    act.wait_ge(sem("hid_proj"), 4 * q + i + 1)
                    act.activation(hidT[:, i, q * BANK:(q + 1) * BANK], ps[:, (4 * q + i) % 8, :], ACT.Gelu,
                                   bias=col(HID_B + i % 2)).then_inc(sem("hid_ready"), 1)
            act.wait_ge(sem("lgT_done"), 1)
            act.activation(lgT, ps[0:C, 0:NQ, :].rearrange("p k n -> p (k n)"), ACT.Copy).then_inc(sem("lgT_ready"), 1)
            act.wait_ge(sem("route_shifted"), 1)
            act.activation(coef[:, :, :], tmp8[:, :, :], ACT.Exp).then_inc(sem("route_exp"), 1)
            act.wait_ge(sem("coefT_done"), 1)
            act.activation(coefT[:, :], ps[:, 6, 0:2 * P], ACT.Copy).then_inc(sem("coefT_ready"), 1)

        def experts_dve(dve, ch):
            layer_norm_stats(dve, ch, "ln6", h[:, :, :], st[1])
            dve.tensor_tensor(fn[:, :, :], xc[:, :, :], bc(st[1][:, 2, :], C), ALU.mult).then_inc(sem("x6_ready"), 1)
            for q in range(1, NQ, 2):
                pairs_out(dve, "x6", 0, q, hT)
            m, r = st[0][:, 0, :], st[0][:, 1, :]
            dve.wait_ge(sem("lg_done"), 1)
            lg = ps[:, 4:6, :].rearrange("p k (t e) -> p (k t) e", e=32)[:, :, 0:EX]
            ch(dve.tensor_tensor(tmp8[:, :, :], lg, row(rows[:, EX_B, 0:EX], NT), ALU.add))
            ch(dve.tensor_reduce(m, tmp8[:, :, :], AX.X, ALU.max))
            dve.tensor_tensor(tmp8[:, :, :], tmp8[:, :, :], bc(m, EX), ALU.subtract).then_inc(sem("route_shifted"), 1)
            dve.wait_ge(sem("route_exp"), 1)
            ch(dve.tensor_reduce(r, coef[:, :, :], AX.X, ALU.add))
            ch(dve.reciprocal(r, r))
            ch(dve.tensor_tensor(coef[:, :, :], coef[:, :, :], bc(r, EX), ALU.mult))
            ch(dve.tensor_reduce(m, coef[:, :, :], AX.X, ALU.max))
            ch(dve.tensor_tensor(tmp8[:, :, :], coef[:, :, :], bc(m, EX), ALU.is_equal))
            dve.wait_ge(sem("rank_ready"), 1)
            ch(dve.tensor_tensor(tmp8[:, :, :], tmp8[:, :, :], row(rank[:, :], NT), ALU.mult))
            ch(dve.tensor_reduce(r, tmp8[:, :, :], AX.X, ALU.max))
            ch(dve.tensor_tensor(tmp8[:, :, :], tmp8[:, :, :], bc(r, EX), ALU.is_equal))
            dve.tensor_tensor(coef[:, :, :], coef[:, :, :], tmp8[:, :, :], ALU.mult).then_inc(sem("coef_ready"), 1)
            dve.wait_ge(sem("coef_ready"), 1)
            for t in range(NT):
                dve.wait_ge(sem("y_done"), t + 1)
                y = scratch[:, t % 4, :]
                dve.tensor_tensor(y.rearrange("p (e c) -> p e c", e=EX),
                                  ps[:, t % 4, :].rearrange("p (e c) -> p e c", e=EX), bc(coef[:, t, :], C), ALU.mult)\
                    .then_inc(sem("y_weighted"), 1)
                dve.wait_ge(sem("y_weighted"), t + 1)
                ch(dve.tensor_reduce(xp[:, t, :], y.rearrange("p (e c) -> p c e", e=EX), AX.X, ALU.add))
            for half in range(2):
                ts = slice(half * NP, (half + 1) * NP)
                dve.wait_ge(sem("bias_done"), half + 1)
                ch(dve.tensor_tensor(h[:, ts, :], h[:, ts, :],
                                     ps[:, 4:6, :].rearrange("p k (t c) -> p (k t) c", c=C), ALU.add))
                dve.tensor_tensor(h[:, ts, :], h[:, ts, :], xp[:, ts, :], ALU.add).then_inc(sem("h_done"), 1)

        def experts_pe(pe):
            pe.wait_ge(sem("x6_ready"), 1)
            transpose_pairs(pe, fn)
            pe.wait_ge(sem("pairs_out0"), turned_out("x6", NQ - 1))
            pe.wait_ge(sem("pairs_out1"), turned_out("x6", NQ - 1))
            for q in range(NQ):
                if q >= 2:
                    pe.wait_ge(sem("hid_ready"), 4 * q - 4)
                for i in range(4):
                    pe.matmul(ps[:, (4 * q + i) % 8, :], w_1[:, i // 2, i % 2 * P:(i % 2 + 1) * P],
                              hT[:, q * BANK:(q + 1) * BANK], start=True, stop=True).then_inc(sem("hid_proj"), 1)
            pe.wait_ge(sem("hid_ready"), 4 * NQ)
            for q in range(NQ):
                for par in range(2):
                    for k in range(2):
                        last = pe.matmul(ps[32 * par:32 * par + 32, q, :], w_g[:, k, :],
                                         hidT[:, 2 * par + k, q * BANK:(q + 1) * BANK], start=k == 0, stop=k == 1)
            last.then_inc(sem("lgT_done"), 1)
            pe.wait_ge(sem("lgT_ready"), 1)
            for p in range(NP):
                last = pe.transpose(ps[:, 4 + p // 8, p % 8 * C:(p % 8 + 1) * C], lgT[:, p * P:(p + 1) * P],
                                    ident[0:C, 0:C])
            last.then_inc(sem("lg_done"), 1)
            for t in range(NT):
                if t == 4:
                    pe.wait_ge(sem("coef_ready"), 1)
                    for half in range(2):
                        last = pe.transpose(ps[:, 6, half * P:(half + 1) * P],
                                            coef[:, half * NP:(half + 1) * NP, :].rearrange("p t e -> p (t e)"),
                                            ident[:, :])
                    last.then_inc(sem("coefT_done"), 1)
                if t >= 4:
                    pe.wait_ge(sem("y_weighted"), t - 3)
                for k in range(2):
                    last = pe.matmul(ps[:, t % 4, :], hidT[:, t % 2 * 2 + k, t // 2 * P:(t // 2 + 1) * P],
                                     w_d[:, k, :], start=k == 0, stop=k == 1)
                last.then_inc(sem("y_done"), 1)
            pe.wait_ge(sem("coefT_ready"), 1)
            for half in range(2):
                if half:
                    pe.wait_ge(sem("h_done"), half)
                for k in range(2):
                    last = pe.matmul(ps[:, 4 + k, :], coefT[:, half * P:(half + 1) * P], w_bias[:, k * BANK:(k + 1) * BANK],
                                     start=True, stop=True)
                last.then_inc(sem("bias_done"), 1)

        @block.sync
        def _(sp):
            sp.dma_start(x_int[:, :], a["x"]).then_inc(sem("x_in"), 16)
            sp.dma_start(wproj[:, :], a["L0_tok_w_proj"]).then_inc(sem("wproj_in"), 16)
            sp.dma_start(gate_w[:, :], a["fside_1S_w_gate"].partition_broadcast(P)).then_inc(sem("gate_in"), 16)
            sp.dma_start(gate_b[:, :], a["L0_tok_b_gate"].unsqueeze(0).partition_broadcast(P)).then_inc(sem("gate_in"), 16)
            sp.wait_ge(sem("wn_zeroed"), 1)

            def put(r, c, src):
                n, m = src.shape
                sp.dma_start(wn[r:r + n, c:c + m], src).then_inc(sem("wn_in"), 16)
                wn_loads.append(1)

            for par in range(2):
                put(par * C, WCOL["hl"] + par * C, a["L0_ffn_hl_w"].rearrange("n d h -> (n d) h"))
                for n in range(NH):
                    r = par * C + n * D
                    for ep in range(2):
                        put(r, WCOL[f"wq{ep}"] + C + n * D, a["L0_ffn_wq"][n, 2 * ep + par])
                    put(r, WCOL["wk"] + C + n * D, a["L0_ffn_wk"][n])
                    put(r, WCOL["wv"] + r, a["L0_ffn_wv"][n])
                    put(r, WCOL["fc1"] + r, a["L0_ffn_fc1_w"])
                    put(r, WCOL["fc2"] + r, a["L0_ffn_fc2_w"])
                put(par * NH, WCOL["fg"] + par * C, a["L0_ffn_fgate_w"])
            for n in range(NH):
                put(n * NE, WCOL[f"gate{n // 2}"] + n % 2 * C, a["L0_ffn_gate_w"][n])
            assert len(wn_loads) == WN_LOADS

            def vector_col(i, src):
                n = src.shape[0]
                for r in range(0, P, n):
                    sp.dma_start(cols[r:r + n, i:i + 1], src.unsqueeze(1)).then_inc(sem("cols_in"), 16)
                    col_loads.append(1)

            def vector_row(i, src):
                n = src.shape[0]
                for r in range(0, C, n):
                    if i == GATE_B and r:
                        break
                    sp.dma_start(rows[:, i, r:r + n], src.unsqueeze(0).partition_broadcast(P))\
                        .then_inc(sem("rows_in"), 16)
                    row_loads.append(1)

            vector_col(HL_B, a["L0_ffn_hl_b"].rearrange("n d -> (n d)"))
            vector_col(FC1_B, a["L0_ffn_fc1_b"])
            for i, name in ((G1, "g1"), (B1, "b1"), (G2, "g2"), (B2, "b2"), (DECAY, "spatial_decay"),
                            (FIRST, "spatial_first")):
                vector_col(i, a[f"L1_attn_{name}"])
            for k in range(2):
                vector_col(HID_B + k, a["L1_ffn_b1"][k * P:(k + 1) * P])
            sp.dma_start(rows[:, EX_B, 0:EX], a["L1_ffn_bg"].unsqueeze(0).partition_broadcast(P))\
                .then_inc(sem("rows_in"), 16)
            row_loads.append(1)
            for i, name in ((LN_G, "ln_g"), (LN_B, "ln_b"), (FN_G, "fnorm_g"), (FN_B, "fnorm_b"), (FC2_B, "fc2_b")):
                vector_row(i, a[f"L0_ffn_{name}"])
            vector_row(GATE_B, a["L0_ffn_gate_b"].rearrange("n e -> (n e)"))
            assert (len(col_loads), len(row_loads)) == (COL_LOADS, ROW_LOADS)
            if stop_after >= 3:
                sp.wait_ge(sem("wl_zeroed"), 1)
                L = "L1_attn_"
                for i, name in ((WK, "Wk"), (WV, "Wv"), (WR, "Wr"), (WO, "Wo"), (WRF, "Wr_ffn")):
                    for par in range(2):
                        r = slice(par * C, (par + 1) * C)
                        sp.dma_start(w_bd[r, i, r], a[L + name]).then_inc(sem("wl_in"), 16)
                for par in range(2):
                    r = slice(par * C, (par + 1) * C)
                    sp.dma_start(w_kf[r, par, :], a[L + "Wk_ffn"]).then_inc(sem("wl_in"), 16)
                    sp.dma_start(w_1[r, par, :], a["L1_ffn_W1"]).then_inc(sem("wl_in"), 16)
                sp.dma_start(w_vf[:, :, :], a[L + "Wv_ffn"].rearrange("(k p) c -> p k c", p=P)).then_inc(sem("wl_in"), 16)
                sp.dma_start(w_g[:, :, 0:EX], a["L1_ffn_Wg"].rearrange("(k p) c -> p k c", p=P)).then_inc(sem("wl_in"), 16)
                for k in range(2):
                    sp.dma_start(w_d[:, k, :].rearrange("p (e c) -> p e c", e=EX),
                                 a["L1_ffn_Wd"][:, k * P:(k + 1) * P, :].rearrange("e p c -> p e c"))\
                        .then_inc(sem("wl_in"), 16)
                for i in range(P // EX):
                    sp.dma_start(w_bias[i * EX:(i + 1) * EX, i * C:(i + 1) * C], a["L1_ffn_bd"]).then_inc(sem("wl_in"), 16)
            sp.wait_ge(sem("h_done"), 2 if stop_after == 4 else 1)
            sp.dma_start(out.rearrange("b s c -> s b c"), h[:, :, :]).then_inc(sem("out_stored"), 16)
            sp.wait_ge(sem("out_stored"), 16)

        @block.gpsimd
        def _(pool):
            ch = Chain(pool, "pool_chain")
            ch(pool.memset(ident[:, :], 0.0))
            ch(pool.memset(ident2[:, :], 0.0))
            pool.affine_select(out=ident[:, :], in_=ident[:, :], compare_op=ALU.not_equal, fill=1.0,
                               base=0, pattern=[[-1, P]], channel_multiplier=1).then_inc(sem("ident_ready"), 1)
            ch(pool.affine_select(out=ident2[:, :], in_=ident2[:, :], compare_op=ALU.not_equal, fill=1.0,
                                  base=0, pattern=[[-1, C]], channel_multiplier=1))
            ch(pool.affine_select(out=ident2[:, :], in_=ident2[:, :], compare_op=ALU.not_equal, fill=1.0,
                                  base=-C, pattern=[[-1, C]], channel_multiplier=1))
            pool.wait_ge(sem("ident_ready"), 1)
            ch(pool.memset(zero16[:, :], 0.0))
            pool.tensor_copy(ident16[:, :], ident[:, :]).then_inc(sem("ident_ready"), 1)
            pool.memset(wn[:, :], 0.0).then_inc(sem("wn_zeroed"), 1)
            pool.wait_ge(sem("idx_ready"), 1)
            for t in range(NT):
                where = bass.IndirectOffsetOnAxis(ap=idx[:, t:t + 1], axis=0)
                for table, dst in (("L0_tok_fourier_table", geo_raw[:, t, 0:FOUR]),
                                   ("L0_tok_visit_table", geo_raw[:, t, FOUR:GEO]),
                                   ("L0_tok_emb_table", gate_in[:, t, 0:EMB])):
                    pool.indirect_dma_start(out=dst, out_offset=None, in_=a[table], in_offset=where)\
                        .then_inc(sem(f"gathered{t // GT}"), 16)
            ch(pool.tensor_copy(ident_bf[:, :], ident[:, :]))
            ch(pool.memset(masked[:, :, :], 0.0))
            ch(pool.affine_select(out=masked[:, :, :], in_=masked[:, :, :], compare_op=ALU.is_ge, fill=MASKED,
                                  base=0, pattern=[[0, NH], [-1, P]], channel_multiplier=1))
            ch(pool.memset(own_rows[:, :], 1.0))
            ch(pool.affine_select(out=own_rows[:, :], in_=own_rows[:, :], compare_op=ALU.is_ge, fill=0.0,
                                  base=0, pattern=[[-D, 2 * NH]], channel_multiplier=1))
            pool.affine_select(out=own_rows[:, :], in_=own_rows[:, :], compare_op=ALU.is_ge, fill=0.0,
                               base=D - 1, pattern=[[D, 2 * NH]], channel_multiplier=-1)\
                .then_inc(sem("masks_ready"), 1)
            if stop_after < 2:
                return
            heads_pool(pool)
            if stop_after < 3:
                return
            recurrent_pool(pool)

        @block.scalar
        def _(act):
            ch = Chain(act, "act_chain")
            for g in range(NT // 4):
                act.wait_ge(sem("geo_transposed"), g + 1)
                if g >= 2:
                    act.wait_ge(sem("geo_projected"), g - 1)
                act.activation(geoT[:, g % 2, :], ps[0:GEO, g % 2, :], ACT.Copy).then_inc(sem("geoT_ready"), 1)
            for i, (lo, hi, bank, off) in enumerate(((0, 512, 4, 0), (512, 1024, 5, 0), (1024, 1320, 6, P))):
                act.wait_ge(sem("wT_done"), i + 1)
                act.activation(WT[:, lo:hi], ps[:, bank, off:off + hi - lo], ACT.Copy).then_inc(sem("WT_ready"), 1)
            act.wait_ge(sem("glogit_ready"), 1)
            act.activation(gate[:, :], glogit[:, :], ACT.Exp, scale=-1.0).then_inc(sem("gate_exp"), 1)
            ln_act(act, "ln1", st[0])
            act.activation(st[0][:, 7, :], st[0][:, 3, :], ACT.Sqrt).then_inc(sem("ss_root"), 1)
            if stop_after < 1:
                return
            attention_act(act)
            if stop_after < 2:
                return
            heads_act(act)
            if stop_after < 3:
                return
            recurrent_act(act)
            if stop_after < 4:
                return
            experts_act(act)

        @block.vector
        def _(dve):
            ch = Chain(dve, "dve_chain")
            dve.wait_ge(sem("x_in"), 16)
            dve.tensor_copy(x_f[:, :], x_int[:, :]).then_inc(sem("x_f_ready"), 1)
            dve.wait_ge(sem("wprojT_done"), 1)
            dve.tensor_copy(wprojT[:, :], ps[0:GEO, 6, 0:C]).then_inc(sem("wprojT_ready"), 1)
            dve.wait_ge(sem("idT_done"), 1)
            dve.tensor_scalar(idx[:, :], ps[:, 7, 0:NT], 0.0, float(ITEMS - 1), ALU.max, ALU.min)\
                .then_inc(sem("idx_ready"), 1)
            ch(dve.tensor_scalar(valid[:, :], ps[:, 7, 0:NT], 0.0, None, ALU.not_equal))
            dve.wait_ge(sem("gate_in"), 32)
            for g in range(NT // 4):
                ts = slice(4 * g, 4 * g + 4)
                dve.wait_ge(sem("geo_projected"), g + 1)
                ch(dve.tensor_tensor(gate_in[:, ts, EMB:], ps[:, 2 + g % 2, 0:4 * C].rearrange("p (t c) -> p t c", t=4),
                                     bc(valid[:, ts], C), ALU.mult))
                if g % 2:
                    ts = slice(4 * g - 4, 4 * g + 4)
                    dve.wait_ge(sem(f"gathered{g // 2}"), 16 * 3 * GT)
                    ch(dve.tensor_tensor(prod[:, ts, :], gate_in[:, ts, :], row(gate_w[:, :], GT), ALU.mult))
                    ch(dve.tensor_reduce(glogit[:, ts], prod[:, ts, :], AX.X, ALU.add))
            dve.tensor_scalar(glogit[:, :], glogit[:, :], gate_b[:, :], None, ALU.add).then_inc(sem("glogit_ready"), 1)
            dve.wait_ge(sem("gate_exp"), 1)
            ch(dve.tensor_scalar(gate[:, :], gate[:, :], 1.0, None, ALU.add))
            ch(dve.reciprocal(gate[:, :], gate[:, :]))
            ch(dve.scalar_tensor_tensor(gate[:, :], gate[:, :], MAX_GATE, valid[:, :], ALU.mult, ALU.mult))
            ch(dve.tensor_tensor(xc[:, :, :], gate_in[:, :, EMB:], bc(gate[:, :], C), ALU.mult))
            ch(dve.tensor_tensor(h[:, :, :], xc[:, :, :], gate_in[:, :, 0:EMB], ALU.add))
            if stop_after < 1:
                dve.tensor_copy(xc[:, 0:1, 0:1], h[:, 0:1, 0:1]).then_inc(sem("h_done"), 1)
                dve.wait_ge(sem("h_done"), 1)
                layer_norm_stats(dve, ch, "ln1", h[:, :, :], st[0])
                return
            layer_norm_stats(dve, ch, "ln1", h[:, :, :], st[0])
            attention_dve(dve, ch)
            if stop_after < 2:
                dve.tensor_copy(xc[:, 0:1, 0:1], h[:, 0:1, 0:1]).then_inc(sem("h_done"), 1)
                dve.wait_ge(sem("h_done"), 1)
                return
            heads_dve(dve, ch)
            if stop_after < 3:
                dve.tensor_copy(xc[:, 0:1, 0:1], h[:, 0:1, 0:1]).then_inc(sem("h_done"), 1)
                dve.wait_ge(sem("h_done"), 1)
                return
            recurrent_dve(dve, ch)
            if stop_after < 4:
                dve.tensor_copy(xc[:, 0:1, 0:1], h[:, 0:1, 0:1]).then_inc(sem("h_done"), 1)
                dve.wait_ge(sem("h_done"), 1)
                return
            experts_dve(dve, ch)

        @block.tensor
        def _(pe):
            pe.wait_ge(sem("ident_ready"), 1)
            pe.wait_ge(sem("wproj_in"), 16)
            pe.transpose(ps[0:GEO, 6, 0:C], wproj[:, :], ident[0:C, 0:C]).then_inc(sem("wprojT_done"), 1)
            pe.wait_ge(sem("x_f_ready"), 1)
            pe.transpose(ps[:, 7, 0:NT], x_f[:, :], ident[0:NT, 0:NT]).then_inc(sem("idT_done"), 1)
            pe.wait_ge(sem("wn_in"), 16 * WN_LOADS)

            def turn(bank, col, name, n, off=0):
                w = WCOL[name] + off
                return pe.transpose(ps[:, bank, col:col + n], wn[0:n, w:w + P], ident[0:n, 0:n])

            turn(4, 0, "hl", P)
            for ep in range(2):
                for par in range(2):
                    i = 1 + 2 * ep + par
                    last = turn(4 + i // 4, i % 4 * P, f"wq{ep}", P, C * (1 - par))
                    if i == 3:
                        last.then_inc(sem("wT_done"), 1)
            for par in range(2):
                turn(5, (1 + par) * P, "wk", P, C * (1 - par))
            turn(5, 3 * P, "wv", P).then_inc(sem("wT_done"), 1)
            pe.wait_ge(sem("wprojT_ready"), 1)
            turn(6, P, "fc1", P)
            turn(6, 2 * P, "fc2", P)
            turn(6, 3 * P, "fg", 2 * NH)
            turn(6, 3 * P + 8, "gate0", NH * NE)
            turn(6, 3 * P + 24, "gate1", NH * NE).then_inc(sem("wT_done"), 1)
            pe.wait_ge(sem("wprojT_ready"), 1)
            for g in range(NT // 4):
                pe.wait_ge(sem(f"gathered{g // 2}"), 16 * 3 * GT)
                if g >= 2:
                    pe.wait_ge(sem("geoT_ready"), g - 1)
                for i in range(4):
                    last = pe.transpose(ps[0:GEO, g % 2, i * P:(i + 1) * P], geo_raw[:, 4 * g + i, :], ident[:, :])
                last.then_inc(sem("geo_transposed"), 1)
                pe.wait_ge(sem("geoT_ready"), g + 1)
                if g >= 2:
                    pe.wait_ge(sem("dve_chain"), g - 1 + (g - 2) // 2 * 2 + 1)
                for i in range(4):
                    last = pe.matmul(ps[:, 2 + g % 2, i * C:(i + 1) * C], geoT[:, g % 2, i * P:(i + 1) * P],
                                     wprojT[:, :], start=True, stop=True)
                last.then_inc(sem("geo_projected"), 1)
            if stop_after < 1:
                return
            attention_pe(pe)
            if stop_after < 2:
                return
            heads_pe(pe)
            if stop_after < 3:
                return
            recurrent_pe(pe)
            if stop_after < 4:
                return
            experts_pe(pe)



def kernel(**inputs):
    import numpy as _np
    import concourse.bacc as _bacc
    from concourse import mybir as _mybir
    from concourse.bass_utils import run_bass_kernel_spmd as _run

    nc = _bacc.Bacc("TRN2", target_bir_lowering=False, num_devices=1)
    arrays, args = {}, {}
    for name in inputs:
        v = _np.ascontiguousarray(inputs[name])
        arrays[f"in_{name}_dram"] = v
        args[name] = nc.dram_tensor(f"in_{name}_dram", v.shape, _mybir.dt.from_np(v.dtype), kind="ExternalInput").ap()
    shape = inputs["x"].shape + (inputs["L0_tok_emb_table"].shape[1],)
    out = nc.dram_tensor("out_dram", shape, _mybir.dt.float32, kind="ExternalOutput").ap()
    tower(nc, args, out)
    r = _run(nc, [arrays], core_ids=[0])
    return r.results[0]["out_dram"]
```

```python
from contextlib import ExitStack

import concourse.bass as bass
from concourse import mybir

ALU = mybir.AluOpType
ACT = mybir.ActivationFunctionType
AX = mybir.AxisListType
F32 = mybir.dt.float32
F16 = mybir.dt.float16
F32R = mybir.dt.float32r
BF16 = mybir.dt.bfloat16
I32 = mybir.dt.int32
U32 = mybir.dt.uint32

P = 128
C = 64
NH = 4
NE = 4
D = C // NH
BANK = 512
LN_EPS = 1e-5
FFN_EPS = 1e-8
FSCALE = 64.0
MASKED = -1e30
NEG = -1e38
MAX_GATE = 0.2
BLEND = 0.8


def tower(nc, a, out, stop_after=4):
    B, S = a["x"].shape
    NT = B
    NP = NT // 2
    T = B * S
    TP = T // 2
    NQ = TP // BANK
    assert S == P and NT % 8 == 0
    EMB = a["L0_tok_emb_table"].shape[1]
    FOUR = a["L0_tok_fourier_table"].shape[1]
    VIS = a["L0_tok_visit_table"].shape[1]
    GEO = FOUR + VIS
    ITEMS = a["L0_tok_emb_table"].shape[0]
    HID = a["L1_ffn_W1"].shape[1]
    EX = a["L1_ffn_Wd"].shape[0]
    GT = 8
    NG = NT // GT
    STORES = [(0, NP), (NP, NP + GT), (NP + GT, NT - 2), (NT - 2, NT)]

    ctx = ExitStack()
    with ctx:
        def sb(name, shape, dt=F32):
            return ctx.enter_context(nc.sbuf_tensor(name, shape, dt))

        sems = {}

        def sem(name):
            if name not in sems:
                sems[name] = ctx.enter_context(nc.semaphore(name))
            return sems[name]

        ident = sb("ident", [P, P])
        ident2 = sb("ident2", [P, C])
        ident16 = sb("ident16", [P, P], F16)
        x_int = sb("x_int", [NT, P], I32)
        x_f = sb("x_f", [NT, P])
        idx = sb("idx", [P, NT], U32)
        idf = sb("idf", [P, NT])
        valid = sb("valid", [P, NT])
        gate_w = sb("gate_w", [P, EMB + C])
        gate_b = sb("gate_b", [P, 1])
        wproj = sb("wproj", [C, GEO])
        wprojT = sb("wprojT", [GEO, C])
        R1 = sb("R1", [P, 8192])
        R2 = sb("R2", [P, 8192])
        R3 = sb("R3", [P, 8192])
        gate_in = R1[:, 0:NT * P].rearrange("p (t c) -> p t c", t=NT)
        geo_raw = R2[:, 0:NT * GEO].rearrange("p (t c) -> p t c", t=NT)
        prod = R3[:, 0:NT * P].rearrange("p (t c) -> p t c", t=NT)
        geoT = R3[0:GEO, 6144:7168].rearrange("p (z n) -> p z n", z=2)
        glogit = sb("glogit", [P, NT])
        gate = sb("gate", [P, NT])
        h = sb("h", [P, NT, C])
        xc = sb("xc", [P, NT, C])
        sq = sb("sq", [P, NT, C])
        fn = sb("fn", [P, NT, C])
        st = [sb(f"st{i}", [P, 8, NT]) for i in range(2)]
        stD = sb("stD", [P, 8, NT * NH])
        F4 = sb("F4", [P, NT, 4 * C], F16)
        F_hi = F4[:, :, C:2 * C]
        F_lo = F4[:, :, 2 * C:3 * C]
        ps = ctx.enter_context(nc.psum_tensor("ps", [P, 8, BANK], F32))
        A_hl = R1[:, 0:T // 2].bitcast(F16)
        M_hh = R1[:, T // 2:T].bitcast(F16)
        M_ll = R1[:, T:T + T // 2].bitcast(F16)
        e32 = R2[:, 0:4096].rearrange("p (u n) -> p u n", u=4)
        eh = R2[:, 4096:6144].bitcast(F16).rearrange("p (u n) -> p u n", u=4)
        el = R2[:, 6144:8192].bitcast(F16).rearrange("p (u n) -> p u n", u=4)
        attT = R3[:, 0:T]
        racc = sb("racc", [P, NT, 4])
        zero16 = sb("zero16", [P, P], F16)
        act_warm = sb("act_warm", [P, 2])

        ident_bf = sb("ident_bf", [P, P], BF16)
        masked = sb("masked", [P, NH, P], BF16)
        own_rows = sb("own_rows", [P, 2 * NH])
        own_head = sb("own_head", [P, NH])
        WCOL = {"hl": 0, "wq0": 128, "wq1": 320, "wq2": 512, "wq3": 704, "wk": 896, "wv": 1088, "fc1": 1216,
                "fc2": 1344, "fg": 1472, "gate0": 1600, "gate1": 1728}
        wn = R3[:, 4096:4096 + 1856]
        WT = sb("WT", [P, 14 * P + 40])
        wT_hl = WT[:, 0:P]
        wT_q = [[WT[:, (1 + 2 * e + par) * P:(2 + 2 * e + par) * P] for par in range(2)] for e in range(NE)]
        wT_k = [WT[:, (9 + par) * P:(10 + par) * P] for par in range(2)]
        wT_v = WT[:, 11 * P:12 * P]
        wT_fc1 = WT[:, 12 * P:13 * P]
        wT_fc2 = WT[:, 13 * P:14 * P]
        wT_fg = WT[:, 14 * P:14 * P + 2 * NH]
        wT_gate = [WT[:, 14 * P + 8 + 16 * c:14 * P + 24 + 16 * c] for c in range(2)]
        cols = sb("cols", [P, 16])
        HL_B, FC1_B, G1, B1, G2, B2, DECAY, FIRST, HID_B, W_COL, U_COL = [*range(9), 10, 11]
        rows = sb("rows", [P, 8, C])
        LN_G, LN_B, FN_G, FN_B, FC2_B, GATE_B, EX_B = range(7)
        sx = sb("sx", [P, NT, C])
        kept = sb("kept", [P, NT, C])
        GL = sb("GL", [P, NT, NH * NE])
        xT = R3[:, 0:TP]
        sxT = R1[:, 0:TP]
        Pb = R1[:, 2048:4096].rearrange("p (e n) -> p e n", e=NE)
        PT = R1[:, 4096:8192].rearrange("p (z e n) -> p z e n", z=2, e=NE)
        O_all = R2[:, :].rearrange("p (t n) -> p t n", t=NT)
        KZ = sb("KZ", [P, 2, 2 * BANK], F32R)
        qs = sb("qs", [P, 2, NE * P], F32R)
        qf = R3[C:P, 4096:5120].rearrange("p (z n) -> p z n", z=2)
        kf = R3[:, 5120:5376]
        kh = sb("kh", [P, 2 * P], F32R)
        kl = R3[:, 2048:2304]
        vs = R3[:, 5376:5888].rearrange("p (z a n d) -> p z a n d", z=2, a=2, n=NH)
        ATs = R3[:, 5888:6400]
        Ost = R3[:, 6400:6912].rearrange("p (z n) -> p z n", z=2)
        OTs = R3[:, 6912:7168]
        O1 = R3[:, 7168:7424]
        sxs = R3[:, 7424:7552]
        hxT = R1[:, 0:TP]
        mixp = R1[:, :].rearrange("p (g d) -> p g d", d=D)
        resid = sb("resid", [P, C])
        fg = sb("fg", [P, NT * NH])
        negmax = R3[:, 7552:7568].rearrange("p (e n) -> p e n", e=NE)
        rl = R3[:, 7568:7584].rearrange("p (e n) -> p e n", e=NE)

        wl = F4[:, :, :].rearrange("p t c -> p (t c)").bitcast(F32)
        w_bd = wl[:, 0:5 * P].rearrange("p (i n) -> p i n", i=5)
        WK, WV, WR, WO, WRF = range(5)
        w_kf = wl[:, 640:1152].rearrange("p (a n) -> p a n", a=2)
        w_1 = wl[:, 1152:1664].rearrange("p (a n) -> p a n", a=2)
        w_vf = wl[:, 1664:1792].rearrange("p (k n) -> p k n", k=2)
        w_g = wl[:, 1792:1856].rearrange("p (k n) -> p k n", k=2)
        w_bias = wl[:, 1856:2880]
        w_d = wl[:, 2880:3904].rearrange("p (k n) -> p k n", k=2)
        kT, vT, srT, W_t = (R1[:, i * TP:(i + 1) * TP] for i in range(4))
        O_prev, k_last, A2, E2 = (R2[:, i * TP:(i + 1) * TP] for i in range(4))
        hT, EV, P_prev, Q_prev = (R3[:, i * TP:(i + 1) * TP] for i in range(4))
        hidT = R1[:, :].rearrange("p (i n) -> p i n", i=4)
        srfT, gatedT = R2[:, 0:TP], R2[:, TP:2 * TP]
        scratch = R2[:, 2 * TP:4 * TP].rearrange("p (z n) -> p z n", z=8)
        lgT = R3[0:C, TP:2 * TP]
        coef = sb("coef", [P, NT, EX])
        tmp8 = sb("tmp8", [P, NT, EX])
        rank = sb("rank", [P, EX])
        coefT = sb("coefT", [P, 2 * P])
        xp = R3[:, 2 * TP:3 * TP].rearrange("p (t c) -> p t c", c=C)

        block = ctx.enter_context(nc.Block())

        def bc(ap, n):
            return ap.unsqueeze(2).broadcast_to(tuple(ap.shape) + (n,))

        def row(ap, t):
            return ap.unsqueeze(1).broadcast_to((ap.shape[0], t, ap.shape[1]))

        class Chain:

            def __init__(self, eng, name):
                self.eng, self.sem, self.n = eng, sem(name), 0

            def __call__(self, ins):
                self.n += 1
                ins.then_inc(self.sem, 1)
                self.eng.wait_ge(self.sem, self.n)

        NORMS = ("ln1", "ln2", "mix", "hx", "ln3", "ln5", "ln6")
        TURNS = ("x", "fx", "fo", "x4", "x5", "x6")

        def nth(name):
            return NORMS.index(name) + 1

        def turned(name, q):
            return TURNS.index(name) * NQ + q + 1

        def turned_out(name, q):
            return TURNS.index(name) * (NQ // 2) + q // 2 + 1

        def refined_rstd(dve, ch, s):
            ch(dve.reciprocal(s[:, 2, :], s[:, 5, :]))
            ch(dve.tensor_tensor(s[:, 6, :], s[:, 2, :], s[:, 2, :], ALU.mult))
            ch(dve.tensor_tensor(s[:, 6, :], s[:, 6, :], s[:, 4, :], ALU.mult))
            ch(dve.tensor_scalar(s[:, 6, :], s[:, 6, :], -0.5, 1.5, ALU.mult, ALU.add))
            ch(dve.tensor_tensor(s[:, 2, :], s[:, 2, :], s[:, 6, :], ALU.mult))

        def layer_norm_stats(dve, ch, name, x, s, eps=LN_EPS, w=C):
            xcv = xc[:, :, :].rearrange("p t (n d) -> p (t n) d", d=w)
            sqv = sq[:, :, :].rearrange("p t (n d) -> p (t n) d", d=w)
            ch(dve.tensor_reduce(s[:, 0, :], x, AX.X, ALU.add))
            ch(dve.tensor_scalar(s[:, 1, :], s[:, 0, :], 1.0 / w, None, ALU.mult))
            groups = x.shape[1]
            halves = [slice(0, groups // 2), slice(groups // 2, groups)]
            for half in halves:
                dve.tensor_tensor(xcv[:, half, :], x[:, half, :], bc(s[:, 1, half], w), ALU.subtract)\
                    .then_inc(sem("ln_centred"), 1)
            for i, half in enumerate(halves):
                dve.wait_ge(sem("ln_squared"), 2 * nth(name) + i - 1)
                last = dve.tensor_reduce(s[:, 3, half], sqv[:, half, :], AX.X, ALU.add)
                ch(last)
            dve.tensor_scalar(s[:, 4, :], s[:, 3, :], 1.0 / w, eps, ALU.mult, ALU.add).then_inc(sem("ln_var"), 1)
            dve.wait_ge(sem("ln_root"), nth(name))
            dve.wait_ge(sem("ln_var"), nth(name))
            refined_rstd(dve, ch, s)
            return xcv

        def ln_act(act, name, s):
            act.activation(act_warm[:, 1:2], act_warm[:, 0:1], ACT.Sqrt)
            for i in range(2):
                ts = slice(i * NT // 2, (i + 1) * NT // 2)
                act.wait_ge(sem("ln_centred"), 2 * nth(name) + i - 1)
                act.activation(sq[:, ts, :], xc[:, ts, :], ACT.Square).then_inc(sem("ln_squared"), 1)
            act.wait_ge(sem("ln_var"), nth(name))
            act.activation(s[:, 5, :], s[:, 4, :], ACT.Sqrt).then_inc(sem("ln_root"), 1)

        HALF = T // 2
        SLOT = HALF // 2
        STEPS = 2 * NT
        U = 4
        SPLITS = [(A_hl, C), (M_hh, 0), (M_ll, 2 * C)]
        FG = [(m, q) for q in range(NT // 8) for m in range(3)]

        def fT_out(eng, g):
            m, q = FG[g]
            eng.wait_ge(sem("fT_done"), g + 1)
            dst = SPLITS[m][0][:, q * 1024:(q + 1) * 1024]
            src = ps[:, g % 8, :].bitcast(F16)
            name = f"fT_out{g % 2}"
            if g % 2:
                eng.tensor_copy(dst, src).then_inc(sem(name), 1)
            else:
                eng.activation(dst, src, ACT.Copy).then_inc(sem(name), 1)

        def attention_act(act):
            act.wait_ge(sem("f_ready"), 1)
            act.activation(F4[:, :, 0:C], fn[:, :, :], ACT.Copy, scale=FSCALE).then_inc(sem("f_doubled"), 1)
            act.wait_ge(sem("f_split"), 1)
            act.activation(F4[:, :, 3 * C:], F_lo, ACT.Copy).then_inc(sem("f_doubled"), 1)
            for g in range(0, len(FG), 2):
                fT_out(act, g)
            for half in range(2):
                base = half * STEPS
                with act.Fori(0, STEPS // U) as it:
                    for u in range(U):
                        slot = u % 2
                        s_in = ps[:, 4 + 2 * slot:6 + 2 * slot, :]
                        act.wait_ge(sem("scores_done"), it * U + base + u + 1)
                        if slot == 0:
                            act.activation(eh[:, u, :].rearrange("p (b n) -> p b n", b=2), s_in, ACT.Exp,
                                           scale=1.0 / FSCALE ** 2)
                        act.activation(e32[:, u, :].rearrange("p (b n) -> p b n", b=2), s_in, ACT.Exp,
                                       scale=1.0 / FSCALE ** 2,
                                       accum_out=racc[:, bass.ds(it * (U // 2) + u // 2, 1), 2 * half + slot])\
                            .then_inc(sem("exp_done"), 1)
                act.wait_ge(sem("att_done"), half + 1)
                act.activation(attT[:, half * HALF:half * HALF + SLOT].rearrange("p (b n) -> p b n", b=2),
                               ps[:, 0:2, :], ACT.Copy).then_inc(sem("att_out_act"), 1)
            act.wait_ge(sem("fcm_ready"), 1)
            act.activation(sq[:, :, :], xc[:, :, :], ACT.Square).then_inc(sem("fcm_squared"), 1)
            act.wait_ge(sem("fcm_ss"), 1)
            act.activation(st[1][:, 5, :], st[1][:, 4, :], ACT.Sqrt).then_inc(sem("fcm_root"), 1)

        def attention_dve(dve, ch):
            s = st[0]
            dve.wait_ge(sem("ss_root"), 1)
            ch(dve.tensor_tensor(s[:, 6, :], s[:, 7, :], s[:, 2, :], ALU.mult))
            ch(dve.tensor_scalar(s[:, 6, :], s[:, 6, :], 1e-12, None, ALU.max))
            ch(dve.reciprocal(s[:, 6, :], s[:, 6, :]))
            ch(dve.tensor_tensor(s[:, 6, :], s[:, 6, :], s[:, 2, :], ALU.mult))
            dve.tensor_tensor(fn[:, :, :], xc[:, :, :], bc(s[:, 6, :], C), ALU.mult).then_inc(sem("f_ready"), 1)
            dve.wait_ge(sem("f_ready"), 1)
            ch(dve.tensor_scalar(F_hi, fn[:, :, :], FSCALE, None, ALU.mult))
            dve.scalar_tensor_tensor(F_lo, fn[:, :, :], FSCALE, F_hi, ALU.mult, ALU.subtract).then_inc(sem("f_split"), 1)
            for g in range(1, len(FG), 2):
                fT_out(dve, g)
            for half in range(2):
                base = half * STEPS
                with dve.Fori(0, STEPS // U) as it:
                    for u in range(U):
                        dve.wait_ge(sem("exp_done"), it * U + base + u + 1)
                        if u % 2 == 1:
                            dve.tensor_copy(eh[:, u, :], e32[:, u, :]).then_inc(sem("eh_done"), 1)
                            dve.wait_ge(sem("eh_done"), it * (U // 2) + base // 2 + u // 2 + 1)
                        dve.tensor_tensor(el[:, u, :], e32[:, u, :], eh[:, u, :], ALU.subtract)\
                            .then_inc(sem("e_split"), 1)
                dve.wait_ge(sem("att_done"), half + 1)
                dve.tensor_copy(attT[:, half * HALF + SLOT:(half + 1) * HALF].rearrange("p (b n) -> p b n", b=2),
                                ps[:, 2:4, :]).then_inc(sem("att_out_dve"), 1)
            s = st[1]
            ch(dve.tensor_reduce(s[:, 0, :], racc[:, :, :], AX.X, ALU.add))
            ch(dve.reciprocal(s[:, 1, :], s[:, 0, :]))
            ch(dve.tensor_scalar(s[:, 1, :], s[:, 1, :], (1.0 - BLEND) / FSCALE, None, ALU.mult))
            dve.wait_ge(sem("att_token"), 1)
            ch(dve.tensor_tensor(xc[:, :, :], ps[:, 0:4, :].rearrange("p k (t c) -> p (k t) c", c=C),
                                 bc(s[:, 1, :], C), ALU.mult))
            dve.scalar_tensor_tensor(xc[:, :, :], fn[:, :, :], BLEND, xc[:, :, :], ALU.mult, ALU.add)\
                .then_inc(sem("fcm_ready"), 1)
            dve.wait_ge(sem("fcm_squared"), 1)
            dve.tensor_reduce(s[:, 4, :], sq[:, :, :], AX.X, ALU.add).then_inc(sem("fcm_ss"), 1)
            dve.wait_ge(sem("fcm_root"), 1)
            ch(dve.tensor_scalar(s[:, 6, :], s[:, 5, :], 1e-12, None, ALU.max))
            ch(dve.reciprocal(s[:, 6, :], s[:, 6, :]))
            ch(dve.tensor_tensor(xc[:, :, :], xc[:, :, :], bc(s[:, 6, :], C), ALU.mult))
            ch(dve.tensor_tensor(h[:, :, :], h[:, :, :], xc[:, :, :], ALU.add))

        def attention_pe(pe):
            pe.wait_ge(sem("f_split"), 1)
            pe.wait_ge(sem("f_doubled"), 2)
            pe.wait_ge(sem("ident_ready"), 2)
            for g, (m, q) in enumerate(FG):
                if g >= 8:
                    pe.wait_ge(sem(f"fT_out{g % 2}"), (g - 8) // 2 + 1)
                bank = ps[:, g % 8, :].bitcast(F16)
                for i in range(8):
                    last = pe.transpose(bank[:, i * P:(i + 1) * P], F4[:, 8 * q + i, SPLITS[m][1]:SPLITS[m][1] + P], ident16[:, :])
                last.then_inc(sem("fT_done"), 1)

            def scores(half, slot, j):
                for c in range(2):
                    col = half * HALF + slot * SLOT + c * BANK
                    lhs = A_hl[:, bass.ds(j * P, P)]
                    pe.matmul(ps[:, 4 + 2 * slot + c, :], lhs, M_hh[:, col:col + BANK], start=True, stop=False)
                    last = pe.matmul(ps[:, 4 + 2 * slot + c, :], lhs, M_ll[:, col:col + BANK], start=False, stop=True)
                last.then_inc(sem("scores_done"), 1)

            def weigh(slot, u, j):
                for part in (eh, el):
                    for c in range(2):
                        pe.matmul(ps[:, 2 * slot + c, :], F4[:, bass.ds(j, 1), C:3 * C].rearrange("p t c -> p (t c)"),
                                  part[:, u, c * BANK:(c + 1) * BANK], start=False, stop=False, skip_group_check=True)

            for half in range(2):
                base = half * STEPS
                if half == 0:
                    pe.wait_ge(sem("fT_out0"), len(FG) // 2)
                    pe.wait_ge(sem("fT_out1"), len(FG) // 2)
                else:
                    pe.wait_ge(sem("att_out_act"), half)
                    pe.wait_ge(sem("att_out_dve"), half)
                for c in range(4):
                    pe.matmul(ps[:, c, :], zero16[:, :], M_hh[:, c * BANK:(c + 1) * BANK], start=True, stop=False,
                              skip_group_check=True)
                scores(half, 0, 0)
                scores(half, 1, 0)
                with pe.Fori(0, STEPS // U - 1) as it:
                    for u in range(U):
                        pe.wait_ge(sem("exp_done"), it * U + base + u + 1)
                        scores(half, u % 2, it * (U // 2) + u // 2 + 1)
                        pe.wait_ge(sem("e_split"), it * U + base + u + 1)
                        weigh(u % 2, u, it * (U // 2) + u // 2)
                for u in range(U):
                    k = STEPS - U + u
                    if u < 2:
                        pe.wait_ge(sem("exp_done"), base + k + 1)
                        scores(half, u % 2, k // 2 + 1)
                    pe.wait_ge(sem("e_split"), base + k + 1)
                    weigh(u % 2, u, k // 2)
                for c in range(4):
                    last = pe.matmul(ps[:, c, :], zero16[:, :], M_hh[:, c * BANK:(c + 1) * BANK], start=False,
                                     stop=True, skip_group_check=True)
                last.then_inc(sem("att_done"), 1)
            pe.wait_ge(sem("att_out_act"), 2)
            pe.wait_ge(sem("att_out_dve"), 2)
            for t in range(NT):
                last = pe.matmul(ps[:, t // 8, t % 8 * C:(t % 8 + 1) * C], attT[:, t * P:(t + 1) * P], ident2[:, :],
                                 start=True, stop=True)
            last.then_inc(sem("att_token"), 1)

        WN_LOADS, COL_LOADS, ROW_LOADS, WL_LOADS = 2 * (1 + NH * (NE + 4) + 1) + NH, 2 + 8 + 12 + 2, 5 * NH + 2, 10 + 4 + 4 + P // EX
        wn_loads, col_loads, row_loads = [], [], []

        def transpose_pairs(pe, src, first_bank=0):
            for p in range(NP):
                last = pe.transpose(ps[:, first_bank + p // 4, p % 4 * P:(p % 4 + 1) * P],
                                    src[:, 2 * p:2 * p + 2, :].rearrange("p t c -> p (t c)"), ident[:, :])
                if p % 4 == 3:
                    last.then_inc(sem("pairs_turned"), 1)

        def project(pe, w, src, name, first_bank):
            for q in range(NQ):
                pe.matmul(ps[:, first_bank + q, :], w, src[:, q * BANK:(q + 1) * BANK], start=True, stop=True)\
                    .then_inc(sem(name), 1)

        def batches(eng, one):
            for b in range(4):
                one(b, b // 2, b, b)
            with eng.Fori(1, NT // 4 - 1) as it:
                for m in range(4):
                    one(it * 4 + m, it * 2 + m // 2, m, None)
            for b in range(NT - 4, NT + 3):
                one(b, b // 2, b % 4, b)

        def has(n, lo, hi=NT):
            return n is None or lo <= n < hi

        def heads_pool(pool):
            pool.wait_ge(sem("att_out_act"), 2)
            pool.wait_ge(sem("att_token"), 1)
            pool.memset(R3[:, 5376:5888], 0.0).then_inc(sem("vs_zeroed"), 1)
            pool.wait_ge(sem("vs_zeroed"), 1)
            pool.memset(vs[:, :, :, :, D:D + 1].rearrange("p z a n d -> p (z a n) d"), 1.0).then_inc(sem("vs_ones"), 1)

            pool.memset(wl[:, 0:3904], 0.0).then_inc(sem("wl_zeroed"), 1)
            for e in range(EX):
                last = pool.memset(rank[:, e:e + 1], float(EX - e))
            last.then_inc(sem("rank_ready"), 1)

            def stage_sxT(p, first=False):
                if not first:
                    pool.wait_ge(sem("q_done"), p * 2)
                pool.tensor_copy(sxs[:, :], sxT[:, bass.ds(p * P, P)]).then_inc(sem("sxs_ready"), 1)

            def spread_keys(b, par, n):
                if n is None or n >= 2:
                    pool.wait_ge(sem("S_done"), (b - 1) * 4)
                for i, part in enumerate((kh, kl)):
                    last = pool.tensor_tensor(KZ[:, par, i * BANK:(i + 1) * BANK].rearrange("p (n t) -> p n t", t=P),
                                              row(part[:, par * P:(par + 1) * P], NH), bc(own_head[:, :], P), ALU.mult)
                last.then_inc(sem("kz_ready"), 1)

            pool.wait_ge(sem("sxT_ready"), 2)
            stage_sxT(0, True)
            pool.wait_ge(sem("masks_ready"), 2)
            pool.wait_ge(sem("kl_ready"), 1)
            spread_keys(0, 0, 0)

            def one(b, p, m, n):
                par = m % 2
                if par == 0:
                    if has(n, 0, NT - 2):
                        stage_sxT(p + 1)
                    if has(n, 0):
                        spread_keys(b + 1, 1, n + 1 if n is not None else None)
                else:
                    if has(n, 0, NT - 2):
                        pool.wait_ge(sem("kl_ready"), p + 2)
                        spread_keys(b + 1, 0, n + 1 if n is not None else None)
                if has(n, 3, NT + 3):
                    pool.wait_ge(sem("O_done"), b - 2)
                    pool.tensor_copy(O_all[:, bass.ds(b - 3, 1), :].rearrange("p t n -> p (t n)"), Ost[:, (m + 1) % 2, :])\
                        .then_inc(sem("O_copied"), 1)
            batches(pool, one)

        def heads_pe(pe):
            pe.wait_ge(sem("ln2_done"), 1)
            transpose_pairs(pe, fn)
            pe.wait_ge(sem("WT_ready"), 4)
            for q in range(NQ):
                pe.wait_ge(sem(f"pairs_out{q % 2}"), turned_out("x", q))
                pe.matmul(ps[:, 4 + q, :], wT_hl, xT[:, q * BANK:(q + 1) * BANK], start=True, stop=True)\
                    .then_inc(sem("sxT_done"), 1)
            pe.wait_ge(sem("sxT_ready"), 2)
            pe.wait_ge(sem("masks_ready"), 1)

            def project_k(p):
                pe.wait_ge(sem("sxs_ready"), p + 1)
                for par in range(2):
                    pe.matmul(ps[:, 7, par * P:(par + 1) * P], wT_k[par], sxs[:, :], start=True, stop=True)
                pe.transpose(ps[:, 7, 3 * P:4 * P], sxs[:, :], ident[:, :]).then_inc(sem("k_done"), 1)

            def project_v(p):
                pe.matmul(ps[:, 7, 3 * P:4 * P], sxs[:, :], wT_v, start=True, stop=True).then_inc(sem("v_done"), 1)

            def project_q(b, par):
                for e in range(NE):
                    last = pe.matmul(ps[:, 7, e * P:(e + 1) * P], wT_q[e][par], sxs[:, :], start=True, stop=True)
                last.then_inc(sem("q_done"), 1)

            project_k(0)
            pe.wait_ge(sem("k_out"), 1)
            pe.wait_ge(sem("sx_out"), 1)
            project_q(0, 0)
            pe.wait_ge(sem("q_out"), 1)
            project_v(0)

            def one(b, p, m, n):
                par, z = m % 2, m // 2
                for e in range(NE):
                    if n is None or n >= 1:
                        if has(n, 1, NT + 1):
                            pe.wait_ge(sem("exp2_done"), b * 4 + e - 3)
                    if has(n, 0):
                        if e == 0:
                            pe.wait_ge(sem("q_split"), b + 1)
                            pe.wait_ge(sem("kz_ready"), b + 1)
                        for i in range(2):
                            pe.matmul(ps[:, e, :], qs[:, par, e * P:(e + 1) * P],
                                      KZ[:, par, i * BANK:(i + 1) * BANK], start=i == 0, stop=False)
                        pe.matmul(ps[:, e, :], ident_bf[:, :], masked[:, :, :].rearrange("p n t -> p (n t)"),
                                  start=False, stop=True).then_inc(sem("S_done"), 1)
                    if has(n, 1, NT + 1):
                        if n is None or 4 * n + e - 5 > 0:
                            pe.wait_ge(sem("PT_out"), b * 4 + e - 5)
                        for g in range(NH):
                            last = pe.transpose(ps[:, 4 + e % 2, g * P:(g + 1) * P], Pb[:, e, g * P:(g + 1) * P],
                                                ident[:, :])
                        last.then_inc(sem("T_done"), 1)
                    if e == 0:
                        if has(n, 0, NT - 1):
                            if par == 0:
                                pe.wait_ge(sem("v_out"), p + 1)
                            else:
                                pe.wait_ge(sem("k_out"), p + 2)
                                pe.wait_ge(sem("sx_out"), p + 2)
                            project_q(b + 1, 1 - par)
                    if e == 1 and has(n, 3, NT + 3):
                        pe.wait_ge(sem("O_done"), b - 2)
                        if has(n, 0, NT - 1):
                            pe.wait_ge(sem("q_out"), b + 2)
                        else:
                            pe.wait_ge(sem("gl_out"), b - 3)
                        for c in range(2):
                            last = pe.transpose(ps[:, 7, c * P:(c + 1) * P], Ost[:, (m + 1) % 2, c * P:(c + 1) * P],
                                                ident[:, :])
                        last.then_inc(sem("OT_done"), 1)
                    if e == 1:
                        if has(n, 2, NT + 2):
                            pe.wait_ge(sem("PT_out"), b * 4 - 4)
                            pe.wait_ge(sem("v_out"), p)
                            if n is None or n >= 3:
                                pe.wait_ge(sem("O_done"), b - 2)
                            for g in range(NH):
                                last = pe.matmul(ps[32 * g:32 * g + 32, 6, :], vs[:, (m // 2 + 1) % 2, par, g, :],
                                                 PT[:, par, :, g * P:(g + 1) * P], start=True, stop=True)
                            last.then_inc(sem("AV_done"), 1)
                    if e == 2:
                        if has(n, 2, NT + 2):
                            pe.wait_ge(sem("AT_out"), b - 1)
                            for g in range(NE):
                                last = pe.transpose(ps[:, 6, g * P:(g + 1) * P], ATs[:, g * P:(g + 1) * P], ident[:, :])
                            last.then_inc(sem("ATt_done"), 1)
                        if has(n, 3, NT + 3):
                            pe.wait_ge(sem("OT_out"), b - 2)
                            for c in range(2):
                                last = pe.matmul(ps[:, 7, 256:256 + NH * NE], OTs[:, c * P:(c + 1) * P], wT_gate[c],
                                                 start=c == 0, stop=c == 1)
                            last.then_inc(sem("gl_done"), 1)
                    if e == 3 and par == 1 and has(n, 0, NT - 2):
                        if n is not None and n < 3:
                            pe.wait_ge(sem("q_out"), b + 2)
                        else:
                            pe.wait_ge(sem("gl_out"), b - 2)
                        project_v(p + 1)
                    if e == 3 and par == 0 and has(n, 0, NT - 2):
                        if n is None or n >= 3:
                            pe.wait_ge(sem("gl_out"), b - 2)
                        else:
                            pe.wait_ge(sem("q_out"), b + 2)
                        project_k(p + 1)
            batches(pe, one)
            tail_pe(pe)

        def heads_act(act):
            ln_act(act, "ln2", st[0])
            for q in range(0, NQ, 2):
                act.wait_ge(sem("pairs_turned"), turned("x", q))
                act.activation(xT[:, q * BANK:(q + 1) * BANK], ps[:, q, :], ACT.Copy).then_inc(sem("pairs_out0"), 1)
            act.wait_ge(sem("cols_in"), 16 * COL_LOADS)
            act.wait_ge(sem("sxT_done"), 2)
            act.activation(sxT[:, 0:2 * BANK].rearrange("p (b n) -> p b n", b=2), ps[:, 4:6, :], ACT.Identity,
                           bias=cols[:, HL_B:HL_B + 1]).then_inc(sem("sxT_ready"), 1)
            act.wait_ge(sem("vs_ones"), 1)

            def k_out(p, z, b=None, n=0):
                act.wait_ge(sem("k_done"), p + 1)
                if b is not None:
                    act.wait_ge(sem("kz_ready"), b + 2)
                act.activation(kf, ps[:, 7, 0:2 * P], ACT.Copy)
                act.activation(kh[:, :], ps[:, 7, 0:2 * P], ACT.Copy).then_inc(sem("k_out"), 1)

            def v_out(p, z):
                act.wait_ge(sem("v_done"), p + 1)
                act.activation(vs[:, z, :, :, 0:D].rearrange("p a n d -> p (a n) d"),
                               ps[:, 7, 3 * P:4 * P].rearrange("p (g d) -> p g d", d=D), ACT.Copy)\
                    .then_inc(sem("v_out"), 1)

            def q_out(b, par):
                act.wait_ge(sem("q_done"), b + 1)
                act.activation(qs[:, par, :], ps[:, 7, :], ACT.Copy, scale=float(D) ** 0.5)
                act.activation(qf[:, par, :], ps[C:P, 7, :], ACT.Copy, scale=float(D) ** 0.5).then_inc(sem("q_out"), 1)

            k_out(0, 0)
            q_out(0, 0)
            v_out(0, 0)

            def one(b, p, m, n):
                par, z = m % 2, m // 2
                for e in range(NE):
                    if e == 0:
                        if has(n, 0, NT - 1):
                            q_out(b + 1, 1 - par)
                    if e == 1 and has(n, 3, NT + 3):
                        act.wait_ge(sem("OT_done"), b - 2)
                        act.activation(OTs[:, :], ps[:, 7, 0:2 * P], ACT.Copy).then_inc(sem("OT_out"), 1)
                    if e == 1:
                        if has(n, 2, NT + 2):
                            act.wait_ge(sem("AV_done"), b - 1)
                            act.activation(ATs[:, :], ps[:, 6, :], ACT.Copy).then_inc(sem("AT_out"), 1)
                    if e == 2 and has(n, 3, NT + 3):
                        act.wait_ge(sem("gl_done"), b - 2)
                        act.activation(GL[:, bass.ds(b - 3, 1), :].rearrange("p t n -> p (t n)"),
                                       ps[:, 7, 256:256 + NH * NE], ACT.Copy).then_inc(sem("gl_out"), 1)
                    if e == 3 and par == 1 and has(n, 0, NT - 2):
                        v_out(p + 1, (z + 1) % 2)
                    if e == 3 and par == 0 and has(n, 0, NT - 2):
                        k_out(p + 1, (z + 1) % 2, b)
                    if has(n, 0):
                        act.wait_ge(sem("max_done"), b * 4 + e + 1)
                        if n is None or n >= 1:
                            act.wait_ge(sem("T_done"), b * 4 + e - 3)
                        for g in range(NH):
                            last = act.activation(Pb[:, e, g * P:(g + 1) * P], ps[:, e, g * P:(g + 1) * P], ACT.Exp,
                                                  bias=negmax[:, e, g:g + 1])
                        last.then_inc(sem("exp2_done"), 1)
            batches(act, one)
            tail_act(act)

        def heads_dve(dve, ch):
            s = st[0]
            layer_norm_stats(dve, ch, "ln2", h[:, :, :], s)
            dve.tensor_tensor(fn[:, :, :], xc[:, :, :], bc(s[:, 2, :], C), ALU.mult).then_inc(sem("ln2_done"), 1)
            for q in range(1, NQ, 2):
                dve.wait_ge(sem("pairs_turned"), turned("x", q))
                dve.tensor_copy(xT[:, q * BANK:(q + 1) * BANK], ps[:, q, :]).then_inc(sem("pairs_out1"), 1)
            dve.wait_ge(sem("cols_in"), 16 * COL_LOADS)
            dve.wait_ge(sem("sxT_done"), 4)
            dve.tensor_scalar(sxT[:, 2 * BANK:].rearrange("p (b n) -> p b n", b=2), ps[:, 6:8, :],
                              cols[:, HL_B:HL_B + 1], None, ALU.add).then_inc(sem("sxT_ready"), 1)

            def sx_out(p):
                dve.wait_ge(sem("k_done"), p + 1)
                dve.wait_ge(sem("k_out"), p + 1)
                dve.tensor_scalar(kept[:, bass.ds(p * 2, 2), :].rearrange("p t c -> p (t c)"), ps[:, 7, 3 * P:4 * P],
                                  0.0, None, ALU.not_equal)
                dve.tensor_copy(sx[:, bass.ds(p * 2, 2), :].rearrange("p t c -> p (t c)"), ps[:, 7, 3 * P:4 * P])\
                    .then_inc(sem("sx_out"), 1)

            def k_split(p):
                dve.tensor_tensor(kl, kf, kh[:, :], ALU.subtract).then_inc(sem("kl_ready"), 1)

            def q_split(b, par):
                dve.wait_ge(sem("q_out"), b + 1)
                dve.tensor_tensor(qs[C:P, par, :], qf[:, par, :], qs[C:P, par, :], ALU.subtract)\
                    .then_inc(sem("q_split"), 1)

            sx_out(0)
            k_split(0)
            q_split(0, 0)

            def one(b, p, m, n):
                par, z = m % 2, m // 2
                for e in range(NE):
                    if has(n, 0):
                        dve.wait_ge(sem("S_done"), b * 4 + e + 1)
                        dve.tensor_reduce(negmax[:, e, :], ps[:, e, :].rearrange("p (n t) -> p n t", t=P), AX.X,
                                          ALU.max, negate=True).then_inc(sem("max_done"), 1)
                    if e == 1 and has(n, 0, NT - 1):
                        q_split(b + 1, 1 - par)
                    if has(n, 1, NT + 1):
                        dve.wait_ge(sem("T_done"), b * 4 + e - 3)
                        if n is None or n >= 3:
                            dve.wait_ge(sem("AV_done"), b - 2)
                        dve.tensor_copy(PT[:, (m + 1) % 2, e, :], ps[:, 4 + e % 2, :]).then_inc(sem("PT_out"), 1)
                if par == 0 and has(n, 0, NT - 2):
                    sx_out(p + 1)
                    k_split(p + 1)
                if has(n, 2, NT + 2):
                    dve.wait_ge(sem("ATt_done"), b - 1)
                    at = ps[:, 6, :].rearrange("p (e n d) -> p e n d", e=NE, n=NH)
                    dve.reciprocal(rl[:, :, :], at[:, :, :, D:D + 1].rearrange("p e n d -> p e (n d)"))\
                        .then_inc(sem("rl_done"), 1)
                    dve.wait_ge(sem("rl_done"), b - 1)
                    dve.tensor_tensor(O1[:, :].rearrange("p (n e d) -> p e n d", n=NH, e=NE), at[:, :, :, 0:D],
                                      rl[:, :, :].unsqueeze(3).broadcast_to((P, NE, NH, D)), ALU.mult)\
                        .then_inc(sem("O1_done"), 1)
                    dve.wait_ge(sem("O1_done"), b - 1)
                    if n is None or n >= 4:
                        dve.wait_ge(sem("O_copied"), b - 3)
                        dve.wait_ge(sem("OT_done"), b - 3)
                    keep = kept[:, bass.ds(b - 2, 1), :].rearrange("p t (n d) -> p (t n) d", d=D).unsqueeze(2)\
                        .broadcast_to((P, NH, NE, D))
                    dve.tensor_tensor(Ost[:, par, :].rearrange("p (n e d) -> p n e d", n=NH, e=NE), keep,
                                      O1[:, :].rearrange("p (n e d) -> p n e d", n=NH, e=NE), ALU.mult)\
                        .then_inc(sem("O_done"), 1)
            batches(dve, one)
            tail_dve(dve, ch)

        def tail_act(act):
            act.wait_ge(sem("gs_shifted"), 1)
            act.activation(GL[:, :, :], GL[:, :, :], ACT.Exp).then_inc(sem("gs_exp"), 1)
            ln_act(act, "mix", stD)
            for q in range(0, NQ, 2):
                act.wait_ge(sem("pairs_turned"), turned("fx", q))
                act.activation(xT[:, q * BANK:(q + 1) * BANK], ps[:, q, :], ACT.Copy).then_inc(sem("pairs_out0"), 1)
            for q in range(NQ):
                act.wait_ge(sem("fc1_done"), q + 1)
                act.activation(hxT[:, q * BANK:(q + 1) * BANK], ps[:, 4 + q, :], ACT.Relu,
                               bias=cols[:, FC1_B:FC1_B + 1]).then_inc(sem("hxT_relu"), 1)
            ln_act(act, "hx", stD)
            for q in range(0, NQ, 2):
                act.wait_ge(sem("pairs_turned"), turned("fo", q))
                act.activation(xT[:, q * BANK:(q + 1) * BANK], ps[:, 4 + q, :], ACT.Copy).then_inc(sem("pairs_out0"), 1)
            act.wait_ge(sem("fg_shifted"), 1)
            act.activation(fg[:, :], fg[:, :], ACT.Exp).then_inc(sem("fg_exp"), 1)

        def tail_dve(dve, ch):
            glv = GL[:, :, :].rearrange("p t (n e) -> p (t n) e", e=NE)
            m, r = stD[:, 0, :], stD[:, 1, :]
            dve.wait_ge(sem("rows_in"), 16 * ROW_LOADS)
            dve.wait_ge(sem("gl_out"), NT)
            ch(dve.tensor_tensor(GL[:, :, :], GL[:, :, :], row(rows[:, GATE_B, 0:NH * NE], NT), ALU.add))
            ch(dve.tensor_reduce(m, glv, AX.X, ALU.max))
            dve.tensor_tensor(glv, glv, bc(m, NE), ALU.subtract).then_inc(sem("gs_shifted"), 1)
            for n in range(NH):
                last = dve.tensor_copy(resid[:, n * D:(n + 1) * D], sx[:, n, n * D:(n + 1) * D])
            ch(last)
            dve.wait_ge(sem("gs_exp"), 1)
            ch(dve.tensor_reduce(r, glv, AX.X, ALU.add))
            ch(dve.reciprocal(r, r))
            ch(dve.tensor_tensor(glv, glv, bc(r, NE), ALU.mult))
            dve.wait_ge(sem("O_copied"), NT)
            ch(dve.tensor_tensor(mixp, O_all.rearrange("p t (g d) -> p (t g) d", d=D),
                                 bc(GL[:, :, :].rearrange("p t g -> p (t g)"), D), ALU.mult))
            ch(dve.tensor_reduce(fn[:, :, :].rearrange("p t (n d) -> p (t n) d", d=D),
                                 mixp.rearrange("p (g e) d -> p g d e", e=NE), AX.X, ALU.add))
            ch(dve.tensor_tensor(fn[:, :, :], fn[:, :, :], row(resid[:, :], NT), ALU.add))

            def norm_affine(name, g, b, done):
                x = layer_norm_stats(dve, ch, name, fn[:, :, :].rearrange("p t (n d) -> p (t n) d", d=D), stD,
                                     FFN_EPS, D)
                ch(dve.tensor_tensor(x, x, bc(stD[:, 2, :], D), ALU.mult))
                ch(dve.tensor_tensor(xc[:, :, :], xc[:, :, :], row(rows[:, g, :], NT), ALU.mult))
                dve.tensor_tensor(fn[:, :, :], xc[:, :, :], row(rows[:, b, :], NT), ALU.add).then_inc(sem(done), 1)

            norm_affine("mix", LN_G, LN_B, "fx_ready")
            for q in range(1, NQ, 2):
                dve.wait_ge(sem("pairs_turned"), turned("fx", q))
                dve.tensor_copy(xT[:, q * BANK:(q + 1) * BANK], ps[:, q, :]).then_inc(sem("pairs_out1"), 1)
            dve.wait_ge(sem("pairs_out1"), turned_out("fx", NQ - 1))
            dve.wait_ge(sem("pairs_out0"), turned_out("fx", NQ - 1))
            for q in range(NQ):
                c = slice(q * BANK, (q + 1) * BANK)
                dve.wait_ge(sem("hxT_relu"), q + 1)
                dve.scalar_tensor_tensor(hxT[:, c], xT[:, c], 0.0, hxT[:, c], ALU.not_equal, ALU.mult)\
                    .then_inc(sem("hxT_ready"), 1)
            dve.wait_ge(sem("fx_ready"), 1)
            dve.wait_ge(sem("fc2_done"), 1)
            ch(dve.tensor_tensor(xc[:, :, :], ps[:, 0:4, :].rearrange("p k (t c) -> p (k t) c", c=C),
                                 row(rows[:, FC2_B, :], NT), ALU.add))
            ch(dve.scalar_tensor_tensor(xc[:, :, :], fn[:, :, :], 0.0, xc[:, :, :], ALU.not_equal, ALU.mult))
            ch(dve.tensor_tensor(fn[:, :, :], fn[:, :, :], xc[:, :, :], ALU.add))
            norm_affine("hx", FN_G, FN_B, "fo_ready")
            for q in range(1, NQ, 2):
                dve.wait_ge(sem("pairs_turned"), turned("fo", q))
                dve.tensor_copy(xT[:, q * BANK:(q + 1) * BANK], ps[:, 4 + q, :]).then_inc(sem("pairs_out1"), 1)
            fgv = fg[:, :].rearrange("p (t n) -> p t n", n=NH)
            m, r = st[0][:, 0, :], st[0][:, 1, :]
            dve.wait_ge(sem("fg_done"), 1)
            ch(dve.tensor_reduce(m, ps[:, 0, 0:NT * NH].rearrange("p (t n) -> p t n", n=NH), AX.X, ALU.max))
            dve.tensor_tensor(fgv, ps[:, 0, 0:NT * NH].rearrange("p (t n) -> p t n", n=NH), bc(m, NH), ALU.subtract)\
                .then_inc(sem("fg_shifted"), 1)
            dve.wait_ge(sem("fg_exp"), 1)
            ch(dve.tensor_reduce(r, fgv, AX.X, ALU.add))
            ch(dve.reciprocal(r, r))
            ch(dve.tensor_tensor(fgv, fgv, bc(r, NH), ALU.mult))
            ch(dve.tensor_tensor(xc[:, :, :].rearrange("p t (n d) -> p (t n) d", d=D),
                                 fn[:, :, :].rearrange("p t (n d) -> p (t n) d", d=D), bc(fg[:, :], D), ALU.mult))
            ch(dve.tensor_tensor(h[:, :, :], h[:, :, :], xc[:, :, :], ALU.add))

        def tail_pe(pe):
            pe.wait_ge(sem("fx_ready"), 1)
            transpose_pairs(pe, fn)
            for q in range(NQ):
                pe.wait_ge(sem(f"pairs_out{q % 2}"), turned_out("fx", q))
                pe.matmul(ps[:, 4 + q, :], wT_fc1, xT[:, q * BANK:(q + 1) * BANK], start=True, stop=True)\
                    .then_inc(sem("fc1_done"), 1)
            for p in range(NP):
                if p % 4 == 0:
                    pe.wait_ge(sem("hxT_ready"), p // 4 + 1)
                last = pe.matmul(ps[:, p // 4, p % 4 * P:(p % 4 + 1) * P], hxT[:, p * P:(p + 1) * P], wT_fc2,
                                 start=True, stop=True)
            last.then_inc(sem("fc2_done"), 1)
            pe.wait_ge(sem("fo_ready"), 1)
            transpose_pairs(pe, fn, 4)
            for p in range(NP):
                if p % 4 == 0:
                    pe.wait_ge(sem(f"pairs_out{p // 4 % 2}"), turned_out("fo", p // 4))
                last = pe.matmul(ps[:, 0, p * 2 * NH:(p + 1) * 2 * NH], xT[:, p * P:(p + 1) * P], wT_fg,
                                 start=True, stop=True)
            last.then_inc(sem("fg_done"), 1)

        def seq(x):
            return x.rearrange("p (b t) -> p b t", t=P)

        def pairs_out(eng, name, first_bank, q, dst, scale=None, bias=None):
            eng.wait_ge(sem("pairs_turned"), turned(name, q))
            src, dst = ps[:, first_bank + q, :], dst[:, q * BANK:(q + 1) * BANK]
            if q % 2:
                if scale is None:
                    ins = eng.tensor_copy(dst, src)
                else:
                    ins = eng.tensor_scalar(dst, src, scale, bias, ALU.mult, ALU.add)
            elif scale is None:
                ins = eng.activation(dst, src, ACT.Copy)
            else:
                ins = eng.activation(dst, src, ACT.Identity, scale=scale, bias=bias)
            ins.then_inc(sem(f"pairs_out{q % 2}"), 1)

        def col(i):
            return cols[:, i:i + 1]

        def banks(first):
            return ps[:, first:first + NQ, :].rearrange("p k n -> p (k n)")

        def recurrent_pool(pool):
            pool.wait_ge(sem("fg_done"), 1)
            pool.memset(seq(k_last)[:, :, 0:1], NEG).then_inc(sem("starts_ready"), 1)
            pool.memset(seq(A2)[:, :, 0:1], 0.0).then_inc(sem("starts_ready"), 1)
            pool.memset(seq(E2)[:, :, 0:1], 0.0).then_inc(sem("starts_ready"), 1)
            pool.memset(seq(EV)[:, :, 0:1], 0.0).then_inc(sem("starts_ready"), 1)

        def recurrent_act(act):
            ln_act(act, "ln3", st[0])
            act.wait_ge(sem("ln4_var"), 1)
            act.activation(st[1][:, 5, :], st[1][:, 4, :], ACT.Sqrt).then_inc(sem("ln4_root"), 1)
            for q in range(0, NQ, 2):
                pairs_out(act, "x4", 0, q, hT, col(G1), col(B1))
            act.wait_ge(sem("starts_ready"), 4)
            act.wait_ge(sem("k_proj"), NQ)
            act.activation(seq(k_last)[:, :, 1:], seq(banks(4))[:, :, 0:P - 1], ACT.Copy).then_inc(sem("k_shifted"), 1)
            act.wait_ge(sem("v_proj"), NQ)
            act.activation(vT, banks(0), ACT.Copy).then_inc(sem("vT_ready"), 1)
            act.wait_ge(sem("r_proj"), NQ)
            act.activation(srT, banks(4), ACT.Sigmoid).then_inc(sem("srT_ready"), 1)
            act.wait_ge(sem("A2_log"), 1)
            act.activation(seq(A2)[:, :, 1:], seq(A2)[:, :, 1:], ACT.Exp, bias=col(W_COL)).then_inc(sem("A2_ready"), 1)
            act.wait_ge(sem("E2_log"), 1)
            act.activation(seq(E2)[:, :, 1:], seq(E2)[:, :, 1:], ACT.Exp).then_inc(sem("E2_ready"), 1)
            act.wait_ge(sem("A_log"), 1)
            act.activation(O_prev, O_prev, ACT.Exp).then_inc(sem("A_ready"), 1)
            act.wait_ge(sem("E_log"), 1)
            act.activation(kT, kT, ACT.Exp).then_inc(sem("E_ready"), 1)
            act.wait_ge(sem("den_ready"), 1)
            act.activation(W_t, Q_prev, ACT.Ln).then_inc(sem("den_log"), 1)
            act.wait_ge(sem("den_log"), 1)
            act.activation(W_t, W_t, ACT.Exp, scale=-1.0).then_inc(sem("den_inverse"), 1)
            ln_act(act, "ln5", st[0])
            for q in range(0, NQ, 2):
                pairs_out(act, "x5", 4, q, hT, col(G2), col(B2))
            for q in range(NQ):
                for i in range(0, 4, 2):
                    act.wait_ge(sem("kk_proj"), 4 * q + i + 1)
                    dst = hidT[:, i, q * BANK:(q + 1) * BANK]
                    act.activation(dst, ps[:, (4 * q + i) % 8, :], ACT.Relu).then_inc(sem("kk_relu"), 1)
                    act.wait_ge(sem("kk_relu"), 2 * q + i // 2 + 1)
                    act.activation(dst, dst, ACT.Square).then_inc(sem("kk_act"), 1)
            act.wait_ge(sem("rf_proj"), NQ)
            act.activation(srfT, banks(4), ACT.Sigmoid).then_inc(sem("srfT_ready"), 1)

        def recurrent_dve(dve, ch):
            ch(dve.tensor_scalar(col(W_COL), col(DECAY), 1.0 / P, None, ALU.mult))
            ch(dve.tensor_scalar(col(U_COL), col(FIRST), 1.0 / P, None, ALU.mult))
            layer_norm_stats(dve, ch, "ln3", h[:, :, :], st[0])
            s, s4 = st[0], st[1]
            ch(dve.tensor_scalar(s4[:, 3, :], s[:, 3, :], 1.0 / C, None, ALU.mult))
            ch(dve.tensor_tensor(s4[:, 3, :], s4[:, 3, :], s[:, 2, :], ALU.mult))
            ch(dve.tensor_tensor(s4[:, 3, :], s4[:, 3, :], s[:, 2, :], ALU.mult))
            dve.tensor_scalar(s4[:, 4, :], s4[:, 3, :], LN_EPS, None, ALU.add).then_inc(sem("ln4_var"), 1)
            dve.tensor_tensor(fn[:, :, :], xc[:, :, :], bc(s[:, 2, :], C), ALU.mult).then_inc(sem("x3_ready"), 1)
            dve.wait_ge(sem("ln4_root"), 1)
            refined_rstd(dve, ch, s4)
            ch(dve.tensor_tensor(s4[:, 2, :], s4[:, 2, :], s[:, 2, :], ALU.mult))
            dve.tensor_tensor(xc[:, :, :], xc[:, :, :], bc(s4[:, 2, :], C), ALU.mult).then_inc(sem("x4_ready"), 1)
            dve.tensor_copy(W_t, col(W_COL).broadcast_to((P, TP))).then_inc(sem("W_t_filled"), 1)
            dve.wait_ge(sem("W_t_filled"), 1)
            ch(dve.memset(seq(W_t)[:, :, 0:1], NEG))
            for q in range(1, NQ, 2):
                pairs_out(dve, "x4", 0, q, hT, col(G1), col(B1))
            dve.wait_ge(sem("k_shifted"), 1)
            dve.tensor_copy(kT, banks(4)).then_inc(sem("kT_ready"), 1)
            ch(dve.tensor_tensor_scan(O_prev, W_t, k_last, 0.0, ALU.add, ALU.max))
            dve.tensor_tensor(seq(A2)[:, :, 1:], seq(O_prev)[:, :, 0:P - 1], seq(O_prev)[:, :, 1:], ALU.subtract)\
                .then_inc(sem("A2_log"), 1)
            dve.wait_ge(sem("kT_ready"), 1)
            dve.tensor_tensor(seq(E2)[:, :, 1:], seq(kT)[:, :, 0:P - 1], seq(O_prev)[:, :, 1:], ALU.subtract)\
                .then_inc(sem("E2_log"), 1)
            no = W_t
            ch(dve.scalar_tensor_tensor(no, kT, col(U_COL), O_prev, ALU.add, ALU.max))
            dve.wait_ge(sem("E2_log"), 1)
            dve.scalar_tensor_tensor(kT, kT, col(U_COL), no, ALU.add, ALU.subtract).then_inc(sem("E_log"), 1)
            dve.wait_ge(sem("A2_log"), 1)
            dve.tensor_tensor(O_prev, O_prev, no, ALU.subtract).then_inc(sem("A_log"), 1)
            dve.wait_ge(sem("E2_ready"), 1)
            dve.wait_ge(sem("vT_ready"), 1)
            ch(dve.tensor_tensor(seq(EV)[:, :, 1:], seq(E2)[:, :, 1:], seq(vT)[:, :, 0:P - 1], ALU.mult))
            dve.wait_ge(sem("A2_ready"), 1)
            ch(dve.tensor_tensor_scan(P_prev, A2, EV, 0.0, ALU.mult, ALU.add))
            ch(dve.tensor_tensor_scan(Q_prev, A2, E2, 0.0, ALU.mult, ALU.add))
            dve.wait_ge(sem("A_ready"), 1)
            dve.wait_ge(sem("E_ready"), 1)
            den, num, rden = Q_prev, P_prev, W_t
            ch(dve.tensor_tensor(den, O_prev, den, ALU.mult))
            dve.tensor_tensor(den, den, kT, ALU.add).then_inc(sem("den_ready"), 1)
            ch(dve.tensor_tensor(num, O_prev, num, ALU.mult))
            ch(dve.tensor_tensor(vT, kT, vT, ALU.mult))
            ch(dve.tensor_tensor(num, num, vT, ALU.add))
            dve.wait_ge(sem("srT_ready"), 1)
            ch(dve.tensor_tensor(num, num, srT, ALU.mult))
            dve.wait_ge(sem("den_inverse"), 1)
            ch(dve.tensor_tensor(den, den, rden, ALU.mult))
            ch(dve.scalar_tensor_tensor(rden, den, -2.0, rden, ALU.add, ALU.mult))
            dve.scalar_tensor_tensor(P_prev, num, -1.0, rden, ALU.mult, ALU.mult).then_inc(sem("ysT_ready"), 1)
            dve.wait_ge(sem("o_proj"), 1)
            dve.wait_ge(sem("x3_ready"), 1)
            ch(dve.tensor_tensor(fn[:, :, :], fn[:, :, :], banks(0).rearrange("p (t c) -> p t c", c=C), ALU.add))
            layer_norm_stats(dve, ch, "ln5", fn[:, :, :], st[0])
            dve.tensor_tensor(xc[:, :, :], xc[:, :, :], bc(st[0][:, 2, :], C), ALU.mult).then_inc(sem("x5_ready"), 1)
            ch(dve.tensor_tensor(h[:, :, :], h[:, :, :], fn[:, :, :], ALU.add))
            for q in range(1, NQ, 2):
                pairs_out(dve, "x5", 4, q, hT, col(G2), col(B2))
            for q in range(NQ):
                for i in range(1, 4, 2):
                    dve.wait_ge(sem("kk_proj"), 4 * q + i + 1)
                    src, dst = ps[:, (4 * q + i) % 8, :], hidT[:, i, q * BANK:(q + 1) * BANK]
                    ch(dve.tensor_scalar(dst, src, 0.0, None, ALU.max))
                    dve.tensor_tensor(dst, dst, dst, ALU.mult).then_inc(sem("kk_dve"), 1)
            dve.wait_ge(sem("srfT_ready"), 1)
            dve.wait_ge(sem("ff_proj"), NQ)
            dve.tensor_tensor(gatedT, srfT, banks(0), ALU.mult).then_inc(sem("gatedT_ready"), 1)
            dve.wait_ge(sem("gated_T"), NQ)
            ch(dve.tensor_tensor(h[:, :, :], h[:, :, :], banks(4).rearrange("p (t c) -> p t c", c=C), ALU.add))

        def recurrent_pe(pe):
            pe.wait_ge(sem("x4_ready"), 1)
            transpose_pairs(pe, xc)
            pe.wait_ge(sem("wl_in"), 16 * WL_LOADS)
            pe.wait_ge(sem("pairs_out0"), turned_out("x4", NQ - 1))
            pe.wait_ge(sem("pairs_out1"), turned_out("x4", NQ - 1))
            project(pe, w_bd[:, WK, :], hT, "k_proj", 4)
            project(pe, w_bd[:, WV, :], hT, "v_proj", 0)
            pe.wait_ge(sem("kT_ready"), 1)
            project(pe, w_bd[:, WR, :], hT, "r_proj", 4)
            pe.wait_ge(sem("ysT_ready"), 1)
            for p in range(NP):
                last = pe.matmul(ps[:, p // 4, p % 4 * P:(p % 4 + 1) * P], P_prev[:, p * P:(p + 1) * P],
                                 w_bd[:, WO, :], start=True, stop=True)
            last.then_inc(sem("o_proj"), 1)
            pe.wait_ge(sem("x5_ready"), 1)
            transpose_pairs(pe, xc, 4)
            for q in range(NQ):
                done = q if q == 0 else NQ - 1
                pe.wait_ge(sem("pairs_out0"), turned_out("x5", done))
                if q:
                    pe.wait_ge(sem("pairs_out1"), turned_out("x5", done))
                if q >= 2:
                    pe.wait_ge(sem("kk_act"), 2 * q - 2)
                    pe.wait_ge(sem("kk_dve"), 2 * q - 2)
                for i in range(4):
                    pe.matmul(ps[:, (4 * q + i) % 8, :], w_kf[:, i // 2, i % 2 * P:(i % 2 + 1) * P],
                              hT[:, q * BANK:(q + 1) * BANK], start=True, stop=True).then_inc(sem("kk_proj"), 1)
            pe.wait_ge(sem("kk_act"), 2 * NQ)
            pe.wait_ge(sem("kk_dve"), 2 * NQ)
            project(pe, w_bd[:, WRF, :], hT, "rf_proj", 4)
            for q in range(NQ):
                for par in range(2):
                    for k in range(2):
                        last = pe.matmul(ps[par * C:(par + 1) * C, q, :], w_vf[:, k, :],
                                         hidT[:, 2 * par + k, q * BANK:(q + 1) * BANK], start=k == 0, stop=k == 1)
                last.then_inc(sem("ff_proj"), 1)
            pe.wait_ge(sem("gatedT_ready"), 1)
            for p in range(NP):
                last = pe.transpose(ps[:, 4 + p // 4, p % 4 * P:(p % 4 + 1) * P], gatedT[:, p * P:(p + 1) * P], ident[:, :])
                if p % 4 == 3:
                    last.then_inc(sem("gated_T"), 1)

        HID_BANKS = (4, 5, 6, 7, 0, 1)

        def experts_act(act):
            ln_act(act, "ln6", st[1])
            for q in range(0, NQ, 2):
                pairs_out(act, "x6", 0, q, hT)
            for q in range(NQ):
                for i in range(4):
                    act.wait_ge(sem("hid_proj"), 4 * q + i + 1)
                    act.activation(hidT[:, i, q * BANK:(q + 1) * BANK], ps[:, HID_BANKS[(4 * q + i) % 6], :], ACT.Gelu,
                                   bias=col(HID_B + i % 2)).then_inc(sem("hid_ready"), 1)
            act.wait_ge(sem("route_shifted"), 1)
            act.activation(coef[:, :, :], tmp8[:, :, :], ACT.Exp).then_inc(sem("route_exp"), 1)
            act.wait_ge(sem("coefT_done"), 1)
            act.activation(coefT[:, :], ps[:, 4, 0:2 * P], ACT.Copy).then_inc(sem("coefT_ready"), 1)

        def experts_dve(dve, ch):
            layer_norm_stats(dve, ch, "ln6", h[:, :, :], st[1])
            dve.tensor_tensor(fn[:, :, :], xc[:, :, :], bc(st[1][:, 2, :], C), ALU.mult).then_inc(sem("x6_ready"), 1)
            for q in range(1, NQ, 2):
                pairs_out(dve, "x6", 0, q, hT)
            for q in range(NQ):
                dve.wait_ge(sem("lgT_done"), q + 1)
                dve.tensor_copy(lgT[:, q * BANK:(q + 1) * BANK], ps[0:C, 2 + q % 2, :]).then_inc(sem("lgT_ready"), 1)
            m, r = st[0][:, 0, :], st[0][:, 1, :]
            dve.wait_ge(sem("lg_done"), 1)
            lg = ps[:, 4, 0:NT * EX].rearrange("p (t e) -> p t e", e=EX)
            ch(dve.tensor_tensor(tmp8[:, :, :], lg, row(rows[:, EX_B, 0:EX], NT), ALU.add))
            ch(dve.tensor_reduce(m, tmp8[:, :, :], AX.X, ALU.max))
            dve.tensor_tensor(tmp8[:, :, :], tmp8[:, :, :], bc(m, EX), ALU.subtract).then_inc(sem("route_shifted"), 1)
            dve.wait_ge(sem("route_exp"), 1)
            ch(dve.tensor_reduce(r, coef[:, :, :], AX.X, ALU.add))
            ch(dve.reciprocal(r, r))
            ch(dve.tensor_tensor(coef[:, :, :], coef[:, :, :], bc(r, EX), ALU.mult))
            ch(dve.tensor_reduce(m, coef[:, :, :], AX.X, ALU.max))
            ch(dve.tensor_tensor(tmp8[:, :, :], coef[:, :, :], bc(m, EX), ALU.is_equal))
            dve.wait_ge(sem("rank_ready"), 1)
            ch(dve.tensor_tensor(tmp8[:, :, :], tmp8[:, :, :], row(rank[:, :], NT), ALU.mult))
            ch(dve.tensor_reduce(r, tmp8[:, :, :], AX.X, ALU.max))
            ch(dve.tensor_tensor(tmp8[:, :, :], tmp8[:, :, :], bc(r, EX), ALU.is_equal))
            dve.tensor_tensor(coef[:, :, :], coef[:, :, :], tmp8[:, :, :], ALU.mult).then_inc(sem("coef_ready"), 1)
            dve.wait_ge(sem("coef_ready"), 1)
            for t in range(NT):
                if t in (4, 8):
                    half = t // 4 - 1
                    ts = slice(half * NP, (half + 1) * NP)
                    dve.wait_ge(sem("bias_done"), half + 1)
                    dve.tensor_tensor(h[:, ts, :], h[:, ts, :],
                                      ps[:, 6:8, :].rearrange("p k (t c) -> p (k t) c", c=C), ALU.add)\
                        .then_inc(sem("bias_added"), 1)
                    if half:
                        dve.wait_ge(sem("bias_added"), 2)
                dve.wait_ge(sem("y_done"), t + 1)
                y = scratch[:, t % 4, :]
                dve.tensor_tensor(y.rearrange("p (e c) -> p e c", e=EX),
                                  ps[:, t % 4, :].rearrange("p (e c) -> p e c", e=EX), bc(coef[:, t, :], C), ALU.mult)\
                    .then_inc(sem("y_weighted"), 1)
                dve.wait_ge(sem("y_weighted"), t + 1)
                ch(dve.tensor_reduce(xp[:, t, :], y.rearrange("p (e c) -> p c e", e=EX), AX.X, ALU.add))
                if t + 1 in [t1 for _, t1 in STORES]:
                    ts = slice(*STORES[[t1 for _, t1 in STORES].index(t + 1)])
                    dve.tensor_tensor(h[:, ts, :], h[:, ts, :], xp[:, ts, :], ALU.add).then_inc(sem("h_done"), 1)

        def experts_pe(pe):
            pe.wait_ge(sem("x6_ready"), 1)
            transpose_pairs(pe, fn)
            def logits(q):
                pe.wait_ge(sem("hid_ready"), 4 * q + 4)
                if q >= 2:
                    pe.wait_ge(sem("lgT_ready"), q - 1)
                for par in range(2):
                    for k in range(2):
                        last = pe.matmul(ps[32 * par:32 * par + 32, 2 + q % 2, :], w_g[:, k, :],
                                         hidT[:, 2 * par + k, q * BANK:(q + 1) * BANK], start=k == 0, stop=k == 1)
                last.then_inc(sem("lgT_done"), 1)

            for q in range(NQ):
                done = q if q == 0 else NQ - 1
                pe.wait_ge(sem("pairs_out0"), turned_out("x6", done))
                if q:
                    pe.wait_ge(sem("pairs_out1"), turned_out("x6", done))
                for i in range(4):
                    if 4 * q + i >= 6:
                        pe.wait_ge(sem("hid_ready"), 4 * q + i - 5)
                    pe.matmul(ps[:, HID_BANKS[(4 * q + i) % 6], :], w_1[:, i // 2, i % 2 * P:(i % 2 + 1) * P],
                              hT[:, q * BANK:(q + 1) * BANK], start=True, stop=True).then_inc(sem("hid_proj"), 1)
                if q:
                    logits(q - 1)
            logits(NQ - 1)
            picked = ident[0:C, 0:C].rearrange("p (a e) -> p a e", a=2)[:, :, 0:EX]
            for p in range(NP):
                if p % 4 == 0:
                    pe.wait_ge(sem("lgT_ready"), p // 4 + 1)
                last = pe.matmul(ps[:, 4, p * 2 * EX:(p + 1) * 2 * EX], lgT[:, p * P:(p + 1) * P], picked,
                                 start=True, stop=True)
            last.then_inc(sem("lg_done"), 1)

            for t in range(NT):
                if t == 2:
                    pe.wait_ge(sem("lgT_ready"), NQ)
                if t == 4:
                    pe.wait_ge(sem("coef_ready"), 1)
                    for half in range(2):
                        last = pe.transpose(ps[:, 4, half * P:(half + 1) * P],
                                            coef[:, half * NP:(half + 1) * NP, :].rearrange("p t e -> p (t e)"),
                                            ident[:, :])
                    last.then_inc(sem("coefT_done"), 1)
                if t >= 4:
                    pe.wait_ge(sem("y_weighted"), t - 3)
                for k in range(2):
                    last = pe.matmul(ps[:, t % 4, :], hidT[:, t % 2 * 2 + k, t // 2 * P:(t // 2 + 1) * P],
                                     w_d[:, k, :], start=k == 0, stop=k == 1)
                last.then_inc(sem("y_done"), 1)
                if t in (4, 8):
                    half = t // 4 - 1
                    pe.wait_ge(sem("coefT_ready"), 1)
                    if half:
                        pe.wait_ge(sem("bias_added"), 1)
                    for k in range(2):
                        last = pe.matmul(ps[:, 6 + k, :], coefT[:, half * P:(half + 1) * P],
                                         w_bias[:, k * BANK:(k + 1) * BANK], start=True, stop=True)
                    last.then_inc(sem("bias_done"), 1)

        @block.sync
        def _(sp):
            sp.dma_start(x_int[:, :], a["x"]).then_inc(sem("x_in"), 16)
            sp.dma_start(wproj[:, :], a["L0_tok_w_proj"]).then_inc(sem("wproj_in"), 16)
            sp.dma_start(gate_w[:, :], a["fside_1S_w_gate"].partition_broadcast(P)).then_inc(sem("gate_in"), 16)
            sp.dma_start(gate_b[:, :], a["L0_tok_b_gate"].unsqueeze(0).partition_broadcast(P)).then_inc(sem("gate_in"), 16)
            sp.wait_ge(sem("wn_zeroed"), 1)

            def put(r, c, src):
                n, m = src.shape
                sp.dma_start(wn[r:r + n, c:c + m], src).then_inc(sem("wn_in"), 16)
                wn_loads.append(1)

            for par in range(2):
                put(par * C, WCOL["hl"] + par * C, a["L0_ffn_hl_w"].rearrange("n d h -> (n d) h"))
                for n in range(NH):
                    r = par * C + n * D
                    for e in range(NE):
                        put(r, WCOL[f"wq{e}"] + C + n * D, a["L0_ffn_wq"][n, e])
                    put(r, WCOL["wk"] + C + n * D, a["L0_ffn_wk"][n])
                    put(r, WCOL["wv"] + r, a["L0_ffn_wv"][n])
                    put(r, WCOL["fc1"] + r, a["L0_ffn_fc1_w"])
                    put(r, WCOL["fc2"] + r, a["L0_ffn_fc2_w"])
                put(par * NH, WCOL["fg"] + par * C, a["L0_ffn_fgate_w"])
            for n in range(NH):
                put(n * NE, WCOL[f"gate{n // 2}"] + n % 2 * C, a["L0_ffn_gate_w"][n])
            assert len(wn_loads) == WN_LOADS

            def vector_col(i, src):
                n = src.shape[0]
                for r in range(0, P, n):
                    sp.dma_start(cols[r:r + n, i:i + 1], src.unsqueeze(1)).then_inc(sem("cols_in"), 16)
                    col_loads.append(1)

            def vector_row(i, src):
                n = src.shape[0]
                for r in range(0, C, n):
                    if i == GATE_B and r:
                        break
                    sp.dma_start(rows[:, i, r:r + n], src.unsqueeze(0).partition_broadcast(P))\
                        .then_inc(sem("rows_in"), 16)
                    row_loads.append(1)

            vector_col(HL_B, a["L0_ffn_hl_b"].rearrange("n d -> (n d)"))
            vector_col(FC1_B, a["L0_ffn_fc1_b"])
            for i, name in ((G1, "g1"), (B1, "b1"), (G2, "g2"), (B2, "b2"), (DECAY, "spatial_decay"),
                            (FIRST, "spatial_first")):
                vector_col(i, a[f"L1_attn_{name}"])
            for k in range(2):
                vector_col(HID_B + k, a["L1_ffn_b1"][k * P:(k + 1) * P])
            sp.dma_start(rows[:, EX_B, 0:EX], a["L1_ffn_bg"].unsqueeze(0).partition_broadcast(P))\
                .then_inc(sem("rows_in"), 16)
            row_loads.append(1)
            for i, name in ((LN_G, "ln_g"), (LN_B, "ln_b"), (FN_G, "fnorm_g"), (FN_B, "fnorm_b"), (FC2_B, "fc2_b")):
                vector_row(i, a[f"L0_ffn_{name}"])
            vector_row(GATE_B, a["L0_ffn_gate_b"].rearrange("n e -> (n e)"))
            assert (len(col_loads), len(row_loads)) == (COL_LOADS, ROW_LOADS)
            if stop_after >= 3:
                sp.wait_ge(sem("wl_zeroed"), 1)
                L = "L1_attn_"
                for i, name in ((WK, "Wk"), (WV, "Wv"), (WR, "Wr"), (WO, "Wo"), (WRF, "Wr_ffn")):
                    for par in range(2):
                        r = slice(par * C, (par + 1) * C)
                        sp.dma_start(w_bd[r, i, r], a[L + name]).then_inc(sem("wl_in"), 16)
                for par in range(2):
                    r = slice(par * C, (par + 1) * C)
                    sp.dma_start(w_kf[r, par, :], a[L + "Wk_ffn"]).then_inc(sem("wl_in"), 16)
                    sp.dma_start(w_1[r, par, :], a["L1_ffn_W1"]).then_inc(sem("wl_in"), 16)
                sp.dma_start(w_vf[:, :, :], a[L + "Wv_ffn"].rearrange("(k p) c -> p k c", p=P)).then_inc(sem("wl_in"), 16)
                sp.dma_start(w_g[:, :, 0:EX], a["L1_ffn_Wg"].rearrange("(k p) c -> p k c", p=P)).then_inc(sem("wl_in"), 16)
                for k in range(2):
                    sp.dma_start(w_d[:, k, :].rearrange("p (e c) -> p e c", e=EX),
                                 a["L1_ffn_Wd"][:, k * P:(k + 1) * P, :].rearrange("e p c -> p e c"))\
                        .then_inc(sem("wl_in"), 16)
                for i in range(P // EX):
                    sp.dma_start(w_bias[i * EX:(i + 1) * EX, i * C:(i + 1) * C], a["L1_ffn_bd"]).then_inc(sem("wl_in"), 16)
            if stop_after == 4:
                for i, (t0, t1) in enumerate(STORES):
                    sp.wait_ge(sem("h_done"), i + 1)
                    sp.dma_start(out[t0:t1].rearrange("b s c -> s b c"), h[:, t0:t1, :]).then_inc(sem("out_stored"), 16)
                sp.wait_ge(sem("out_stored"), 16 * len(STORES))
            else:
                sp.wait_ge(sem("h_done"), 1)
                sp.dma_start(out.rearrange("b s c -> s b c"), h[:, :, :]).then_inc(sem("out_stored"), 16)
                sp.wait_ge(sem("out_stored"), 16)

        @block.gpsimd
        def _(pool):
            ch = Chain(pool, "pool_chain")
            ch(pool.memset(ident[:, :], 0.0))
            ch(pool.memset(ident2[:, :], 0.0))
            pool.affine_select(out=ident[:, :], in_=ident[:, :], compare_op=ALU.not_equal, fill=1.0,
                               base=0, pattern=[[-1, P]], channel_multiplier=1).then_inc(sem("ident_ready"), 1)
            ch(pool.affine_select(out=ident2[:, :], in_=ident2[:, :], compare_op=ALU.not_equal, fill=1.0,
                                  base=0, pattern=[[-1, C]], channel_multiplier=1))
            ch(pool.affine_select(out=ident2[:, :], in_=ident2[:, :], compare_op=ALU.not_equal, fill=1.0,
                                  base=-C, pattern=[[-1, C]], channel_multiplier=1))
            pool.wait_ge(sem("ident_ready"), 1)
            ch(pool.memset(zero16[:, :], 0.0))
            pool.tensor_copy(ident16[:, :], ident[:, :]).then_inc(sem("ident_ready"), 1)
            pool.memset(wn[:, :], 0.0).then_inc(sem("wn_zeroed"), 1)
            pool.wait_ge(sem("idx_ready"), 1)
            for t in range(NT):
                where = bass.IndirectOffsetOnAxis(ap=idx[:, t:t + 1], axis=0)
                for table, dst in (("L0_tok_fourier_table", geo_raw[:, t, 0:FOUR]),
                                   ("L0_tok_visit_table", geo_raw[:, t, FOUR:GEO]),
                                   ("L0_tok_emb_table", gate_in[:, t, 0:EMB])):
                    pool.indirect_dma_start(out=dst, out_offset=None, in_=a[table], in_offset=where)\
                        .then_inc(sem(f"gathered{t // GT}"), 16)
            ch(pool.tensor_copy(ident_bf[:, :], ident[:, :]))
            ch(pool.memset(masked[:, :, :], 0.0))
            ch(pool.affine_select(out=masked[:, :, :], in_=masked[:, :, :], compare_op=ALU.is_ge, fill=MASKED,
                                  base=0, pattern=[[0, NH], [-1, P]], channel_multiplier=1))
            ch(pool.memset(own_rows[:, :], 1.0))
            ch(pool.affine_select(out=own_rows[:, :], in_=own_rows[:, :], compare_op=ALU.is_ge, fill=0.0,
                                  base=0, pattern=[[-D, 2 * NH]], channel_multiplier=1))
            pool.affine_select(out=own_rows[:, :], in_=own_rows[:, :], compare_op=ALU.is_ge, fill=0.0,
                               base=D - 1, pattern=[[D, 2 * NH]], channel_multiplier=-1)\
                .then_inc(sem("masks_ready"), 1)
            pool.wait_ge(sem("masks_ready"), 1)
            pool.tensor_tensor(own_head[:, :], own_rows[:, 0:NH], own_rows[:, NH:], ALU.add)\
                .then_inc(sem("masks_ready"), 1)
            if stop_after < 2:
                return
            heads_pool(pool)
            if stop_after < 3:
                return
            recurrent_pool(pool)

        @block.scalar
        def _(act):
            ch = Chain(act, "act_chain")
            act.wait_ge(sem("gate_in"), 32)
            ch(act.activation(act_warm[:, 0:1], gate_b[:, :], ACT.Square))
            for g in range(NT // 4):
                act.wait_ge(sem("geo_transposed"), g + 1)
                if g >= 2:
                    act.wait_ge(sem("geo_projected"), g - 1)
                act.activation(geoT[:, g % 2, :], ps[0:GEO, g % 2, :], ACT.Copy).then_inc(sem("geoT_ready"), 1)
            for i in range(4):
                n = min(BANK, 14 * P + 40 - i * BANK)
                act.wait_ge(sem("wT_done"), i + 1)
                act.activation(WT[:, i * BANK:i * BANK + n], ps[:, 4 + i, 0:n], ACT.Copy).then_inc(sem("WT_ready"), 1)
            act.wait_ge(sem("glogit_ready"), 1)
            act.activation(gate[:, :], glogit[:, :], ACT.Exp, scale=-1.0).then_inc(sem("gate_exp"), 1)
            ln_act(act, "ln1", st[0])
            act.activation(st[0][:, 7, :], st[0][:, 3, :], ACT.Sqrt).then_inc(sem("ss_root"), 1)
            if stop_after < 1:
                return
            attention_act(act)
            if stop_after < 2:
                return
            heads_act(act)
            if stop_after < 3:
                return
            recurrent_act(act)
            if stop_after < 4:
                return
            experts_act(act)

        @block.vector
        def _(dve):
            ch = Chain(dve, "dve_chain")
            dve.wait_ge(sem("x_in"), 16)
            dve.tensor_copy(x_f[:, :], x_int[:, :]).then_inc(sem("x_f_ready"), 1)
            dve.wait_ge(sem("wprojT_done"), 1)
            dve.tensor_copy(wprojT[:, :], ps[0:GEO, 6, 0:C]).then_inc(sem("wprojT_ready"), 1)
            dve.wait_ge(sem("idT_done"), 1)
            dve.tensor_scalar(idx[:, :], ps[:, 7, 0:NT], 0.0, float(ITEMS - 1), ALU.max, ALU.min)\
                .then_inc(sem("idx_ready"), 1)
            dve.tensor_scalar(valid[:, :], ps[:, 7, 0:NT], 0.0, None, ALU.not_equal).then_inc(sem("idx_ready"), 1)
            dve.wait_ge(sem("idx_ready"), 2)
            dve.wait_ge(sem("gate_in"), 32)
            for g in range(NT // 4):
                ts = slice(4 * g, 4 * g + 4)
                dve.wait_ge(sem("geo_projected"), g + 1)
                dve.tensor_tensor(gate_in[:, ts, EMB:], ps[:, 2 + g % 2, 0:4 * C].rearrange("p (t c) -> p t c", t=4),
                                  bc(valid[:, ts], C), ALU.mult).then_inc(sem("geo_taken"), 1)
                dve.wait_ge(sem("geo_taken"), g + 1)
                if g % 2:
                    ts = slice(4 * g - 4, 4 * g + 4)
                    dve.wait_ge(sem(f"gathered{g // 2}"), 16 * 3 * GT)
                    ch(dve.tensor_tensor(prod[:, ts, :], gate_in[:, ts, :], row(gate_w[:, :], GT), ALU.mult))
                    ch(dve.tensor_reduce(glogit[:, ts], prod[:, ts, :], AX.X, ALU.add))
            dve.tensor_scalar(glogit[:, :], glogit[:, :], gate_b[:, :], None, ALU.add).then_inc(sem("glogit_ready"), 1)
            dve.wait_ge(sem("gate_exp"), 1)
            ch(dve.tensor_scalar(gate[:, :], gate[:, :], 1.0, None, ALU.add))
            ch(dve.reciprocal(gate[:, :], gate[:, :]))
            ch(dve.scalar_tensor_tensor(gate[:, :], gate[:, :], MAX_GATE, valid[:, :], ALU.mult, ALU.mult))
            ch(dve.tensor_tensor(xc[:, :, :], gate_in[:, :, EMB:], bc(gate[:, :], C), ALU.mult))
            ch(dve.tensor_tensor(h[:, :, :], xc[:, :, :], gate_in[:, :, 0:EMB], ALU.add))
            if stop_after < 1:
                dve.tensor_copy(xc[:, 0:1, 0:1], h[:, 0:1, 0:1]).then_inc(sem("h_done"), 1)
                dve.wait_ge(sem("h_done"), 1)
                layer_norm_stats(dve, ch, "ln1", h[:, :, :], st[0])
                return
            layer_norm_stats(dve, ch, "ln1", h[:, :, :], st[0])
            attention_dve(dve, ch)
            if stop_after < 2:
                dve.tensor_copy(xc[:, 0:1, 0:1], h[:, 0:1, 0:1]).then_inc(sem("h_done"), 1)
                dve.wait_ge(sem("h_done"), 1)
                return
            heads_dve(dve, ch)
            if stop_after < 3:
                dve.tensor_copy(xc[:, 0:1, 0:1], h[:, 0:1, 0:1]).then_inc(sem("h_done"), 1)
                dve.wait_ge(sem("h_done"), 1)
                return
            recurrent_dve(dve, ch)
            if stop_after < 4:
                dve.tensor_copy(xc[:, 0:1, 0:1], h[:, 0:1, 0:1]).then_inc(sem("h_done"), 1)
                dve.wait_ge(sem("h_done"), 1)
                return
            experts_dve(dve, ch)

        @block.tensor
        def _(pe):
            pe.wait_ge(sem("ident_ready"), 1)
            pe.wait_ge(sem("wproj_in"), 16)
            pe.transpose(ps[0:GEO, 6, 0:C], wproj[:, :], ident[0:C, 0:C]).then_inc(sem("wprojT_done"), 1)
            pe.wait_ge(sem("x_f_ready"), 1)
            pe.transpose(ps[:, 7, 0:NT], x_f[:, :], ident[0:NT, 0:NT]).then_inc(sem("idT_done"), 1)
            pe.wait_ge(sem("wn_in"), 16 * WN_LOADS)

            def turn(bank, col, name, n, off=0):
                w = WCOL[name] + off
                return pe.transpose(ps[:, bank, col:col + n], wn[0:n, w:w + P], ident[0:n, 0:n])

            turns = [("hl", 0)] + [(f"wq{e}", C * (1 - par)) for e in range(NE) for par in range(2)]\
                + [("wk", C * (1 - par)) for par in range(2)] + [("wv", 0)]
            for i, (name, off) in enumerate(turns):
                if i == 8:
                    pe.wait_ge(sem("wprojT_ready"), 1)
                last = turn(4 + i // 4, i % 4 * P, name, P, off)
                if i % 4 == 3:
                    last.then_inc(sem("wT_done"), 1)
            pe.wait_ge(sem("idx_ready"), 2)
            turn(7, 0, "fc1", P)
            turn(7, P, "fc2", P)
            turn(7, 2 * P, "fg", 2 * NH)
            turn(7, 2 * P + 8, "gate0", NH * NE)
            turn(7, 2 * P + 24, "gate1", NH * NE).then_inc(sem("wT_done"), 1)
            pe.wait_ge(sem("wprojT_ready"), 1)
            for g in range(NT // 4):
                pe.wait_ge(sem(f"gathered{g // 2}"), 16 * 3 * GT)
                if g >= 2:
                    pe.wait_ge(sem("geoT_ready"), g - 1)
                for i in range(4):
                    last = pe.transpose(ps[0:GEO, g % 2, i * P:(i + 1) * P], geo_raw[:, 4 * g + i, :], ident[:, :])
                last.then_inc(sem("geo_transposed"), 1)
                pe.wait_ge(sem("geoT_ready"), g + 1)
                if g >= 2:
                    pe.wait_ge(sem("geo_taken"), g - 1)
                for i in range(4):
                    last = pe.matmul(ps[:, 2 + g % 2, i * C:(i + 1) * C], geoT[:, g % 2, i * P:(i + 1) * P],
                                     wprojT[:, :], start=True, stop=True)
                last.then_inc(sem("geo_projected"), 1)
            if stop_after < 1:
                return
            attention_pe(pe)
            if stop_after < 2:
                return
            heads_pe(pe)
            if stop_after < 3:
                return
            recurrent_pe(pe)
            if stop_after < 4:
                return
            experts_pe(pe)



def kernel(**inputs):
    import numpy as _np
    import concourse.bacc as _bacc
    from concourse import mybir as _mybir
    from concourse.bass_utils import run_bass_kernel_spmd as _run

    nc = _bacc.Bacc("TRN2", target_bir_lowering=False, num_devices=1)
    arrays, args = {}, {}
    for name in inputs:
        v = _np.ascontiguousarray(inputs[name])
        arrays[f"in_{name}_dram"] = v
        args[name] = nc.dram_tensor(f"in_{name}_dram", v.shape, _mybir.dt.from_np(v.dtype), kind="ExternalInput").ap()
    shape = inputs["x"].shape + (inputs["L0_tok_emb_table"].shape[1],)
    out = nc.dram_tensor("out_dram", shape, _mybir.dt.float32, kind="ExternalOutput").ap()
    tower(nc, args, out)
    r = _run(nc, [arrays], core_ids=[0])
    return r.results[0]["out_dram"]
```

```python
from contextlib import ExitStack

import concourse.bass as bass
from concourse import mybir

ALU = mybir.AluOpType
ACT = mybir.ActivationFunctionType
AX = mybir.AxisListType
F32 = mybir.dt.float32
F16 = mybir.dt.float16
F32R = mybir.dt.float32r
BF16 = mybir.dt.bfloat16
I32 = mybir.dt.int32
U32 = mybir.dt.uint32

P = 128
C = 64
NH = 4
NE = 4
D = C // NH
BANK = 512
LN_EPS = 1e-5
FFN_EPS = 1e-8
FSCALE = 64.0
MASKED = -1e30
NEG = -1e38
MAX_GATE = 0.2
BLEND = 0.8




def tower(nc, a, out):
    B, S = a["x"].shape
    NT = B
    NP = NT // 2
    T = B * S
    TP = T // 2
    NQ = TP // BANK
    assert S == P and NT % 8 == 0
    EMB = a["L0_tok_emb_table"].shape[1]
    FOUR = a["L0_tok_fourier_table"].shape[1]
    VIS = a["L0_tok_visit_table"].shape[1]
    GEO = FOUR + VIS
    ITEMS = a["L0_tok_emb_table"].shape[0]
    EX = a["L1_ffn_Wd"].shape[0]
    GT = 8
    GROUPS = [(0, GT), (GT, 2 * GT), (2 * GT, NT)]
    NG = len(GROUPS)
    STORES = [(0, NP), (NP, NP + GT), (NP + GT, NT - 2), (NT - 2, NT)]

    ctx = ExitStack()
    with ctx:
        def sb(name, shape, dt=F32):
            return ctx.enter_context(nc.sbuf_tensor(name, shape, dt))

        sems = {}

        def sem(name):
            if name not in sems:
                sems[name] = ctx.enter_context(nc.semaphore(name))
            return sems[name]

        ident = sb("ident", [P, P])
        ident2 = sb("ident2", [P, C])
        ident16 = sb("ident16", [P, P], F16)
        x_int = sb("x_int", [NT, P], I32)
        x_f = sb("x_f", [NT, P])
        idx = sb("idx", [P, NT], U32)
        valid = sb("valid", [P, NT])
        gate_w = sb("gate_w", [P, EMB + C])
        gate_b = sb("gate_b", [P, 1])
        wproj = sb("wproj", [C, GEO])
        wprojT = sb("wprojT", [GEO, C])
        R1 = sb("R1", [P, 8192])
        R2 = sb("R2", [P, 8192])
        R3 = sb("R3", [P, 8192])
        gate_in = R3[:, 0:NT * P].rearrange("p (t c) -> p t c", t=NT)
        geo_raw = [x[:, 0:NP * GEO].rearrange("p (t c) -> p t c", t=NP) for x in (R2, R1[:, T + T // 2:])]
        geoT = R3[0:GEO, 6144:7168].rearrange("p (z n) -> p z n", z=2)
        glogit = sb("glogit", [P, NT])
        gate = sb("gate", [P, NT])
        h = sb("h", [P, NT, C])
        xc = sb("xc", [P, NT, C])
        sq = sb("sq", [P, NT, C])
        fn = sb("fn", [P, NT, C])
        prod = sq[:, :, :].rearrange("p (t z) c -> p t (z c)", z=2)
        st = [sb(f"st{i}", [P, 8, NT]) for i in range(2)]
        stD = sb("stD", [P, 8, NT * NH])
        F4 = sb("F4", [P, NT, 4 * C], F16)
        F_hi = F4[:, :, C:2 * C]
        F_lo = F4[:, :, 2 * C:3 * C]
        ps = ctx.enter_context(nc.psum_tensor("ps", [P, 8, BANK], F32))
        A_hl = R1[:, 0:T // 2].bitcast(F16)
        M_hh = R1[:, T // 2:T].bitcast(F16)
        M_ll = R1[:, T:T + T // 2].bitcast(F16)
        e32 = R2[:, 0:4096].rearrange("p (u n) -> p u n", u=4)
        eh = R2[:, 4096:6144].bitcast(F16).rearrange("p (u n) -> p u n", u=4)
        el = R2[:, 6144:8192].bitcast(F16).rearrange("p (u n) -> p u n", u=4)
        attT = R3[:, 0:T]
        racc = sb("racc", [P, NT, 4])
        zero16 = sb("zero16", [P, P], F16)
        act_warm = sb("act_warm", [P, 2])

        ident_bf = sb("ident_bf", [P, P], BF16)
        masked = sb("masked", [P, NH, P], BF16)
        own_rows = sb("own_rows", [P, 2 * NH])
        own_head = sb("own_head", [P, NH])
        WCOL = {"hl": 0, "wq0": 128, "wq1": 320, "wq2": 512, "wq3": 704, "wk": 896, "wv": 1088, "fc1": 1216,
                "fc2": 1344, "fg": 1472, "gate0": 1600, "gate1": 1728}
        wn = R3[:, 4096:4096 + 1856]
        WT = sb("WT", [P, 14 * P + 40])
        wT_hl = WT[:, 0:P]
        wT_q = [[WT[:, (1 + 2 * e + par) * P:(2 + 2 * e + par) * P] for par in range(2)] for e in range(NE)]
        wT_k = [WT[:, (9 + par) * P:(10 + par) * P] for par in range(2)]
        wT_v = WT[:, 11 * P:12 * P]
        wT_fc1 = WT[:, 12 * P:13 * P]
        wT_fc2 = WT[:, 13 * P:14 * P]
        wT_fg = WT[:, 14 * P:14 * P + 2 * NH]
        wT_gate = [WT[:, 14 * P + 8 + 16 * c:14 * P + 24 + 16 * c] for c in range(2)]
        cols = sb("cols", [P, 17])
        HL_B, FC1_B, G1, B1, G2, B2, DECAY, FIRST, HID_B, W_COL, U_COL = [*range(9), 10, 11]
        LN_G, LN_B, FC2_B, FG_COL, FB_COL = range(12, 17)
        rows = sb("rows", [P, 8, C])
        FN_G, FN_B, GATE_B, EX_B = range(4)
        sx = sb("sx", [P, NT, C])
        kept = sb("kept", [P, NT, C])
        GL4 = sb("GL4", [P, 4, NH * NE])
        gates4 = sb("gates4", [P, 4, NH * NE])
        xT = R3[:, 0:TP]
        sxT = R1[:, 0:TP]
        Pb = R1[:, 2048:4096].rearrange("p (e n) -> p e n", e=NE)
        PT = R1[:, 4096:8192].rearrange("p (z e n) -> p z e n", z=2, e=NE)
        O4 = R2[:, 0:4 * NH * C].rearrange("p (t n) -> p t n", t=4)
        mixed4 = R2[:, 1024:1280].rearrange("p (t c) -> p t c", t=4)
        KZ = sb("KZ", [P, 2, 2 * BANK], F32R)
        qs = sb("qs", [P, 2, NE * P], F32R)
        qf = R3[C:P, 4096:5120].rearrange("p (z n) -> p z n", z=2)
        kf = R3[:, 5120:5376]
        kh = sb("kh", [P, 2 * P], F32R)
        kl = R3[:, 2048:2304]
        vs = R3[:, 5376:5888].rearrange("p (z a n d) -> p z a n d", z=2, a=2, n=NH)
        ATs = R3[:, 5888:6400]
        Ost = R3[:, 6400:6912].rearrange("p (z n) -> p z n", z=2)
        OTs = R3[:, 6912:7168]
        O1 = R3[:, 7168:7424]
        sxs = R3[:, 7424:7552]
        hxT, hx2T = R1[:, 0:TP], R1[:, TP:2 * TP]
        resid = sb("resid", [P, C])
        gm = sb("gm", [P, 4 * NH])
        ones = sb("ones", [P, 1])
        fg = sb("fg", [P, NT * NH])
        negmax = R3[:, 7552:7568].rearrange("p (e n) -> p e n", e=NE)
        rl = R3[:, 7568:7584].rearrange("p (e n) -> p e n", e=NE)

        wl = F4[:, :, :].rearrange("p t c -> p (t c)").bitcast(F32)
        w_bd = wl[:, 0:5 * P].rearrange("p (i n) -> p i n", i=5)
        WK, WV, WR, WO, WRF = range(5)
        w_kf = wl[:, 640:1152].rearrange("p (a n) -> p a n", a=2)
        w_1 = wl[:, 1152:1664].rearrange("p (a n) -> p a n", a=2)
        w_vf = wl[:, 1664:1792].rearrange("p (k n) -> p k n", k=2)
        w_g = wl[:, 1792:1856].rearrange("p (k n) -> p k n", k=2)
        w_bias = wl[:, 1856:2880]
        w_d = wl[:, 2880:3904].rearrange("p (k n) -> p k n", k=2)
        kT, vT, srT, W_t = (R1[:, i * TP:(i + 1) * TP] for i in range(4))
        O_prev, k_last, A2, E2 = (R2[:, i * TP:(i + 1) * TP] for i in range(4))
        hT, EV, P_prev, Q_prev = (R3[:, i * TP:(i + 1) * TP] for i in range(4))
        hidT = R1[:, :].rearrange("p (i n) -> p i n", i=4)
        srfT, gatedT = R2[:, 0:TP], R2[:, TP:2 * TP]
        scratch = R2[:, 2 * TP:4 * TP].rearrange("p (z n) -> p z n", z=8)
        lgT = R3[:, TP:2 * TP]
        picked = sb("picked", [P, 2, EX])
        coef = sb("coef", [P, NT, EX])
        tmp8 = sb("tmp8", [P, NT, EX])
        rank = sb("rank", [P, EX])
        coefT = sb("coefT", [P, 2 * P])
        xp = R3[:, 2 * TP:3 * TP].rearrange("p (t c) -> p t c", c=C)

        block = ctx.enter_context(nc.Block())

        def bc(ap, n):
            return ap.unsqueeze(2).broadcast_to(tuple(ap.shape) + (n,))

        def row(ap, t):
            return ap.unsqueeze(1).broadcast_to((ap.shape[0], t, ap.shape[1]))

        class Chain:

            def __init__(self, eng, name):
                self.eng, self.sem, self.n = eng, sem(name), 0

            def __call__(self, ins):
                self.n += 1
                ins.then_inc(self.sem, 1)
                self.eng.wait_ge(self.sem, self.n)

        NORMS = ("ln2", "mix", "hx", "ln3", "ln5", "ln6")
        TURNS = ("x", "fx", "fo", "x4", "x5", "x6")

        def nth(name):
            return NG + NORMS.index(name) + 1

        def nth_half(name, half):
            return NG + 2 * NORMS.index(name) + half + 1

        def turned(name, q):
            return TURNS.index(name) * NQ + q + 1

        def turned_out(name, q):
            return TURNS.index(name) * (NQ // 2) + q // 2 + 1

        def refined_rstd(dve, ch, s):
            ch(dve.reciprocal(s[:, 2, :], s[:, 5, :]))
            ch(dve.tensor_tensor(s[:, 6, :], s[:, 2, :], s[:, 2, :], ALU.mult))
            ch(dve.tensor_tensor(s[:, 6, :], s[:, 6, :], s[:, 4, :], ALU.mult))
            ch(dve.tensor_scalar(s[:, 6, :], s[:, 6, :], -0.5, 1.5, ALU.mult, ALU.add))
            ch(dve.tensor_tensor(s[:, 2, :], s[:, 2, :], s[:, 6, :], ALU.mult))

        def scaled(dve, dst, x, r, w, name):
            n = x.shape[1]
            for half in (slice(0, n // 2), slice(n // 2, n)):
                dve.tensor_tensor(dst[:, half, :], x[:, half, :], bc(r[:, half], w), ALU.mult).then_inc(sem(name), 1)

        def layer_norm_stats(dve, ch, name, x, s, eps=LN_EPS, w=C, arrives=None):
            xcv = xc[:, :, :].rearrange("p t (n d) -> p (t n) d", d=w)
            sqv = sq[:, :, :].rearrange("p t (n d) -> p (t n) d", d=w)
            if arrives is None:
                last = dve.tensor_reduce(s[:, 0, :], x, AX.X, ALU.add)
            else:
                for q in range(NQ):
                    part = slice(q * x.shape[1] // NQ, (q + 1) * x.shape[1] // NQ)
                    dve.wait_ge(sem(arrives), q + 1)
                    last = dve.tensor_reduce(s[:, 0, part], x[:, part, :], AX.X, ALU.add)
            ch(last)
            ch(dve.tensor_scalar(s[:, 1, :], s[:, 0, :], 1.0 / w, None, ALU.mult))
            groups = x.shape[1]
            halves = [slice(0, groups // 2), slice(groups // 2, groups)]
            for half in halves:
                dve.tensor_tensor(xcv[:, half, :], x[:, half, :], bc(s[:, 1, half], w), ALU.subtract)\
                    .then_inc(sem("ln_centred"), 1)
            for i, half in enumerate(halves):
                dve.wait_ge(sem("ln_squared"), nth_half(name, i))
                last = dve.tensor_reduce(s[:, 3, half], sqv[:, half, :], AX.X, ALU.add)
                ch(last)
            dve.tensor_scalar(s[:, 4, :], s[:, 3, :], 1.0 / w, eps, ALU.mult, ALU.add).then_inc(sem("ln_var"), 1)
            dve.wait_ge(sem("ln_root"), nth(name))
            dve.wait_ge(sem("ln_var"), nth(name))
            refined_rstd(dve, ch, s)
            return xcv

        def ln_act(act, name, s):
            act.activation(act_warm[:, 1:2], act_warm[:, 0:1], ACT.Sqrt)
            for i in range(2):
                ts = slice(i * NT // 2, (i + 1) * NT // 2)
                act.wait_ge(sem("ln_centred"), nth_half(name, i))
                act.activation(sq[:, ts, :], xc[:, ts, :], ACT.Square).then_inc(sem("ln_squared"), 1)
            act.wait_ge(sem("ln_var"), nth(name))
            act.activation(s[:, 5, :], s[:, 4, :], ACT.Sqrt).then_inc(sem("ln_root"), 1)

        HALF = T // 2
        SLOT = HALF // 2
        STEPS = 2 * NT
        U = 4
        SEGMENTS = [(0, 0, 4), (0, 4, STEPS // U), (1, 0, STEPS // U)]
        BEFORE = [(0, 1), (2,), ()]

        def iterations(eng, it0, it1, body):
            if it1 - it0 == 1:
                body(it0)
            elif it1 - it0 > 1:
                with eng.Fori(it0, it1) as it:
                    body(it)

        SPLITS = [(A_hl, C), (M_hh, 0), (M_ll, 2 * C)]
        FG = [(m, q) for q in range(NT // 8) for m in range(3)]

        def fg_range(g):
            return GROUPS[g][0] * 3 // GT, GROUPS[g][1] * 3 // GT

        def fT_out(eng, g):
            m, q = FG[g]
            eng.wait_ge(sem("fT_done"), g + 1)
            dst = SPLITS[m][0][:, q * 1024:(q + 1) * 1024]
            src = ps[:, 4 + g % 4, :].bitcast(F16)
            name = f"fT_out{g % 2}"
            if g % 2:
                eng.tensor_copy(dst, src).then_inc(sem(name), 1)
            else:
                eng.activation(dst, src, ACT.Copy).then_inc(sem(name), 1)

        def geo_act(act, g):
            act.wait_ge(sem("geo_transposed"), g + 1)
            if g >= 2:
                act.wait_ge(sem("geo_projected"), g - 1)
            act.activation(geoT[:, g % 2, :], ps[0:GEO, 4 + g % 2, :], ACT.Copy).then_inc(sem("geoT_ready"), 1)

        def geo_dve(dve, g):
            ts = slice(4 * g, 4 * g + 4)
            dve.wait_ge(sem("geo_projected"), g + 1)
            dve.tensor_tensor(gate_in[:, ts, EMB:], ps[:, 6 + g % 2, 0:4 * C].rearrange("p (t c) -> p t c", t=4),
                              bc(valid[:, ts], C), ALU.mult).then_inc(sem("geo_taken"), 1)

        def tokens_act(act, g):
            ts, s = slice(*GROUPS[g]), st[0]
            for i in range(ts.start // 4, ts.stop // 4):
                geo_act(act, i)
            act.wait_ge(sem("glogit_ready"), g + 1)
            act.activation(gate[:, ts], glogit[:, ts], ACT.Exp, scale=-1.0).then_inc(sem("gate_exp"), 1)
            act.activation(act_warm[:, 1:2], act_warm[:, 0:1], ACT.Sqrt)
            act.wait_ge(sem("ln_centred"), g + 1)
            act.activation(sq[:, ts, :], xc[:, ts, :], ACT.Square).then_inc(sem("ln_squared"), 1)
            act.wait_ge(sem("ln_var"), g + 1)
            act.activation(s[:, 5:8:2, ts], s[:, 4:8:2, ts], ACT.Sqrt).then_inc(sem("ln_root"), 1)
            act.wait_ge(sem("f_ready"), g + 1)
            act.activation(F4[:, ts, 0:C], fn[:, ts, :], ACT.Copy, scale=FSCALE).then_inc(sem("f_doubled"), 1)
            act.wait_ge(sem("f_split"), g + 1)
            act.activation(F4[:, ts, 3 * C:], F_lo[:, ts, :], ACT.Copy).then_inc(sem("f_doubled"), 1)
            for i in range(*fg_range(g)):
                if i % 2 == 0:
                    fT_out(act, i)

        def tokens_dve(dve, ch, g):
            ts, s = slice(*GROUPS[g]), st[0]
            for i in range(ts.start // 4, ts.stop // 4):
                geo_dve(dve, i)
            dve.wait_ge(sem("geo_taken"), ts.stop // 4)
            for i in range(ts.start // GT, ts.stop // GT):
                dve.wait_ge(sem(f"gathered{i}"), 16 * 3 * GT)
            n = ts.stop - ts.start
            ch(dve.tensor_tensor(prod[:, 0:n, :], gate_in[:, ts, :], row(gate_w[:, :], n), ALU.mult))
            ch(dve.tensor_reduce(glogit[:, ts], prod[:, 0:n, :], AX.X, ALU.add))
            dve.tensor_scalar(glogit[:, ts], glogit[:, ts], gate_b[:, :], None, ALU.add).then_inc(sem("glogit_ready"), 1)
            dve.wait_ge(sem("gate_exp"), g + 1)
            ch(dve.tensor_scalar(gate[:, ts], gate[:, ts], 1.0, None, ALU.add))
            ch(dve.reciprocal(gate[:, ts], gate[:, ts]))
            ch(dve.scalar_tensor_tensor(gate[:, ts], gate[:, ts], MAX_GATE, valid[:, ts], ALU.mult, ALU.mult))
            ch(dve.tensor_tensor(xc[:, ts, :], gate_in[:, ts, EMB:], bc(gate[:, ts], C), ALU.mult))
            ch(dve.tensor_tensor(h[:, ts, :], xc[:, ts, :], gate_in[:, ts, 0:EMB], ALU.add))
            ch(dve.tensor_reduce(s[:, 0, ts], h[:, ts, :], AX.X, ALU.add))
            ch(dve.tensor_scalar(s[:, 1, ts], s[:, 0, ts], 1.0 / C, None, ALU.mult))
            dve.tensor_tensor(xc[:, ts, :], h[:, ts, :], bc(s[:, 1, ts], C), ALU.subtract).then_inc(sem("ln_centred"), 1)
            dve.wait_ge(sem("ln_squared"), g + 1)
            ch(dve.tensor_reduce(s[:, 6, ts], sq[:, ts, :], AX.X, ALU.add))
            dve.tensor_scalar(s[:, 4, ts], s[:, 6, ts], 1.0 / C, LN_EPS, ALU.mult, ALU.add).then_inc(sem("ln_var"), 1)
            dve.wait_ge(sem("ln_root"), g + 1)
            refined_rstd(dve, ch, s[:, :, ts])
            ch(dve.tensor_tensor(s[:, 6, ts], s[:, 7, ts], s[:, 2, ts], ALU.mult))
            ch(dve.tensor_scalar(s[:, 6, ts], s[:, 6, ts], 1e-12, None, ALU.max))
            ch(dve.reciprocal(s[:, 6, ts], s[:, 6, ts]))
            ch(dve.tensor_tensor(s[:, 6, ts], s[:, 6, ts], s[:, 2, ts], ALU.mult))
            dve.tensor_tensor(fn[:, ts, :], xc[:, ts, :], bc(s[:, 6, ts], C), ALU.mult).then_inc(sem("f_ready"), 1)
            dve.wait_ge(sem("f_ready"), g + 1)
            ch(dve.tensor_scalar(F_hi[:, ts, :], fn[:, ts, :], FSCALE, None, ALU.mult))
            dve.scalar_tensor_tensor(F_lo[:, ts, :], fn[:, ts, :], FSCALE, F_hi[:, ts, :], ALU.mult, ALU.subtract)\
                .then_inc(sem("f_split"), 1)
            for i in range(*fg_range(g)):
                if i % 2:
                    fT_out(dve, i)

        def tokens_pe(pe, g):
            t0, t1 = GROUPS[g]
            if g:
                pe.wait_ge(sem("fT_out0"), fg_range(g)[0] - fg_range(g)[0] // 2)
                pe.wait_ge(sem("fT_out1"), fg_range(g)[0] // 2)
            if g == 2:
                pe.wait_ge(sem("exp_done"), SEGMENTS[0][2] * U)
            first = t0 // 4
            for i in range(first, t1 // 4 + 1):
                if i < t1 // 4:
                    if i % (GT // 4) == 0:
                        pe.wait_ge(sem(f"gathered{4 * i // GT}"), 16 * 3 * GT)
                    if i >= first + 2:
                        pe.wait_ge(sem("geoT_ready"), i - 1)
                    for k in range(4):
                        t = 4 * i + k
                        last = pe.transpose(ps[0:GEO, 4 + i % 2, k * P:(k + 1) * P], geo_raw[t // NP][:, t % NP, :],
                                            ident[:, :])
                    last.then_inc(sem("geo_transposed"), 1)
                if i > first:
                    pe.wait_ge(sem("geoT_ready"), i)
                    if i >= first + 3:
                        pe.wait_ge(sem("geo_taken"), i - 2)
                    for k in range(4):
                        last = pe.matmul(ps[:, 6 + (i - 1) % 2, k * C:(k + 1) * C],
                                         geoT[:, (i - 1) % 2, k * P:(k + 1) * P], wprojT[:, :], start=True, stop=True)
                    last.then_inc(sem("geo_projected"), 1)
            pe.wait_ge(sem("f_split"), g + 1)
            pe.wait_ge(sem("f_doubled"), 2 * g + 2)
            pe.wait_ge(sem("geo_taken"), t1 // 4)
            if g == 0:
                pe.wait_ge(sem("ident_ready"), 2)
            for i in range(*fg_range(g)):
                if i >= 4 + fg_range(g)[0]:
                    pe.wait_ge(sem(f"fT_out{i % 2}"), (i - 4) // 2 + 1)
                m, q = FG[i]
                bank = ps[:, 4 + i % 4, :].bitcast(F16)
                for k in range(GT):
                    last = pe.transpose(bank[:, k * P:(k + 1) * P], F4[:, GT * q + k, SPLITS[m][1]:SPLITS[m][1] + P],
                                        ident16[:, :])
                last.then_inc(sem("fT_done"), 1)

        def turn_weights(pe):
            pe.wait_ge(sem("wn_in"), 16 * WN_LOADS)

            def turn(bank, col, name, n, off=0):
                w = WCOL[name] + off
                return pe.transpose(ps[:, bank, col:col + n], wn[0:n, w:w + P], ident[0:n, 0:n])

            turns = [("hl", 0)] + [(f"wq{e}", C * (1 - par)) for e in range(NE) for par in range(2)]\
                + [("wk", C * (1 - par)) for par in range(2)] + [("wv", 0)]
            for i, (name, off) in enumerate(turns):
                last = turn(i // 4, i % 4 * P, name, P, off)
                if i % 4 == 3:
                    last.then_inc(sem("wT_done"), 1)
            turn(3, 0, "fc1", P)
            turn(3, P, "fc2", P)
            turn(3, 2 * P, "fg", 2 * NH)
            turn(3, 2 * P + 8, "gate0", NH * NE)
            turn(3, 2 * P + 24, "gate1", NH * NE).then_inc(sem("wT_done"), 1)

        def attention_act(act):
            for seg, (half, it0, it1) in enumerate(SEGMENTS):
                base = half * STEPS
                for g in BEFORE[seg]:
                    tokens_act(act, g)
                    if g == 0:
                        for i in range(4):
                            n = min(BANK, 14 * P + 40 - i * BANK)
                            act.wait_ge(sem("wT_done"), i + 1)
                            act.activation(WT[:, i * BANK:i * BANK + n], ps[:, i, 0:n], ACT.Copy)\
                                .then_inc(sem("WT_ready"), 1)
                act.activation(act_warm[:, 1:2], act_warm[:, 0:1], ACT.Exp)

                def exponentials(it):
                    for u in range(U):
                        slot = u % 2
                        s_in = ps[:, 4 + 2 * slot:6 + 2 * slot, :]
                        act.wait_ge(sem("scores_done"), it * U + base + u + 1)
                        if slot == 0:
                            act.activation(eh[:, u, :].rearrange("p (b n) -> p b n", b=2), s_in, ACT.Exp,
                                           scale=1.0 / FSCALE ** 2)
                        act.activation(e32[:, u, :].rearrange("p (b n) -> p b n", b=2), s_in, ACT.Exp,
                                       scale=1.0 / FSCALE ** 2,
                                       accum_out=racc[:, bass.ds(it * (U // 2) + u // 2, 1), 2 * half + slot])\
                            .then_inc(sem("exp_done"), 1)
                iterations(act, it0, it1, exponentials)
                if it1 < STEPS // U:
                    continue
                act.wait_ge(sem("att_done"), half + 1)
                act.activation(attT[:, half * HALF:half * HALF + SLOT].rearrange("p (b n) -> p b n", b=2),
                               ps[:, 0:2, :], ACT.Copy).then_inc(sem("att_out_act"), 1)
            act.activation(act_warm[:, 1:2], act_warm[:, 0:1], ACT.Sqrt)
            for q in range(4):
                ts = slice(q * 8, (q + 1) * 8)
                act.wait_ge(sem("fcm_dve"), q + 1)
                act.activation(sq[:, ts, :], xc[:, ts, :], ACT.Square).then_inc(sem("fcm_act"), 1)
            act.wait_ge(sem("fcm_dve"), 8)
            act.activation(st[1][:, 5, :], st[1][:, 4, :], ACT.Sqrt).then_inc(sem("fcm_act"), 1)

        def attention_dve(dve, ch):
            for seg, (half, it0, it1) in enumerate(SEGMENTS):
                base = half * STEPS
                for g in BEFORE[seg]:
                    tokens_dve(dve, ch, g)
                def split(it):
                    for u in range(U):
                        dve.wait_ge(sem("exp_done"), it * U + base + u + 1)
                        if u % 2 == 1:
                            dve.tensor_copy(eh[:, u, :], e32[:, u, :]).then_inc(sem("eh_done"), 1)
                            dve.wait_ge(sem("eh_done"), it * (U // 2) + base // 2 + u // 2 + 1)
                        dve.tensor_tensor(el[:, u, :], e32[:, u, :], eh[:, u, :], ALU.subtract)\
                            .then_inc(sem("e_split"), 1)
                iterations(dve, it0, it1, split)
                if it1 < STEPS // U:
                    continue
                dve.wait_ge(sem("att_done"), half + 1)
                dve.tensor_copy(attT[:, half * HALF + SLOT:(half + 1) * HALF].rearrange("p (b n) -> p b n", b=2),
                                ps[:, 2:4, :]).then_inc(sem("att_out_dve"), 1)
            s = st[1]
            ch(dve.tensor_reduce(s[:, 0, :], racc[:, :, :], AX.X, ALU.add))
            ch(dve.reciprocal(s[:, 1, :], s[:, 0, :]))
            ch(dve.tensor_scalar(s[:, 1, :], s[:, 1, :], (1.0 - BLEND) / FSCALE, None, ALU.mult))
            for q in range(4):
                ts = slice(q * 8, (q + 1) * 8)
                dve.wait_ge(sem("att_token"), q + 1)
                ch(dve.tensor_tensor(xc[:, ts, :], ps[:, 4 + q, :].rearrange("p (t c) -> p t c", c=C), bc(s[:, 1, ts], C),
                                     ALU.mult))
                dve.scalar_tensor_tensor(xc[:, ts, :], fn[:, ts, :], BLEND, xc[:, ts, :], ALU.mult, ALU.add)\
                    .then_inc(sem("fcm_dve"), 1)
            for q in range(4):
                ts = slice(q * 8, (q + 1) * 8)
                dve.wait_ge(sem("fcm_act"), q + 1)
                dve.tensor_reduce(s[:, 4, ts], sq[:, ts, :], AX.X, ALU.add).then_inc(sem("fcm_dve"), 1)
            dve.wait_ge(sem("fcm_act"), 5)
            ch(dve.tensor_scalar(s[:, 6, :], s[:, 5, :], 1e-12, None, ALU.max))
            ch(dve.reciprocal(s[:, 6, :], s[:, 6, :]))
            ch(dve.tensor_tensor(xc[:, :, :], xc[:, :, :], bc(s[:, 6, :], C), ALU.mult))
            ch(dve.tensor_tensor(h[:, :, :], h[:, :, :], xc[:, :, :], ALU.add))

        def attention_pe(pe):
            def scores(half, slot, j):
                for c in range(2):
                    col = half * HALF + slot * SLOT + c * BANK
                    lhs = A_hl[:, bass.ds(j * P, P)]
                    pe.matmul(ps[:, 4 + 2 * slot + c, :], lhs, M_hh[:, col:col + BANK], start=True, stop=False)
                    last = pe.matmul(ps[:, 4 + 2 * slot + c, :], lhs, M_ll[:, col:col + BANK], start=False, stop=True)
                last.then_inc(sem("scores_done"), 1)

            def weigh(slot, u, j):
                for part in (eh, el):
                    for c in range(2):
                        pe.matmul(ps[:, 2 * slot + c, :], F4[:, bass.ds(j, 1), C:3 * C].rearrange("p t c -> p (t c)"),
                                  part[:, u, c * BANK:(c + 1) * BANK], start=False, stop=False, skip_group_check=True)

            for seg, (half, it0, it1) in enumerate(SEGMENTS):
                base = half * STEPS
                for g in BEFORE[seg]:
                    tokens_pe(pe, g)
                    if g == 0:
                        turn_weights(pe)
                n = fg_range(max(g for b in BEFORE[:seg + 1] for g in b))[1]
                pe.wait_ge(sem("fT_out0"), n - n // 2)
                pe.wait_ge(sem("fT_out1"), n // 2)
                if half:
                    pe.wait_ge(sem("att_out_act"), half)
                    pe.wait_ge(sem("att_out_dve"), half)
                if it0 == 0:
                    pe.wait_ge(sem("WT_ready"), 4)
                    for c in range(4):
                        pe.matmul(ps[:, c, :], zero16[:, :], M_hh[:, c * BANK:(c + 1) * BANK], start=True, stop=False,
                                  skip_group_check=True)
                for slot in range(2):
                    scores(half, slot, it0 * (U // 2))
                pe.wait_ge(sem("exp_done"), base + it0 * U + 1)
                scores(half, 0, it0 * (U // 2) + 1)

                def steps(it, last=False):
                    for u in range(U):
                        if u == 0 or not last:
                            pe.wait_ge(sem("exp_done"), it * U + base + u + 2)
                            scores(half, (u + 1) % 2, it * (U // 2) + (u + 3) // 2)
                        pe.wait_ge(sem("e_split"), it * U + base + u + 1)
                        weigh(u % 2, u, it * (U // 2) + u // 2)
                iterations(pe, it0, it1 - 1, steps)
                steps(it1 - 1, last=True)
                if it1 < STEPS // U:
                    continue
                for c in range(4):
                    last = pe.matmul(ps[:, c, :], zero16[:, :], M_hh[:, c * BANK:(c + 1) * BANK], start=False,
                                     stop=True, skip_group_check=True)
                last.then_inc(sem("att_done"), 1)
            pe.wait_ge(sem("exp_done"), 2 * STEPS)
            for t in range(NT):
                if t == NP:
                    pe.wait_ge(sem("att_out_act"), 2)
                if t == NP + GT:
                    pe.wait_ge(sem("att_out_dve"), 2)
                last = pe.matmul(ps[:, 4 + t // 8, t % 8 * C:(t % 8 + 1) * C], attT[:, t * P:(t + 1) * P], ident2[:, :],
                                 start=True, stop=True)
                if t % 8 == 7:
                    last.then_inc(sem("att_token"), 1)

        WN_LOADS, COL_LOADS, ROW_LOADS, WL_LOADS = 2 * (1 + NH * (NE + 4) + 1) + NH, 2 + 8 + 12 + 2 + 5 * P // D, 2 * NH + 2, 10 + 4 + 4 + P // EX
        wn_loads, col_loads, row_loads = [], [], []

        def transpose_pairs(pe, src, first_bank, ready):
            for p in range(NP):
                if p % (NP // 2) == 0:
                    pe.wait_ge(sem(ready), 1 + p // (NP // 2))
                last = pe.transpose(ps[:, first_bank + p // 4, p % 4 * P:(p % 4 + 1) * P],
                                    src[:, 2 * p:2 * p + 2, :].rearrange("p t c -> p (t c)"), ident[:, :])
                if p % 4 == 3:
                    last.then_inc(sem("pairs_turned"), 1)

        def project(pe, w, src, name, first_bank):
            for q in range(NQ):
                pe.matmul(ps[:, first_bank + q, :], w, src[:, q * BANK:(q + 1) * BANK], start=True, stop=True)\
                    .then_inc(sem(name), 1)

        def batches(eng, one):
            for b in range(4):
                one(b, b // 2, b, b, 0)
            with eng.Fori(1, NT // 4 - 1) as it:
                for m in range(4):
                    one(it * 4 + m, it * 2 + m // 2, m, None, it)
            for b in range(NT - 4, NT + 3):
                one(b, b // 2, b % 4, b, b // 4)

        def has(n, lo, hi=NT):
            return n is None or lo <= n < hi

        def grouped(n, m, step):
            return m == step and has(n, 4, NT)

        gates = gates4[:, :, :].rearrange("p t (n e) -> p (t n) e", e=NE)

        def mix(eng, g):
            o = O4.rearrange("p t (g d) -> p (t g) d", d=D)
            o4 = O4.rearrange("p t (n f) -> p (t n) f", f=NE * D)
            m4 = mixed4.rearrange("p t (n d) -> p (t n) d", d=D)
            half = NE // 2 * D
            eng.tensor_tensor(o, o, bc(gates4[:, :, :].rearrange("p t g -> p (t g)"), D), ALU.mult)\
                .then_inc(sem("mixing"), 1)
            eng.wait_ge(sem("mixing"), g * 5 + 2)
            eng.tensor_tensor(o4[:, :, 0:half], o4[:, :, 0:half], o4[:, :, half:], ALU.add)\
                .then_inc(sem("mixing"), 1)
            eng.wait_ge(sem("mixing"), g * 5 + 3)
            eng.tensor_tensor(m4, o4[:, :, 0:D], o4[:, :, D:half], ALU.add).then_inc(sem("mixing"), 1)
            eng.wait_ge(sem("mixing"), g * 5 + 4)
            eng.tensor_tensor(mixed4, mixed4, row(resid[:, :], 4), ALU.add).then_inc(sem("mixing"), 1)
            eng.wait_ge(sem("mixing"), g * 5 + 5)
            eng.tensor_copy(fn[:, bass.ds(g * 4, 4), :], mixed4).then_inc(sem("mixing"), 1)

        SXT_BANKS = (7, 4, 5, 6)

        def heads_pool(pool):
            pool.wait_ge(sem("att_out_act"), 2)
            pool.wait_ge(sem("att_token"), 4)
            pool.memset(R3[:, 5376:5888], 0.0).then_inc(sem("vs_zeroed"), 1)
            pool.wait_ge(sem("vs_zeroed"), 1)
            pool.memset(vs[:, :, :, :, D:D + 1].rearrange("p z a n d -> p (z a n) d"), 1.0).then_inc(sem("vs_ones"), 1)

            pool.memset(ones[:, :], 1.0)
            pool.memset(mixed4, 0.0).then_inc(sem("mixing"), 1)
            pool.wait_ge(sem("mixing"), 1)
            pool.memset(wl[:, 0:3904], 0.0).then_inc(sem("wl_zeroed"), 1)
            for e in range(EX):
                last = pool.memset(rank[:, e:e + 1], float(EX - e))
            last.then_inc(sem("rank_ready"), 1)

            def stage_sxT(p, first=False):
                if not first:
                    pool.wait_ge(sem("q_done"), p * 2)
                pool.tensor_copy(sxs[:, :], sxT[:, bass.ds(p * P, P)]).then_inc(sem("sxs_ready"), 1)

            def spread_keys(b, par, n):
                if n is None or n >= 2:
                    pool.wait_ge(sem("S_done"), (b - 1) * 4)
                for i, part in enumerate((kh, kl)):
                    last = pool.tensor_tensor(KZ[:, par, i * BANK:(i + 1) * BANK].rearrange("p (n t) -> p n t", t=P),
                                              row(part[:, par * P:(par + 1) * P], NH), bc(own_head[:, :], P), ALU.mult)
                last.then_inc(sem("kz_ready"), 1)

            pool.wait_ge(sem("sxT_ready"), 1)
            stage_sxT(0, True)
            pool.wait_ge(sem("sxT_ready"), NQ)
            pool.wait_ge(sem("masks_ready"), 2)
            pool.wait_ge(sem("kl_ready"), 1)
            spread_keys(0, 0, 0)

            def one(b, p, m, n, it):
                par = m % 2
                if par == 0:
                    if has(n, 0, NT - 2):
                        stage_sxT(p + 1)
                    if has(n, 0):
                        spread_keys(b + 1, 1, n + 1 if n is not None else None)
                else:
                    if has(n, 0, NT - 2):
                        pool.wait_ge(sem("kl_ready"), p + 2)
                        spread_keys(b + 1, 0, n + 1 if n is not None else None)
                if grouped(n, m, 3):
                    pool.wait_ge(sem("gs_ready"), it)
                    pool.wait_ge(sem("O_copied"), it * 4)
                    pool.wait_ge(sem("resid_ready"), 1)
                    mix(pool, it - 1)
                if has(n, 3, NT + 3):
                    pool.wait_ge(sem("O_done"), b - 2)
                    if m == 3 and grouped(n, m, 3):
                        pool.wait_ge(sem("mixing"), it * 5 + 1)
                    done = Ost[:, (m + 1) % 2, :]
                    pool.tensor_tensor(O4[:, (m + 1) % 4, :], done, ones[:, :].broadcast_to((P, NH * C)),
                                       ALU.mult).then_inc(sem("O_copied"), 1)
            batches(pool, one)

        def heads_pe(pe):
            transpose_pairs(pe, fn, 0, "ln2_done")
            pe.wait_ge(sem("WT_ready"), 4)
            for q in range(NQ):
                pe.wait_ge(sem(f"pairs_out{q % 2}"), turned_out("x", q))
                pe.matmul(ps[:, SXT_BANKS[q], :], wT_hl, xT[:, q * BANK:(q + 1) * BANK], start=True, stop=True)\
                    .then_inc(sem("sxT_done"), 1)
            pe.wait_ge(sem("masks_ready"), 1)

            def project_k(p):
                pe.wait_ge(sem("sxs_ready"), p + 1)
                for par in range(2):
                    pe.matmul(ps[:, 7, par * P:(par + 1) * P], wT_k[par], sxs[:, :], start=True, stop=True)
                pe.transpose(ps[:, 7, 3 * P:4 * P], sxs[:, :], ident[:, :]).then_inc(sem("k_done"), 1)

            def project_v(p):
                pe.matmul(ps[:, 7, 3 * P:4 * P], sxs[:, :], wT_v, start=True, stop=True).then_inc(sem("v_done"), 1)

            def project_q(b, par):
                for e in range(NE):
                    last = pe.matmul(ps[:, 7, e * P:(e + 1) * P], wT_q[e][par], sxs[:, :], start=True, stop=True)
                last.then_inc(sem("q_done"), 1)

            project_k(0)
            pe.wait_ge(sem("sxT_ready"), NQ)
            pe.wait_ge(sem("k_out"), 1)
            pe.wait_ge(sem("sx_out"), 1)
            project_q(0, 0)
            pe.wait_ge(sem("q_out"), 1)
            project_v(0)

            def one(b, p, m, n, it):
                par, z = m % 2, m // 2
                for e in range(NE):
                    if n is None or n >= 1:
                        if has(n, 1, NT + 1):
                            pe.wait_ge(sem("exp2_done"), b * 4 + e - 3)
                    if has(n, 0):
                        if e == 0:
                            pe.wait_ge(sem("q_split"), b + 1)
                            pe.wait_ge(sem("kz_ready"), b + 1)
                        for i in range(2):
                            pe.matmul(ps[:, e, :], qs[:, par, e * P:(e + 1) * P],
                                      KZ[:, par, i * BANK:(i + 1) * BANK], start=i == 0, stop=False)
                        pe.matmul(ps[:, e, :], ident_bf[:, :], masked[:, :, :].rearrange("p n t -> p (n t)"),
                                  start=False, stop=True).then_inc(sem("S_done"), 1)
                    if e == 3 and par == 1 and has(n, 0, NT - 2):
                        if n is not None and n < 3:
                            pe.wait_ge(sem("q_out"), b + 2)
                        else:
                            pe.wait_ge(sem("gl_out"), b - 2)
                        project_v(p + 1)
                    if e == 3 and par == 0 and has(n, 0, NT - 2):
                        if n is None or n >= 3:
                            pe.wait_ge(sem("gl_out"), b - 2)
                        else:
                            pe.wait_ge(sem("q_out"), b + 2)
                        project_k(p + 1)
                    if has(n, 1, NT + 1):
                        if n is None or 4 * n + e - 5 > 0:
                            pe.wait_ge(sem("PT_out"), b * 4 + e - 5)
                        for g in range(NH):
                            last = pe.transpose(ps[:, 4 + e % 2, g * P:(g + 1) * P], Pb[:, e, g * P:(g + 1) * P],
                                                ident[:, :])
                        last.then_inc(sem("T_done"), 1)
                    if e == 0:
                        if has(n, 0, NT - 1):
                            if par == 0:
                                pe.wait_ge(sem("v_out"), p + 1)
                            else:
                                pe.wait_ge(sem("k_out"), p + 2)
                                pe.wait_ge(sem("sx_out"), p + 2)
                            project_q(b + 1, 1 - par)
                    if e == 1:
                        if has(n, 2, NT + 2):
                            pe.wait_ge(sem("PT_out"), b * 4 - 4)
                            pe.wait_ge(sem("v_out"), p)
                            if n is None or n >= 3:
                                pe.wait_ge(sem("O_done"), b - 2)
                            for g in range(NH):
                                last = pe.matmul(ps[32 * g:32 * g + 32, 6, :], vs[:, (m // 2 + 1) % 2, par, g, :],
                                                 PT[:, par, :, g * P:(g + 1) * P], start=True, stop=True)
                            last.then_inc(sem("AV_done"), 1)
                    if e == 1 and has(n, 3, NT + 3):
                        pe.wait_ge(sem("O_done"), b - 2)
                        if has(n, 0, NT - 1):
                            pe.wait_ge(sem("q_out"), b + 2)
                        else:
                            pe.wait_ge(sem("gl_out"), b - 3)
                        for c in range(2):
                            last = pe.transpose(ps[:, 7, c * P:(c + 1) * P], Ost[:, (m + 1) % 2, c * P:(c + 1) * P],
                                                ident[:, :])
                        last.then_inc(sem("OT_done"), 1)
                    if e == 2:
                        if has(n, 3, NT + 3):
                            pe.wait_ge(sem("OT_out"), b - 2)
                            for c in range(2):
                                last = pe.matmul(ps[:, 7, 256:256 + NH * NE], OTs[:, c * P:(c + 1) * P], wT_gate[c],
                                                 start=c == 0, stop=c == 1)
                            last.then_inc(sem("gl_done"), 1)
                    if e == 3:
                        if has(n, 2, NT + 2):
                            pe.wait_ge(sem("AT_out"), b - 1)
                            for g in range(NE):
                                last = pe.transpose(ps[:, 6, g * P:(g + 1) * P], ATs[:, g * P:(g + 1) * P], ident[:, :])
                            last.then_inc(sem("ATt_done"), 1)
            batches(pe, one)
            tail_pe(pe)

        def heads_act(act):
            ln_act(act, "ln2", st[0])
            for q in range(0, NQ, 2):
                act.wait_ge(sem("pairs_turned"), turned("x", q))
                act.activation(xT[:, q * BANK:(q + 1) * BANK], ps[:, q, :], ACT.Copy).then_inc(sem("pairs_out0"), 1)
            act.wait_ge(sem("cols_in"), 16 * COL_LOADS)
            for q in range(0, NQ, 2):
                act.wait_ge(sem("sxT_done"), q + 1)
                act.activation(sxT[:, q * BANK:(q + 1) * BANK], ps[:, SXT_BANKS[q], :], ACT.Identity,
                               bias=col(HL_B)).then_inc(sem("sxT_ready"), 1)
            act.wait_ge(sem("vs_ones"), 1)

            def k_out(p, z, b=None, n=0):
                act.wait_ge(sem("k_done"), p + 1)
                if b is not None:
                    act.wait_ge(sem("kz_ready"), b + 2)
                act.activation(kf, ps[:, 7, 0:2 * P], ACT.Copy)
                act.activation(kh[:, :], ps[:, 7, 0:2 * P], ACT.Copy).then_inc(sem("k_out"), 1)

            def v_out(p, z):
                act.wait_ge(sem("v_done"), p + 1)
                act.activation(vs[:, z, :, :, 0:D].rearrange("p a n d -> p (a n) d"),
                               ps[:, 7, 3 * P:4 * P].rearrange("p (g d) -> p g d", d=D), ACT.Copy)\
                    .then_inc(sem("v_out"), 1)

            def q_out(b, par):
                act.wait_ge(sem("q_done"), b + 1)
                act.activation(qs[:, par, :], ps[:, 7, :], ACT.Copy, scale=float(D) ** 0.5)
                act.activation(qf[:, par, :], ps[C:P, 7, :], ACT.Copy, scale=float(D) ** 0.5).then_inc(sem("q_out"), 1)

            k_out(0, 0)
            q_out(0, 0)
            v_out(0, 0)

            def one(b, p, m, n, it):
                par, z = m % 2, m // 2
                for e in range(NE):
                    if e == 0:
                        if has(n, 0, NT - 1):
                            q_out(b + 1, 1 - par)
                    if e == 0 and grouped(n, m, 3):
                        act.wait_ge(sem("gs_shifted"), it)
                        act.activation(gates, gates, ACT.Exp).then_inc(sem("gs_exp"), 1)
                    if e == 1 and has(n, 3, NT + 3):
                        act.wait_ge(sem("OT_done"), b - 2)
                        act.activation(OTs[:, :], ps[:, 7, 0:2 * P], ACT.Copy).then_inc(sem("OT_out"), 1)
                    if e == 1:
                        if has(n, 2, NT + 2):
                            act.wait_ge(sem("AV_done"), b - 1)
                            act.activation(ATs[:, :], ps[:, 6, :], ACT.Copy).then_inc(sem("AT_out"), 1)
                    if e == 2 and has(n, 3, NT + 3):
                        act.wait_ge(sem("gl_done"), b - 2)
                        act.activation(GL4[:, (m + 1) % 4, :], ps[:, 7, 256:256 + NH * NE], ACT.Copy).then_inc(sem("gl_out"), 1)
                    if e == 3 and par == 1 and has(n, 0, NT - 2):
                        v_out(p + 1, (z + 1) % 2)
                    if e == 3 and par == 0 and has(n, 0, NT - 2):
                        k_out(p + 1, (z + 1) % 2, b)
                    if has(n, 0):
                        act.wait_ge(sem("max_done"), b * 4 + e + 1)
                        if n is None or n >= 1:
                            act.wait_ge(sem("T_done"), b * 4 + e - 3)
                        for g in range(NH):
                            last = act.activation(Pb[:, e, g * P:(g + 1) * P], ps[:, e, g * P:(g + 1) * P], ACT.Exp,
                                                  bias=negmax[:, e, g:g + 1])
                        last.then_inc(sem("exp2_done"), 1)
            batches(act, one)
            tail_act(act)

        def heads_dve(dve, ch):
            s = st[0]
            layer_norm_stats(dve, ch, "ln2", h[:, :, :], s)
            scaled(dve, fn[:, :, :], xc[:, :, :], s[:, 2, :], C, "ln2_done")
            for q in range(1, NQ, 2):
                dve.wait_ge(sem("pairs_turned"), turned("x", q))
                dve.tensor_copy(xT[:, q * BANK:(q + 1) * BANK], ps[:, q, :]).then_inc(sem("pairs_out1"), 1)
            dve.wait_ge(sem("cols_in"), 16 * COL_LOADS)
            dve.wait_ge(sem("sxT_ready"), 1)
            for q in range(1, NQ, 2):
                dve.wait_ge(sem("sxT_done"), q + 1)
                dve.tensor_scalar(sxT[:, q * BANK:(q + 1) * BANK], ps[:, SXT_BANKS[q], :], col(HL_B), None, ALU.add)\
                    .then_inc(sem("sxT_ready"), 1)

            def sx_out(p):
                dve.wait_ge(sem("k_done"), p + 1)
                dve.wait_ge(sem("k_out"), p + 1)
                dve.tensor_scalar(kept[:, bass.ds(p * 2, 2), :].rearrange("p t c -> p (t c)"), ps[:, 7, 3 * P:4 * P],
                                  0.0, None, ALU.not_equal)
                dve.tensor_copy(sx[:, bass.ds(p * 2, 2), :].rearrange("p t c -> p (t c)"), ps[:, 7, 3 * P:4 * P])\
                    .then_inc(sem("sx_out"), 1)

            def k_split(p):
                dve.tensor_tensor(kl, kf, kh[:, :], ALU.subtract).then_inc(sem("kl_ready"), 1)

            def q_split(b, par):
                dve.wait_ge(sem("q_out"), b + 1)
                dve.tensor_tensor(qs[C:P, par, :], qf[:, par, :], qs[C:P, par, :], ALU.subtract)\
                    .then_inc(sem("q_split"), 1)

            def gate_shift(g):
                dve.wait_ge(sem("gl_out"), g * 4 + 4)
                dve.wait_ge(sem("mixing"), g * 5 + 1)
                dve.tensor_tensor(gates4[:, :, :], GL4[:, :, :], row(rows[:, GATE_B, 0:NH * NE], 4), ALU.add).then_inc(sem("gate_step"), 1)
                dve.wait_ge(sem("gate_step"), g * 4 + 1)
                dve.tensor_reduce(gm[:, :], gates, AX.X, ALU.max).then_inc(sem("gate_step"), 1)
                dve.wait_ge(sem("gate_step"), g * 4 + 2)
                dve.tensor_tensor(gates, gates, bc(gm[:, :], NE), ALU.subtract).then_inc(sem("gs_shifted"), 1)

            def gate_weights(g):
                dve.wait_ge(sem("gs_exp"), g + 1)
                dve.tensor_reduce(gm[:, :], gates, AX.X, ALU.add).then_inc(sem("gate_step"), 1)
                dve.wait_ge(sem("gate_step"), g * 4 + 3)
                dve.reciprocal(gm[:, :], gm[:, :]).then_inc(sem("gate_step"), 1)
                dve.wait_ge(sem("gate_step"), g * 4 + 4)
                dve.tensor_tensor(gates, gates, bc(gm[:, :], NE), ALU.mult).then_inc(sem("gs_ready"), 1)

            sx_out(0)
            k_split(0)
            q_split(0, 0)

            def one(b, p, m, n, it):
                par, z = m % 2, m // 2
                for e in range(NE):
                    if has(n, 0):
                        dve.wait_ge(sem("S_done"), b * 4 + e + 1)
                        dve.tensor_reduce(negmax[:, e, :], ps[:, e, :].rearrange("p (n t) -> p n t", t=P), AX.X,
                                          ALU.max, negate=True).then_inc(sem("max_done"), 1)
                    if e == 1 and has(n, 0, NT - 1):
                        q_split(b + 1, 1 - par)
                    if e == 0 and grouped(n, m, 3):
                        gate_weights(it - 1)
                    if has(n, 1, NT + 1):
                        dve.wait_ge(sem("T_done"), b * 4 + e - 3)
                        if n is None or n >= 3:
                            dve.wait_ge(sem("AV_done"), b - 2)
                        dve.tensor_copy(PT[:, (m + 1) % 2, e, :], ps[:, 4 + e % 2, :]).then_inc(sem("PT_out"), 1)
                if par == 0 and has(n, 0, NT - 2):
                    sx_out(p + 1)
                    k_split(p + 1)
                if n == 3:
                    dve.wait_ge(sem("rows_in"), 16 * ROW_LOADS)
                    dve.wait_ge(sem("sx_out"), 2)
                    for i in range(NH):
                        last = dve.tensor_copy(resid[:, i * D:(i + 1) * D], sx[:, i, i * D:(i + 1) * D])
                    last.then_inc(sem("resid_ready"), 1)
                if has(n, 2, NT + 2):
                    dve.wait_ge(sem("ATt_done"), b - 1)
                    at = ps[:, 6, :].rearrange("p (e n d) -> p e n d", e=NE, n=NH)
                    dve.reciprocal(rl[:, :, :], at[:, :, :, D:D + 1].rearrange("p e n d -> p e (n d)"))\
                        .then_inc(sem("out_step"), 1)
                    dve.wait_ge(sem("out_step"), b * 2 - 3)
                    dve.tensor_tensor(O1[:, :].rearrange("p (n e d) -> p e n d", n=NH, e=NE), at[:, :, :, 0:D],
                                      rl[:, :, :].unsqueeze(3).broadcast_to((P, NE, NH, D)), ALU.mult)\
                        .then_inc(sem("out_step"), 1)
                    dve.wait_ge(sem("out_step"), b * 2 - 2)
                    if n is None or n >= 4:
                        dve.wait_ge(sem("O_copied"), b - 3)
                        dve.wait_ge(sem("OT_done"), b - 3)
                    keep = kept[:, bass.ds(b - 2, 1), :].rearrange("p t (n d) -> p (t n) d", d=D).unsqueeze(2)\
                        .broadcast_to((P, NH, NE, D))
                    dve.tensor_tensor(Ost[:, par, :].rearrange("p (n e d) -> p n e d", n=NH, e=NE), keep,
                                      O1[:, :].rearrange("p (n e d) -> p n e d", n=NH, e=NE), ALU.mult)\
                        .then_inc(sem("O_done"), 1)
                if grouped(n, m, 2):
                    gate_shift(it - 1)
            batches(dve, one)
            last = NT // 4 - 1
            gate_shift(last)
            gate_weights(last)
            dve.wait_ge(sem("O_copied"), NT)
            dve.wait_ge(sem("gs_ready"), NT // 4)
            dve.wait_ge(sem("mixing"), last * 5 + 1)
            mix(dve, last)
            tail_dve(dve, ch)

        def tail_act(act):
            act.wait_ge(sem("gs_shifted"), NT // 4)
            act.activation(gates, gates, ACT.Exp).then_inc(sem("gs_exp"), 1)
            ln_act(act, "mix", stD)
            for q in range(0, NQ, 2):
                pairs_out(act, "fx", 0, q, xT, col(LN_G), col(LN_B))
            for q in range(NQ):
                act.wait_ge(sem("fc_done"), q + 1)
                act.activation(hxT[:, q * BANK:(q + 1) * BANK], ps[:, 4 + q, :], ACT.Relu,
                               bias=cols[:, FC1_B:FC1_B + 1]).then_inc(sem("hxT_biased"), 1)
            for q in range(NQ):
                act.wait_ge(sem("fc_done"), NQ + q + 1)
                act.activation(hx2T[:, q * BANK:(q + 1) * BANK], ps[:, q, :], ACT.Identity,
                               bias=col(FC2_B)).then_inc(sem("hxT_biased"), 1)
            ln_act(act, "hx", stD)
            for q in range(0, NQ, 2):
                pairs_out(act, "fo", 0, q, xT, col(FG_COL), col(FB_COL))
            act.wait_ge(sem("fg_shifted"), 1)
            act.activation(fg[:, :], fg[:, :], ACT.Exp).then_inc(sem("fg_exp"), 1)

        def tail_dve(dve, ch):
            dve.wait_ge(sem("mixing"), NT // 4 * 5 + 1)

            def normalised(name, x, done, arrives=None):
                xcv = layer_norm_stats(dve, ch, name, x, stD, FFN_EPS, D, arrives)
                scaled(dve, xcv, xcv, stD[:, 2, :], D, done)

            normalised("mix", fn[:, :, :].rearrange("p t (n d) -> p (t n) d", d=D), "fx_ready")
            for q in range(1, NQ, 2):
                pairs_out(dve, "fx", 0, q, xT, col(LN_G), col(LN_B))
            dve.wait_ge(sem("pairs_out1"), turned_out("fx", NQ - 1))
            dve.wait_ge(sem("pairs_out0"), turned_out("fx", NQ - 1))
            for q in range(NQ):
                c = slice(q * BANK, (q + 1) * BANK)
                dve.wait_ge(sem("hxT_biased"), q + 1)
                dve.scalar_tensor_tensor(hxT[:, c], xT[:, c], 0.0, hxT[:, c], ALU.not_equal, ALU.mult)\
                    .then_inc(sem("hxT_ready"), 1)
            for q in range(NQ):
                c = slice(q * BANK, (q + 1) * BANK)
                dve.wait_ge(sem("hxT_biased"), NQ + q + 1)
                dve.scalar_tensor_tensor(hx2T[:, c], xT[:, c], 0.0, hx2T[:, c], ALU.not_equal, ALU.mult)\
                    .then_inc(sem("hxT_ready"), 1)
            normalised("hx", ps[:, 4:8, :].rearrange("p k (n d) -> p (k n) d", d=D), "fo_ready", "hx_token")
            dve.wait_ge(sem("fo_ready"), 2)
            ch(dve.tensor_tensor(fn[:, :, :], xc[:, :, :], row(rows[:, FN_G, :], NT), ALU.mult))
            for q in range(1, NQ, 2):
                pairs_out(dve, "fo", 0, q, xT, col(FG_COL), col(FB_COL))
            ch(dve.tensor_tensor(fn[:, :, :], fn[:, :, :], row(rows[:, FN_B, :], NT), ALU.add))
            fgv = fg[:, :].rearrange("p (t n) -> p t n", n=NH)
            m, r = st[0][:, 0, :], st[0][:, 1, :]
            dve.wait_ge(sem("fg_done"), 1)
            ch(dve.tensor_reduce(m, ps[:, 4, 0:NT * NH].rearrange("p (t n) -> p t n", n=NH), AX.X, ALU.max))
            dve.tensor_tensor(fgv, ps[:, 4, 0:NT * NH].rearrange("p (t n) -> p t n", n=NH), bc(m, NH), ALU.subtract)\
                .then_inc(sem("fg_shifted"), 1)
            dve.wait_ge(sem("fg_exp"), 1)
            ch(dve.tensor_reduce(r, fgv, AX.X, ALU.add))
            ch(dve.reciprocal(r, r))
            ch(dve.tensor_tensor(fgv, fgv, bc(r, NH), ALU.mult))
            ch(dve.tensor_tensor(xc[:, :, :].rearrange("p t (n d) -> p (t n) d", d=D),
                                 fn[:, :, :].rearrange("p t (n d) -> p (t n) d", d=D), bc(fg[:, :], D), ALU.mult))
            ch(dve.tensor_tensor(h[:, :, :], h[:, :, :], xc[:, :, :], ALU.add))

        def tail_pe(pe):
            transpose_pairs(pe, xc, 0, "fx_ready")
            for q in range(NQ):
                pe.wait_ge(sem(f"pairs_out{q % 2}"), turned_out("fx", q))
                pe.matmul(ps[:, 4 + q, :], wT_fc1, xT[:, q * BANK:(q + 1) * BANK], start=True, stop=True)\
                    .then_inc(sem("fc_done"), 1)
            for q in range(NQ):
                pe.wait_ge(sem("hxT_ready"), q + 1)
                pe.matmul(ps[:, q, :], wT_fc2, hxT[:, q * BANK:(q + 1) * BANK], start=True, stop=True)\
                    .then_inc(sem("fc_done"), 1)
            for p in range(NP):
                if p % 4 == 0:
                    pe.wait_ge(sem("hxT_ready"), NQ + p // 4 + 1)
                for i, part in enumerate((hx2T, xT)):
                    last = pe.matmul(ps[:, 4 + p // 4, p % 4 * P:(p % 4 + 1) * P], part[:, p * P:(p + 1) * P],
                                     ident[:, :], start=i == 0, stop=i == 1)
                if p % 4 == 3:
                    last.then_inc(sem("hx_token"), 1)
            transpose_pairs(pe, xc, 0, "fo_ready")
            for p in range(NP):
                if p % 4 == 0:
                    pe.wait_ge(sem(f"pairs_out{p // 4 % 2}"), turned_out("fo", p // 4))
                last = pe.matmul(ps[:, 4, p * 2 * NH:(p + 1) * 2 * NH], xT[:, p * P:(p + 1) * P], wT_fg,
                                 start=True, stop=True)
            last.then_inc(sem("fg_done"), 1)

        def seq(x):
            return x.rearrange("p (b t) -> p b t", t=P)

        def pairs_out(eng, name, first_bank, q, dst, scale=None, bias=None):
            eng.wait_ge(sem("pairs_turned"), turned(name, q))
            src, dst = ps[:, first_bank + q, :], dst[:, q * BANK:(q + 1) * BANK]
            if q % 2:
                if scale is None:
                    ins = eng.tensor_copy(dst, src)
                else:
                    ins = eng.tensor_scalar(dst, src, scale, bias, ALU.mult, ALU.add)
            elif scale is None:
                ins = eng.activation(dst, src, ACT.Copy)
            else:
                ins = eng.activation(dst, src, ACT.Identity, scale=scale, bias=bias)
            ins.then_inc(sem(f"pairs_out{q % 2}"), 1)

        def col(i):
            return cols[:, i:i + 1]

        def banks(first):
            return ps[:, first:first + NQ, :].rearrange("p k n -> p (k n)")

        def recurrent_pool(pool):
            pool.wait_ge(sem("fg_done"), 1)
            pool.memset(seq(k_last)[:, :, 0:1], NEG).then_inc(sem("starts_ready"), 1)
            pool.memset(seq(A2)[:, :, 0:1], 0.0).then_inc(sem("starts_ready"), 1)
            pool.memset(seq(E2)[:, :, 0:1], 0.0).then_inc(sem("starts_ready"), 1)
            pool.memset(seq(EV)[:, :, 0:1], 0.0).then_inc(sem("starts_ready"), 1)
            pool.wait_ge(sem("ln4_var"), 1)
            pool.tensor_tensor(fn[:, :, :], xc[:, :, :], bc(st[0][:, 2, :], C), ALU.mult).then_inc(sem("x3_ready"), 1)
            pool.wait_ge(sem("E_ready"), 2)
            pool.wait_ge(sem("EV_ready"), 1)
            pool.tensor_tensor(vT, kT, vT, ALU.mult).then_inc(sem("pool_recurrent"), 1)
            pool.wait_ge(sem("x5_ready"), 2)
            pool.tensor_tensor(h[:, :, :], h[:, :, :], fn[:, :, :], ALU.add).then_inc(sem("pool_recurrent"), 1)

        def recurrent_act(act):
            ln_act(act, "ln3", st[0])
            act.wait_ge(sem("ln4_var"), 1)
            act.activation(st[1][:, 5, :], st[1][:, 4, :], ACT.Sqrt).then_inc(sem("ln4_root"), 1)
            for q in range(0, NQ, 2):
                pairs_out(act, "x4", 0, q, hT, col(G1), col(B1))
            act.wait_ge(sem("starts_ready"), 4)
            for q in range(NQ):
                act.wait_ge(sem("k_proj"), q + 1)
                act.activation(seq(k_last)[:, 4 * q:4 * q + 4, 1:], seq(ps[:, 4 + q, :])[:, :, 0:P - 1], ACT.Copy)\
                    .then_inc(sem("k_shifted"), 1)
            act.activation(kT, banks(4), ACT.Copy).then_inc(sem("kT_ready"), 1)
            act.wait_ge(sem("v_proj"), NQ)
            act.activation(vT, banks(0), ACT.Copy).then_inc(sem("vT_ready"), 1)
            act.wait_ge(sem("A2_log"), 1)
            act.activation(seq(A2)[:, :, 1:], seq(A2)[:, :, 1:], ACT.Exp, bias=col(W_COL)).then_inc(sem("A2_ready"), 1)
            act.wait_ge(sem("E2_log"), 1)
            act.activation(seq(E2)[:, :, 1:], seq(E2)[:, :, 1:], ACT.Exp).then_inc(sem("E2_ready"), 1)
            act.wait_ge(sem("d_ready"), 1)
            act.activation(O_prev, W_t, ACT.Relu).then_inc(sem("A_ready"), 1)
            act.wait_ge(sem("A_ready"), 1)
            act.activation(O_prev, O_prev, ACT.Exp, scale=-1.0).then_inc(sem("A_ready"), 1)
            act.activation(kT, W_t, ACT.Relu, scale=-1.0).then_inc(sem("E_ready"), 1)
            act.wait_ge(sem("E_ready"), 1)
            act.activation(kT, kT, ACT.Exp, scale=-1.0).then_inc(sem("E_ready"), 1)
            act.wait_ge(sem("r_proj"), NQ)
            act.activation(srT, banks(4), ACT.Sigmoid).then_inc(sem("srT_ready"), 1)
            act.wait_ge(sem("den_ready"), 1)
            act.activation(W_t, Q_prev, ACT.Ln).then_inc(sem("den_log"), 1)
            act.wait_ge(sem("den_log"), 1)
            act.activation(W_t, W_t, ACT.Exp, scale=-1.0).then_inc(sem("den_inverse"), 1)
            ln_act(act, "ln5", st[0])
            for q in range(0, NQ, 2):
                pairs_out(act, "x5", 4, q, hT, col(G2), col(B2))
            for q in range(NQ):
                for i in range(0, 4, 2):
                    act.wait_ge(sem("kk_proj"), 4 * q + i + 1)
                    dst = hidT[:, i, q * BANK:(q + 1) * BANK]
                    act.activation(dst, ps[:, i, :], ACT.Relu).then_inc(sem("kk_relu"), 1)
                    act.wait_ge(sem("kk_relu"), 2 * q + i // 2 + 1)
                    act.activation(dst, dst, ACT.Square).then_inc(sem("kk_act"), 1)
                if q == 0:
                    for r in range(NQ):
                        act.wait_ge(sem("rf_proj"), r + 1)
                        act.activation(srfT[:, r * BANK:(r + 1) * BANK], ps[:, 4 + r, :], ACT.Sigmoid)\
                            .then_inc(sem("srfT_ready"), 1)

        def recurrent_dve(dve, ch):
            ch(dve.tensor_scalar(col(W_COL), col(DECAY), 1.0 / P, None, ALU.mult))
            ch(dve.tensor_scalar(col(U_COL), col(FIRST), 1.0 / P, None, ALU.mult))
            layer_norm_stats(dve, ch, "ln3", h[:, :, :], st[0])
            s, s4 = st[0], st[1]
            ch(dve.tensor_scalar(s4[:, 3, :], s[:, 3, :], 1.0 / C, None, ALU.mult))
            ch(dve.tensor_tensor(s4[:, 3, :], s4[:, 3, :], s[:, 2, :], ALU.mult))
            ch(dve.tensor_tensor(s4[:, 3, :], s4[:, 3, :], s[:, 2, :], ALU.mult))
            dve.tensor_scalar(s4[:, 4, :], s4[:, 3, :], LN_EPS, None, ALU.add).then_inc(sem("ln4_var"), 1)
            dve.wait_ge(sem("ln4_root"), 1)
            refined_rstd(dve, ch, s4)
            ch(dve.tensor_tensor(s4[:, 2, :], s4[:, 2, :], s[:, 2, :], ALU.mult))
            scaled(dve, sq[:, :, :], xc[:, :, :], s4[:, 2, :], C, "x4_ready")
            ch(dve.tensor_copy(W_t, col(W_COL).broadcast_to((P, TP))))
            ch(dve.memset(seq(W_t)[:, :, 0:1], NEG))
            for q in range(1, NQ, 2):
                pairs_out(dve, "x4", 0, q, hT, col(G1), col(B1))
            for q in range(NQ):
                c = slice(q * BANK, (q + 1) * BANK)
                dve.wait_ge(sem("k_shifted"), q + 1)
                last = dve.tensor_tensor_scan(O_prev[:, c], W_t[:, c], k_last[:, c], 0.0, ALU.add, ALU.max)
            ch(last)
            dve.tensor_tensor(seq(A2)[:, :, 1:], seq(O_prev)[:, :, 0:P - 1], seq(O_prev)[:, :, 1:], ALU.subtract)\
                .then_inc(sem("A2_log"), 1)
            dve.wait_ge(sem("kT_ready"), 1)
            dve.tensor_tensor(seq(E2)[:, :, 1:], seq(kT)[:, :, 0:P - 1], seq(O_prev)[:, :, 1:], ALU.subtract)\
                .then_inc(sem("E2_log"), 1)
            dve.scalar_tensor_tensor(W_t, kT, col(U_COL), O_prev, ALU.add, ALU.subtract).then_inc(sem("d_ready"), 1)
            dve.wait_ge(sem("E2_ready"), 1)
            dve.wait_ge(sem("vT_ready"), 1)
            dve.tensor_tensor(seq(EV)[:, :, 1:], seq(E2)[:, :, 1:], seq(vT)[:, :, 0:P - 1], ALU.mult)\
                .then_inc(sem("EV_ready"), 1)
            dve.wait_ge(sem("EV_ready"), 1)
            dve.wait_ge(sem("A2_ready"), 1)
            ch(dve.tensor_tensor_scan(P_prev, A2, EV, 0.0, ALU.mult, ALU.add))
            ch(dve.tensor_tensor_scan(Q_prev, A2, E2, 0.0, ALU.mult, ALU.add))
            dve.wait_ge(sem("A_ready"), 2)
            dve.wait_ge(sem("E_ready"), 2)
            den, num, rden = Q_prev, P_prev, W_t
            ch(dve.tensor_tensor(den, O_prev, den, ALU.mult))
            dve.tensor_tensor(den, den, kT, ALU.add).then_inc(sem("den_ready"), 1)
            ch(dve.tensor_tensor(num, O_prev, num, ALU.mult))
            dve.wait_ge(sem("pool_recurrent"), 1)
            ch(dve.tensor_tensor(num, num, vT, ALU.add))
            dve.wait_ge(sem("srT_ready"), 1)
            ch(dve.tensor_tensor(num, num, srT, ALU.mult))
            dve.wait_ge(sem("den_inverse"), 1)
            ch(dve.tensor_tensor(den, den, rden, ALU.mult))
            ch(dve.scalar_tensor_tensor(rden, den, -2.0, rden, ALU.add, ALU.mult))
            for q in range(NQ):
                c = slice(q * BANK, (q + 1) * BANK)
                dve.scalar_tensor_tensor(P_prev[:, c], num[:, c], -1.0, rden[:, c], ALU.mult, ALU.mult)\
                    .then_inc(sem("ysT_ready"), 1)
            dve.wait_ge(sem("x3_ready"), 1)
            for q in range(NQ):
                ts = slice(q * GT, (q + 1) * GT)
                dve.wait_ge(sem("o_proj"), q + 1)
                last = dve.tensor_tensor(fn[:, ts, :], fn[:, ts, :], ps[:, q, :].rearrange("p (t c) -> p t c", c=C),
                                         ALU.add)
            ch(last)
            layer_norm_stats(dve, ch, "ln5", fn[:, :, :], st[0])
            scaled(dve, xc[:, :, :], xc[:, :, :], st[0][:, 2, :], C, "x5_ready")
            for q in range(1, NQ, 2):
                pairs_out(dve, "x5", 4, q, hT, col(G2), col(B2))

            def gated(q):
                c = slice(q * BANK, (q + 1) * BANK)
                dve.wait_ge(sem("srfT_ready"), q + 1)
                dve.wait_ge(sem("ff_proj"), q + 1)
                dve.tensor_tensor(gatedT[:, c], srfT[:, c], ps[:, 4 + q, :], ALU.mult).then_inc(sem("gatedT_ready"), 1)

            for q in range(NQ):
                for i in range(1, 4, 2):
                    dve.wait_ge(sem("kk_proj"), 4 * q + i + 1)
                    dst = hidT[:, i, q * BANK:(q + 1) * BANK]
                    ch(dve.tensor_scalar(dst, ps[:, i, :], 0.0, None, ALU.max))
                    dve.tensor_tensor(dst, dst, dst, ALU.mult).then_inc(sem("kk_dve"), 1)
                if q >= 2:
                    gated(q - 2)
            gated(NQ - 2)
            gated(NQ - 1)
            dve.wait_ge(sem("pool_recurrent"), 2)
            for q in range(NQ):
                ts = slice(q * GT, (q + 1) * GT)
                dve.wait_ge(sem("gated_T"), q + 1)
                last = dve.tensor_tensor(h[:, ts, :], h[:, ts, :], ps[:, q, :].rearrange("p (t c) -> p t c", c=C), ALU.add)
            ch(last)

        def recurrent_pe(pe):
            transpose_pairs(pe, sq, 0, "x4_ready")
            pe.wait_ge(sem("wl_in"), 16 * WL_LOADS)
            pe.wait_ge(sem("pairs_out0"), turned_out("x4", NQ - 1))
            pe.wait_ge(sem("pairs_out1"), turned_out("x4", NQ - 1))
            project(pe, w_bd[:, WK, :], hT, "k_proj", 4)
            project(pe, w_bd[:, WV, :], hT, "v_proj", 0)
            pe.wait_ge(sem("kT_ready"), 1)
            project(pe, w_bd[:, WR, :], hT, "r_proj", 4)
            for p in range(NP):
                if p % 4 == 0:
                    pe.wait_ge(sem("ysT_ready"), p // 4 + 1)
                last = pe.matmul(ps[:, p // 4, p % 4 * P:(p % 4 + 1) * P], P_prev[:, p * P:(p + 1) * P],
                                 w_bd[:, WO, :], start=True, stop=True)
                if p % 4 == 3:
                    last.then_inc(sem("o_proj"), 1)
            transpose_pairs(pe, xc, 4, "x5_ready")
            def forward(q):
                pe.wait_ge(sem("kk_act"), 2 * q + 2)
                pe.wait_ge(sem("kk_dve"), 2 * q + 2)
                pe.wait_ge(sem("srfT_ready"), q + 1)
                for par in range(2):
                    for k in range(2):
                        last = pe.matmul(ps[par * C:(par + 1) * C, 4 + q, :], w_vf[:, k, :],
                                         hidT[:, 2 * par + k, q * BANK:(q + 1) * BANK], start=k == 0, stop=k == 1)
                last.then_inc(sem("ff_proj"), 1)

            for q in range(NQ):
                pe.wait_ge(sem(f"pairs_out{q % 2}"), turned_out("x5", q))
                if q == 1:
                    pe.wait_ge(sem("pairs_out0"), turned_out("x5", NQ - 1))
                    pe.wait_ge(sem("pairs_out1"), turned_out("x5", NQ - 1))
                    project(pe, w_bd[:, WRF, :], hT, "rf_proj", 4)
                for i in range(4):
                    if q:
                        pe.wait_ge(sem("kk_dve" if i % 2 else "kk_relu"), 2 * (q - 1) + i // 2 + 1)
                    pe.matmul(ps[:, i, :], w_kf[:, i // 2, i % 2 * P:(i % 2 + 1) * P],
                              hT[:, q * BANK:(q + 1) * BANK], start=True, stop=True).then_inc(sem("kk_proj"), 1)
                if q:
                    forward(q - 1)
            forward(NQ - 1)
            for p in range(NP):
                if p % 4 == 0:
                    pe.wait_ge(sem("gatedT_ready"), p // 4 + 1)
                last = pe.transpose(ps[:, p // 4, p % 4 * P:(p % 4 + 1) * P], gatedT[:, p * P:(p + 1) * P], ident[:, :])
                if p % 4 == 3:
                    last.then_inc(sem("gated_T"), 1)

        HID_BANKS = (4, 5, 6, 7, 0, 1)

        def experts_act(act):
            ln_act(act, "ln6", st[1])
            for q in range(0, NQ, 2):
                pairs_out(act, "x6", 0, q, hT)
            for q in range(NQ):
                for i in range(4):
                    act.wait_ge(sem("hid_proj"), 4 * q + i + 1)
                    act.activation(hidT[:, i, q * BANK:(q + 1) * BANK], ps[:, HID_BANKS[(4 * q + i) % 6], :], ACT.Gelu,
                                   bias=col(HID_B + i % 2)).then_inc(sem("hid_ready"), 1)
            act.wait_ge(sem("route_shifted"), 1)
            act.activation(coef[:, :, :], tmp8[:, :, :], ACT.Exp).then_inc(sem("route_exp"), 1)
            act.wait_ge(sem("coefT_done"), 1)
            act.activation(coefT[:, :], ps[:, 4, 0:2 * P], ACT.Copy).then_inc(sem("coefT_ready"), 1)

        def experts_dve(dve, ch):
            layer_norm_stats(dve, ch, "ln6", h[:, :, :], st[1])
            scaled(dve, fn[:, :, :], xc[:, :, :], st[1][:, 2, :], C, "x6_ready")
            for q in range(1, NQ, 2):
                pairs_out(dve, "x6", 0, q, hT)
            parts = ident[:, :].rearrange("p (a k e) -> p a k e", a=2, k=2)
            ch(dve.tensor_tensor(picked[:, :, :], parts[:, :, 0, 0:EX], parts[:, :, 1, 0:EX], ALU.add))
            for q in range(NQ):
                dve.wait_ge(sem("lgT_done"), q + 1)
                dve.tensor_copy(lgT[:, q * BANK:(q + 1) * BANK], ps[:, 2 + q % 2, :]).then_inc(sem("lgT_ready"), 1)
            m, r = st[0][:, 0, :], st[0][:, 1, :]
            dve.wait_ge(sem("lg_done"), 1)
            lg = ps[:, 4, 0:NT * EX].rearrange("p (t e) -> p t e", e=EX)
            ch(dve.tensor_tensor(tmp8[:, :, :], lg, row(rows[:, EX_B, 0:EX], NT), ALU.add))
            ch(dve.tensor_reduce(m, tmp8[:, :, :], AX.X, ALU.max))
            dve.tensor_tensor(tmp8[:, :, :], tmp8[:, :, :], bc(m, EX), ALU.subtract).then_inc(sem("route_shifted"), 1)
            dve.wait_ge(sem("route_exp"), 1)
            ch(dve.tensor_reduce(r, coef[:, :, :], AX.X, ALU.add))
            ch(dve.reciprocal(r, r))
            ch(dve.tensor_tensor(coef[:, :, :], coef[:, :, :], bc(r, EX), ALU.mult))
            ch(dve.tensor_reduce(m, coef[:, :, :], AX.X, ALU.max))
            ch(dve.tensor_tensor(tmp8[:, :, :], coef[:, :, :], bc(m, EX), ALU.is_equal))
            dve.wait_ge(sem("rank_ready"), 1)
            ch(dve.tensor_tensor(tmp8[:, :, :], tmp8[:, :, :], row(rank[:, :], NT), ALU.mult))
            ch(dve.tensor_reduce(r, tmp8[:, :, :], AX.X, ALU.max))
            ch(dve.tensor_tensor(tmp8[:, :, :], tmp8[:, :, :], bc(r, EX), ALU.is_equal))
            dve.tensor_tensor(coef[:, :, :], coef[:, :, :], tmp8[:, :, :], ALU.mult).then_inc(sem("coef_ready"), 1)
            dve.wait_ge(sem("coef_ready"), 1)
            for t in range(NT):
                if t in (4, 8):
                    half = t // 4 - 1
                    ts = slice(half * NP, (half + 1) * NP)
                    dve.wait_ge(sem("bias_done"), half + 1)
                    dve.tensor_tensor(h[:, ts, :], h[:, ts, :],
                                      ps[:, 6:8, :].rearrange("p k (t c) -> p (k t) c", c=C), ALU.add)\
                        .then_inc(sem("bias_added"), 1)
                    if half:
                        dve.wait_ge(sem("bias_added"), 2)
                dve.wait_ge(sem("y_done"), t + 1)
                y = scratch[:, t % 4, :]
                dve.tensor_tensor(y.rearrange("p (e c) -> p e c", e=EX),
                                  ps[:, t % 4, :].rearrange("p (e c) -> p e c", e=EX), bc(coef[:, t, :], C), ALU.mult)\
                    .then_inc(sem("y_weighted"), 1)
                dve.wait_ge(sem("y_weighted"), t + 1)
                ch(dve.tensor_reduce(xp[:, t, :], y.rearrange("p (e c) -> p c e", e=EX), AX.X, ALU.add))
                if t + 1 in [t1 for _, t1 in STORES]:
                    ts = slice(*STORES[[t1 for _, t1 in STORES].index(t + 1)])
                    dve.tensor_tensor(h[:, ts, :], h[:, ts, :], xp[:, ts, :], ALU.add).then_inc(sem("h_done"), 1)

        def experts_pe(pe):
            transpose_pairs(pe, fn, 0, "x6_ready")
            def logits(q):
                pe.wait_ge(sem("hid_ready"), 4 * q + 4)
                if q >= 2:
                    pe.wait_ge(sem("lgT_ready"), q - 1)
                for par in range(2):
                    for k in range(2):
                        i = 2 * par + k
                        last = pe.matmul(ps[32 * i:32 * i + 32, 2 + q % 2, :], w_g[:, k, :],
                                         hidT[:, i, q * BANK:(q + 1) * BANK], start=True, stop=True)
                last.then_inc(sem("lgT_done"), 1)

            for q in range(NQ):
                done = q if q == 0 else NQ - 1
                pe.wait_ge(sem("pairs_out0"), turned_out("x6", done))
                if q:
                    pe.wait_ge(sem("pairs_out1"), turned_out("x6", done))
                for i in range(4):
                    if 4 * q + i >= 6:
                        pe.wait_ge(sem("hid_ready"), 4 * q + i - 5)
                    pe.matmul(ps[:, HID_BANKS[(4 * q + i) % 6], :], w_1[:, i // 2, i % 2 * P:(i % 2 + 1) * P],
                              hT[:, q * BANK:(q + 1) * BANK], start=True, stop=True).then_inc(sem("hid_proj"), 1)
                if q:
                    logits(q - 1)
            logits(NQ - 1)
            for p in range(NP):
                if p % 4 == 0:
                    pe.wait_ge(sem("lgT_ready"), p // 4 + 1)
                last = pe.matmul(ps[:, 4, p * 2 * EX:(p + 1) * 2 * EX], lgT[:, p * P:(p + 1) * P], picked[:, :, :],
                                 start=True, stop=True)
            last.then_inc(sem("lg_done"), 1)

            for t in range(NT):
                if t == 2:
                    pe.wait_ge(sem("lgT_ready"), NQ)
                if t == 4:
                    pe.wait_ge(sem("coef_ready"), 1)
                    for half in range(2):
                        last = pe.transpose(ps[:, 4, half * P:(half + 1) * P],
                                            coef[:, half * NP:(half + 1) * NP, :].rearrange("p t e -> p (t e)"),
                                            ident[:, :])
                    last.then_inc(sem("coefT_done"), 1)
                if t >= 4:
                    pe.wait_ge(sem("y_weighted"), t - 3)
                for k in range(2):
                    last = pe.matmul(ps[:, t % 4, :], hidT[:, t % 2 * 2 + k, t // 2 * P:(t // 2 + 1) * P],
                                     w_d[:, k, :], start=k == 0, stop=k == 1)
                last.then_inc(sem("y_done"), 1)
                if t in (4, 8):
                    half = t // 4 - 1
                    pe.wait_ge(sem("coefT_ready"), 1)
                    if half:
                        pe.wait_ge(sem("bias_added"), 1)
                    for k in range(2):
                        last = pe.matmul(ps[:, 6 + k, :], coefT[:, half * P:(half + 1) * P],
                                         w_bias[:, k * BANK:(k + 1) * BANK], start=True, stop=True)
                    last.then_inc(sem("bias_done"), 1)

        @block.sync
        def _(sp):
            sp.dma_start(x_int[:, :], a["x"]).then_inc(sem("x_in"), 16)
            sp.dma_start(wproj[:, :], a["L0_tok_w_proj"]).then_inc(sem("wproj_in"), 16)
            sp.dma_start(gate_w[:, :], a["fside_1S_w_gate"].partition_broadcast(P)).then_inc(sem("gate_in"), 16)
            sp.dma_start(gate_b[:, :], a["L0_tok_b_gate"].unsqueeze(0).partition_broadcast(P)).then_inc(sem("gate_in"), 16)
            sp.wait_ge(sem("wn_zeroed"), 1)

            def put(r, c, src):
                n, m = src.shape
                sp.dma_start(wn[r:r + n, c:c + m], src).then_inc(sem("wn_in"), 16)
                wn_loads.append(1)

            for par in range(2):
                put(par * C, WCOL["hl"] + par * C, a["L0_ffn_hl_w"].rearrange("n d h -> (n d) h"))
                for n in range(NH):
                    r = par * C + n * D
                    for e in range(NE):
                        put(r, WCOL[f"wq{e}"] + C + n * D, a["L0_ffn_wq"][n, e])
                    put(r, WCOL["wk"] + C + n * D, a["L0_ffn_wk"][n])
                    put(r, WCOL["wv"] + r, a["L0_ffn_wv"][n])
                    put(r, WCOL["fc1"] + r, a["L0_ffn_fc1_w"])
                    put(r, WCOL["fc2"] + r, a["L0_ffn_fc2_w"])
                put(par * NH, WCOL["fg"] + par * C, a["L0_ffn_fgate_w"])
            for n in range(NH):
                put(n * NE, WCOL[f"gate{n // 2}"] + n % 2 * C, a["L0_ffn_gate_w"][n])
            assert len(wn_loads) == WN_LOADS

            def vector_col(i, src):
                n = src.shape[0]
                for r in range(0, P, n):
                    sp.dma_start(cols[r:r + n, i:i + 1], src.unsqueeze(1)).then_inc(sem("cols_in"), 16)
                    col_loads.append(1)

            def vector_row(i, src):
                n = src.shape[0]
                for r in range(0, C, n):
                    if i == GATE_B and r:
                        break
                    sp.dma_start(rows[:, i, r:r + n], src.unsqueeze(0).partition_broadcast(P))\
                        .then_inc(sem("rows_in"), 16)
                    row_loads.append(1)

            vector_col(HL_B, a["L0_ffn_hl_b"].rearrange("n d -> (n d)"))
            vector_col(FC1_B, a["L0_ffn_fc1_b"])
            for i, name in ((G1, "g1"), (B1, "b1"), (G2, "g2"), (B2, "b2"), (DECAY, "spatial_decay"),
                            (FIRST, "spatial_first")):
                vector_col(i, a[f"L1_attn_{name}"])
            for i, name in ((LN_G, "ln_g"), (LN_B, "ln_b"), (FC2_B, "fc2_b"), (FG_COL, "fnorm_g"), (FB_COL, "fnorm_b")):
                vector_col(i, a[f"L0_ffn_{name}"])
            for k in range(2):
                vector_col(HID_B + k, a["L1_ffn_b1"][k * P:(k + 1) * P])
            sp.dma_start(rows[:, EX_B, 0:EX], a["L1_ffn_bg"].unsqueeze(0).partition_broadcast(P))\
                .then_inc(sem("rows_in"), 16)
            row_loads.append(1)
            for i, name in ((FN_G, "fnorm_g"), (FN_B, "fnorm_b")):
                vector_row(i, a[f"L0_ffn_{name}"])
            vector_row(GATE_B, a["L0_ffn_gate_b"].rearrange("n e -> (n e)"))
            assert (len(col_loads), len(row_loads)) == (COL_LOADS, ROW_LOADS)
            sp.wait_ge(sem("wl_zeroed"), 1)
            L = "L1_attn_"
            for i, name in ((WK, "Wk"), (WV, "Wv"), (WR, "Wr"), (WO, "Wo"), (WRF, "Wr_ffn")):
                for par in range(2):
                    r = slice(par * C, (par + 1) * C)
                    sp.dma_start(w_bd[r, i, r], a[L + name]).then_inc(sem("wl_in"), 16)
            for par in range(2):
                r = slice(par * C, (par + 1) * C)
                sp.dma_start(w_kf[r, par, :], a[L + "Wk_ffn"]).then_inc(sem("wl_in"), 16)
                sp.dma_start(w_1[r, par, :], a["L1_ffn_W1"]).then_inc(sem("wl_in"), 16)
            sp.dma_start(w_vf[:, :, :], a[L + "Wv_ffn"].rearrange("(k p) c -> p k c", p=P)).then_inc(sem("wl_in"), 16)
            sp.dma_start(w_g[:, :, 0:EX], a["L1_ffn_Wg"].rearrange("(k p) c -> p k c", p=P)).then_inc(sem("wl_in"), 16)
            for k in range(2):
                sp.dma_start(w_d[:, k, :].rearrange("p (e c) -> p e c", e=EX),
                             a["L1_ffn_Wd"][:, k * P:(k + 1) * P, :].rearrange("e p c -> p e c"))\
                    .then_inc(sem("wl_in"), 16)
            for i in range(P // EX):
                sp.dma_start(w_bias[i * EX:(i + 1) * EX, i * C:(i + 1) * C], a["L1_ffn_bd"]).then_inc(sem("wl_in"), 16)
            for i, (t0, t1) in enumerate(STORES):
                sp.wait_ge(sem("h_done"), i + 1)
                sp.dma_start(out[t0:t1].rearrange("b s c -> s b c"), h[:, t0:t1, :]).then_inc(sem("out_stored"), 16)
            sp.wait_ge(sem("out_stored"), 16 * len(STORES))

        @block.gpsimd
        def _(pool):
            ch = Chain(pool, "pool_chain")
            ch(pool.memset(ident[:, :], 0.0))
            ch(pool.memset(ident2[:, :], 0.0))
            pool.affine_select(out=ident[:, :], in_=ident[:, :], compare_op=ALU.not_equal, fill=1.0,
                               base=0, pattern=[[-1, P]], channel_multiplier=1).then_inc(sem("ident_ready"), 1)
            ch(pool.affine_select(out=ident2[:, :], in_=ident2[:, :], compare_op=ALU.not_equal, fill=1.0,
                                  base=0, pattern=[[-1, C]], channel_multiplier=1))
            ch(pool.affine_select(out=ident2[:, :], in_=ident2[:, :], compare_op=ALU.not_equal, fill=1.0,
                                  base=-C, pattern=[[-1, C]], channel_multiplier=1))
            pool.wait_ge(sem("ident_ready"), 1)
            ch(pool.memset(zero16[:, :], 0.0))
            pool.tensor_copy(ident16[:, :], ident[:, :]).then_inc(sem("ident_ready"), 1)
            pool.memset(wn[:, :], 0.0).then_inc(sem("wn_zeroed"), 1)
            pool.wait_ge(sem("idx_ready"), 1)
            for t in range(NT):
                where = bass.IndirectOffsetOnAxis(ap=idx[:, t:t + 1], axis=0)
                for table, dst in (("L0_tok_fourier_table", geo_raw[t // NP][:, t % NP, 0:FOUR]),
                                   ("L0_tok_visit_table", geo_raw[t // NP][:, t % NP, FOUR:GEO]),
                                   ("L0_tok_emb_table", gate_in[:, t, 0:EMB])):
                    pool.indirect_dma_start(out=dst, out_offset=None, in_=a[table], in_offset=where)\
                        .then_inc(sem(f"gathered{t // GT}"), 16)
            ch(pool.tensor_copy(ident_bf[:, :], ident[:, :]))
            ch(pool.memset(masked[:, :, :], 0.0))
            ch(pool.affine_select(out=masked[:, :, :], in_=masked[:, :, :], compare_op=ALU.is_ge, fill=MASKED,
                                  base=0, pattern=[[0, NH], [-1, P]], channel_multiplier=1))
            ch(pool.memset(own_rows[:, :], 1.0))
            ch(pool.affine_select(out=own_rows[:, :], in_=own_rows[:, :], compare_op=ALU.is_ge, fill=0.0,
                                  base=0, pattern=[[-D, 2 * NH]], channel_multiplier=1))
            pool.affine_select(out=own_rows[:, :], in_=own_rows[:, :], compare_op=ALU.is_ge, fill=0.0,
                               base=D - 1, pattern=[[D, 2 * NH]], channel_multiplier=-1)\
                .then_inc(sem("masks_ready"), 1)
            pool.wait_ge(sem("masks_ready"), 1)
            pool.tensor_tensor(own_head[:, :], own_rows[:, 0:NH], own_rows[:, NH:], ALU.add)\
                .then_inc(sem("masks_ready"), 1)
            heads_pool(pool)
            recurrent_pool(pool)

        @block.scalar
        def _(act):
            ch = Chain(act, "act_chain")
            act.wait_ge(sem("gate_in"), 32)
            ch(act.activation(act_warm[:, 0:1], gate_b[:, :], ACT.Square))
            attention_act(act)
            heads_act(act)
            recurrent_act(act)
            experts_act(act)

        @block.vector
        def _(dve):
            ch = Chain(dve, "dve_chain")
            dve.wait_ge(sem("x_in"), 16)
            dve.tensor_copy(x_f[:, :], x_int[:, :]).then_inc(sem("x_f_ready"), 1)
            dve.wait_ge(sem("wprojT_done"), 1)
            dve.tensor_copy(wprojT[:, :], ps[0:GEO, 6, 0:C]).then_inc(sem("wprojT_ready"), 1)
            dve.wait_ge(sem("idT_done"), 1)
            dve.tensor_scalar(idx[:, :], ps[:, 7, 0:NT], 0.0, float(ITEMS - 1), ALU.max, ALU.min)\
                .then_inc(sem("idx_ready"), 1)
            dve.tensor_scalar(valid[:, :], ps[:, 7, 0:NT], 0.0, None, ALU.not_equal).then_inc(sem("idx_ready"), 1)
            dve.wait_ge(sem("idx_ready"), 2)
            dve.wait_ge(sem("gate_in"), 32)
            attention_dve(dve, ch)
            heads_dve(dve, ch)
            recurrent_dve(dve, ch)
            experts_dve(dve, ch)

        @block.tensor
        def _(pe):
            pe.wait_ge(sem("ident_ready"), 1)
            pe.wait_ge(sem("wproj_in"), 16)
            pe.transpose(ps[0:GEO, 6, 0:C], wproj[:, :], ident[0:C, 0:C]).then_inc(sem("wprojT_done"), 1)
            pe.wait_ge(sem("x_f_ready"), 1)
            pe.transpose(ps[:, 7, 0:NT], x_f[:, :], ident[0:NT, 0:NT]).then_inc(sem("idT_done"), 1)
            pe.wait_ge(sem("idx_ready"), 2)
            pe.wait_ge(sem("wprojT_ready"), 1)
            attention_pe(pe)
            heads_pe(pe)
            recurrent_pe(pe)
            experts_pe(pe)



def kernel(**inputs):
    import numpy as _np
    import concourse.bacc as _bacc
    from concourse import mybir as _mybir
    from concourse.bass_utils import run_bass_kernel_spmd as _run

    nc = _bacc.Bacc("TRN2", target_bir_lowering=False, num_devices=1)
    arrays, args = {}, {}
    for name in inputs:
        v = _np.ascontiguousarray(inputs[name])
        arrays[f"in_{name}_dram"] = v
        args[name] = nc.dram_tensor(f"in_{name}_dram", v.shape, _mybir.dt.from_np(v.dtype), kind="ExternalInput").ap()
    shape = inputs["x"].shape + (inputs["L0_tok_emb_table"].shape[1],)
    out = nc.dram_tensor("out_dram", shape, _mybir.dt.float32, kind="ExternalOutput").ap()
    tower(nc, args, out)
    r = _run(nc, [arrays], core_ids=[0])
    return r.results[0]["out_dram"]
```
